# Optimizing a Trainium2 kernel written in Bass

```python
import numpy as np
import jax
import jax.numpy as jnp

def _softmax(x, axis=-1):
    return jax.nn.softmax(x, axis=axis)

def _gelu(x):
    return jax.nn.gelu(x, approximate=True)

def _silu(x):
    return jax.nn.silu(x)

def _sigmoid(x):
    return jax.nn.sigmoid(x)

def _layernorm(x, axis=-1, eps=1e-05):
    m = jnp.mean(x, axis=axis, keepdims=True)
    v = jnp.var(x, axis=axis, keepdims=True)
    return (x - m) / jnp.sqrt(v + eps)

def _scatter_add(tgt, idx, src, axis=0):
    return tgt.at[idx].add(src)

def _segment_sum(src, seg, n):
    return jax.ops.segment_sum(src, seg, n)
kernel_name = 'mk_decoder_postln_d1_seqx_r2_d5625b'

def setup_inputs(seed: int=0):
    np.random.seed(seed)
    _w = jnp.asarray

    def _rec_inputs():
        import jax
        import jax.numpy as jnp
        _rk = jax.random.key(seed)
        x = 7.22e-05 + 1 * jax.random.normal(jax.random.fold_in(_rk, 1), (2, 1024, 512), jnp.float32)
        _lenS = 1024 - jax.random.randint(jax.random.fold_in(_rk, 7), (2,), 0, max(1, 1024 // 4) + 1, jnp.int32)
        _lenS2 = 2048 - jax.random.randint(jax.random.fold_in(_rk, 8), (2,), 0, max(1, 2048 // 4) + 1, jnp.int32)
        _ctx_1024P = jax.random.normal(jax.random.fold_in(_rk, 11), (2, 16, 512), jnp.float32)
        _ctx_1024c = jax.random.dirichlet(jax.random.fold_in(_rk, 511), 0.3 * jnp.ones((16,), jnp.float32), (2, 2048))
        _ctx_1024t = jnp.einsum('bsk,bkd->bsd', _ctx_1024c, _ctx_1024P)
        _ctx_1024t = _ctx_1024t * jax.lax.rsqrt(jnp.mean(jnp.square(_ctx_1024t)) + 1e-12) * 0.953939
        ctx_1024 = 4.13588e-05 + 0.999923 * (_ctx_1024t + 0.3 * jax.random.normal(jax.random.fold_in(_rk, 611), (2, 2048, 512), jnp.float32))
        _validS = jnp.arange(1024)[None, :] < _lenS[:, None]
        _validS2 = jnp.arange(2048)[None, :] < _lenS2[:, None]
        _causal = jnp.tril(jnp.ones((1024, 1024), dtype=bool))
        mask_Bx1xSxS2_ik1 = jnp.where(jnp.broadcast_to(_validS2[:, None, None, :], (2, 1, 1024, 2048)), 1, 0).astype(jnp.int32)
        return (x, ctx_1024, mask_Bx1xSxS2_ik1)
    x, ctx_1024, mask_Bx1xSxS2_ik1 = _rec_inputs()

    def _L0_attn_setup():
        import jax, jax.numpy as jnp
        import numpy as np
        D_MODEL = 512
        QHEADS = 16
        KVHEADS = 4
        G = QHEADS // KVHEADS
        D_Q = D_MODEL // QHEADS
        D_KV = D_MODEL // QHEADS * KVHEADS
        BATCH, SEQ = (2, 1024)

        def _xavier(key, shape):
            fan_out, fan_in = shape
            lim = (6.0 / (fan_in + fan_out)) ** 0.5
            return jax.random.uniform(key, shape, jnp.float32, -lim, lim)
        key = jax.random.key(seed)
        ks = jax.random.split(key, 5)
        x = jax.random.normal(ks[0], (BATCH, SEQ, D_MODEL), jnp.float32)
        wq = _xavier(ks[1], (D_MODEL, D_MODEL))
        bq = jnp.zeros((D_MODEL,), jnp.float32)
        wk = _xavier(ks[2], (D_KV, D_MODEL))
        bk = jnp.zeros((D_KV,), jnp.float32)
        wv = _xavier(ks[3], (D_KV, D_MODEL))
        bv = jnp.zeros((D_KV,), jnp.float32)
        wo = _xavier(ks[4], (D_MODEL, D_MODEL))
        bo = jnp.zeros((D_MODEL,), jnp.float32)
        return {'x': x, 'wq': wq, 'bq': bq, 'wk': wk, 'bk': bk, 'wv': wv, 'bv': bv, 'wo': wo, 'bo': bo}
    _L0_attn_all = _L0_attn_setup()
    _L0_attn_in = {k: v for k, v in _L0_attn_all.items() if k in ('wq', 'bq', 'wk', 'bk', 'wv', 'bv', 'wo', 'bo')}
    del _L0_attn_all

    def _L0_xattn_setup():
        import jax, jax.numpy as jnp
        import numpy as np
        EMB, HEADS = (512, 16)
        B, S = (4, 1024)
        key = jax.random.key(seed)
        ks = jax.random.split(key, 12)
        scale = 1.0 / np.sqrt(EMB)
        inp = {'q': jax.random.normal(ks[0], (B, S, EMB), jnp.float32), 'k': jax.random.normal(ks[1], (B, S, EMB), jnp.float32), 'v': jax.random.normal(ks[2], (B, S, EMB), jnp.float32), 'mask': jax.random.randint(ks[3], (B, 1, S, S), 0, 2, jnp.int32), 'Wq': jax.random.normal(ks[4], (EMB, EMB), jnp.float32) * scale, 'bq': jnp.zeros((EMB,), jnp.float32), 'Wk': jax.random.normal(ks[5], (EMB, EMB), jnp.float32) * scale, 'bk': jnp.zeros((EMB,), jnp.float32), 'Wv': jax.random.normal(ks[6], (EMB, EMB), jnp.float32) * scale, 'bv': jnp.zeros((EMB,), jnp.float32), 'Wo': jax.random.normal(ks[7], (EMB, EMB), jnp.float32) * scale, 'bo': jnp.zeros((EMB,), jnp.float32)}
        return inp
    _L0_xattn_all = _L0_xattn_setup()
    _L0_xattn_in = {k: v for k, v in _L0_xattn_all.items() if k in ('Wq', 'bq', 'Wk', 'bk', 'Wv', 'bv', 'Wo', 'bo')}
    del _L0_xattn_all

    def _L0_ffn_setup():
        import jax, jax.numpy as jnp
        import numpy as np
        B, S, H, E = (4, 1024, 512, 8)
        key = jax.random.key(seed)
        k1, k2, k3 = jax.random.split(key, 3)
        scale_w = 1.0 / np.sqrt(H)
        return {'x': jax.random.normal(k1, (B, S, H), dtype=jnp.float32), 'router_w': jax.random.normal(k2, (H, E), dtype=jnp.float32) * scale_w, 'router_b': jnp.zeros((E,), dtype=jnp.float32), 'expert_w': jax.random.normal(k3, (E, H, H), dtype=jnp.float32) * scale_w, 'expert_b': jnp.zeros((E, H), dtype=jnp.float32)}
    _L0_ffn_all = _L0_ffn_setup()
    _L0_ffn_in = {k: v for k, v in _L0_ffn_all.items() if k in ('router_w', 'router_b', 'expert_w', 'expert_b')}
    del _L0_ffn_all
    return {'x': x, 'ctx_1024': ctx_1024, 'mask_Bx1xSxS2_ik1': mask_Bx1xSxS2_ik1, 'L0_attn_wq': _L0_attn_in['wq'], 'L0_attn_bq': _L0_attn_in['bq'], 'L0_attn_wk': _L0_attn_in['wk'], 'L0_attn_bk': _L0_attn_in['bk'], 'L0_attn_wv': _L0_attn_in['wv'], 'L0_attn_bv': _L0_attn_in['bv'], 'L0_attn_wo': _L0_attn_in['wo'], 'L0_attn_bo': _L0_attn_in['bo'], 'L0_xattn_Wq': _L0_xattn_in['Wq'], 'L0_xattn_bq': _L0_xattn_in['bq'], 'L0_xattn_Wk': _L0_xattn_in['Wk'], 'L0_xattn_bk': _L0_xattn_in['bk'], 'L0_xattn_Wv': _L0_xattn_in['Wv'], 'L0_xattn_bv': _L0_xattn_in['bv'], 'L0_xattn_Wo': _L0_xattn_in['Wo'], 'L0_xattn_bo': _L0_xattn_in['bo'], 'L0_ffn_router_w': _L0_ffn_in['router_w'], 'L0_ffn_router_b': _L0_ffn_in['router_b'], 'L0_ffn_expert_w': _L0_ffn_in['expert_w'], 'L0_ffn_expert_b': _L0_ffn_in['expert_b']}

def reference(x, ctx_1024, mask_Bx1xSxS2_ik1, L0_attn_wq, L0_attn_bq, L0_attn_wk, L0_attn_bk, L0_attn_wv, L0_attn_bv, L0_attn_wo, L0_attn_bo, L0_xattn_Wq, L0_xattn_bq, L0_xattn_Wk, L0_xattn_bk, L0_xattn_Wv, L0_xattn_bv, L0_xattn_Wo, L0_xattn_bo, L0_ffn_router_w, L0_ffn_router_b, L0_ffn_expert_w, L0_ffn_expert_b):
    import jax
    import jax.numpy as jnp

    def _L0_attn_ref(x, wq, bq, wk, bk, wv, bv, wo, bo):
        import jax, jax.numpy as jnp
        import numpy as np
        D_MODEL = 512
        QHEADS = 16
        KVHEADS = 4
        G = QHEADS // KVHEADS
        D_Q = D_MODEL // QHEADS
        D_KV = D_MODEL // QHEADS * KVHEADS
        BATCH, SEQ = (2, 1024)

        def _xavier(key, shape):
            fan_out, fan_in = shape
            lim = (6.0 / (fan_in + fan_out)) ** 0.5
            return jax.random.uniform(key, shape, jnp.float32, -lim, lim)
        b, n, _ = x.shape
        scaling = D_Q ** (-0.5)
        q = (x @ wq.T + bq).reshape(b, n, QHEADS, D_Q).transpose(0, 2, 1, 3)
        k = (x @ wk.T + bk).reshape(b, n, KVHEADS, D_Q).transpose(0, 2, 1, 3)
        v = (x @ wv.T + bv).reshape(b, n, KVHEADS, D_Q).transpose(0, 2, 1, 3)
        q = q.reshape(b, KVHEADS, G, n, D_Q).transpose(0, 2, 1, 3, 4)
        attn = jnp.einsum('bghnd,bhsd->bghns', q, k) * scaling
        attn = jax.nn.softmax(attn, axis=-1)
        out = jnp.einsum('bghns,bhsd->bghnd', attn, v)
        out = out.transpose(0, 3, 2, 1, 4).reshape(b, n, D_MODEL)
        return out @ wo.T + bo

    def _L0_xattn_ref(q, k, v, mask, Wq, bq, Wk, bk, Wv, bv, Wo, bo):
        import jax, jax.numpy as jnp
        import numpy as np
        EMB, HEADS = (512, 16)
        B, S = (4, 1024)
        Bq, Sq, E = q.shape
        H = HEADS
        D = E // H
        Q = (q @ Wq.T + bq).reshape(Bq, Sq, H, D).transpose(0, 2, 1, 3)
        K = (k @ Wk.T + bk).reshape(Bq, -1, H, D).transpose(0, 2, 1, 3)
        V = (v @ Wv.T + bv).reshape(Bq, -1, H, D).transpose(0, 2, 1, 3)
        scores = jnp.einsum('bhqd,bhkd->bhqk', Q, K) / jnp.sqrt(jnp.float32(D))
        scores = jnp.where(mask == 1, jnp.float32(-1000000000.0), scores)
        attn = jax.nn.softmax(scores, axis=-1)
        out = jnp.einsum('bhqk,bhkd->bhqd', attn, V)
        out = out.transpose(0, 2, 1, 3).reshape(Bq, Sq, E)
        return out @ Wo.T + bo

    def _L0_ffn_ref(x, router_w, router_b, expert_w, expert_b):
        import jax, jax.numpy as jnp
        import numpy as np
        B, S, H, E = (4, 1024, 512, 8)
        b, s, h = x.shape
        xt = x.reshape(b * s, h)
        logits = xt @ router_w + router_b
        probs = jax.nn.softmax(logits, axis=-1)
        gate = jnp.max(probs, axis=-1)
        idx = jnp.argmax(probs, axis=-1)
        out_all = jnp.einsum('th,ehd->ted', xt, expert_w) + expert_b[None, :, :]
        e_out = jnp.take_along_axis(out_all, idx[:, None, None], axis=1)[:, 0, :]
        y = gate[:, None] * e_out
        return y.reshape(b, s, h)
    x = _layernorm(x + _L0_attn_ref(x, L0_attn_wq, L0_attn_bq, L0_attn_wk, L0_attn_bk, L0_attn_wv, L0_attn_bv, L0_attn_wo, L0_attn_bo), axis=-1)
    x = _layernorm(x + _L0_xattn_ref(x, ctx_1024, ctx_1024, mask_Bx1xSxS2_ik1, L0_xattn_Wq, L0_xattn_bq, L0_xattn_Wk, L0_xattn_bk, L0_xattn_Wv, L0_xattn_bv, L0_xattn_Wo, L0_xattn_bo), axis=-1)
    x = _layernorm(x + _L0_ffn_ref(x, L0_ffn_router_w, L0_ffn_router_b, L0_ffn_expert_w, L0_ffn_expert_b), axis=-1)
    return x

_drawn_inputs = setup_inputs


def setup_inputs(seed=0):
    import zlib

    import numpy as np

    out = dict(_drawn_inputs(seed))
    spreads = {'L0_attn_bq': (0.0, 0.1),
     'L0_attn_bk': (0.0, 0.1),
     'L0_attn_bv': (0.0, 0.1),
     'L0_attn_bo': (0.0, 0.1),
     'L0_xattn_bq': (0.0, 0.1),
     'L0_xattn_bk': (0.0, 0.1),
     'L0_xattn_bv': (0.0, 0.1),
     'L0_xattn_bo': (0.0, 0.1),
     'L0_ffn_router_b': (0.0, 0.1),
     'L0_ffn_expert_b': (0.0, 0.1)}
    factors = {}
    for name, (base, spread) in spreads.items():
        noise = np.random.default_rng([zlib.crc32(name.encode()), seed]).standard_normal(out[name].shape)
        drawn = base * np.exp(spread * noise) if base else spread * noise
        out[name] = jnp.asarray(drawn.astype(out[name].dtype))
    for name, factor in factors.items():
        out[name] = (out[name] * factor).astype(out[name].dtype)
    return out
```

```python
from contextlib import ExitStack

import concourse.bass as bass
from concourse import mybir

F32 = mybir.dt.float32
F32R = mybir.dt.float32r
BF16 = mybir.dt.bfloat16
I32 = mybir.dt.int32
U32 = mybir.dt.uint32
ALU = mybir.AluOpType
ACT = mybir.ActivationFunctionType
AX = mybir.AxisListType
RMAX = bass.bass_isa.ReduceOp.max
ds = bass.ds

P = 128
B, S, D = 2, 1024, 512
SK = 2048
T = B * S
H, HKV, DH = 16, 4, 32
KC = D // P
GK = 256
NG = SK // GK
E = 8
EPS = 1e-5
SCALE = float(DH) ** -0.5
MASKED = -float(2 ** 100)
QT = S // P
NT = T // P
NB = 4
STK = 7 * 16

BANK_S = 0
BANK_O = 4
BANK_A = 5
BANK_T = 7


def decoder_layer(nc, x, xT, ctxT, mask, wqT, bq, wkT, bk, wvT, bv, woT, bo,
                  xwqT, xbq, xwkT, xbk, xwvT, xbv, xwoT, xbo, rw, rb, ew, eb, out):
    with ExitStack() as ctx:
        def sb(name, shape, dt=F32):
            return ctx.enter_context(nc.sbuf_tensor(name, shape, dt))

        def sem(name):
            return ctx.enter_context(nc.semaphore(name))

        def dram(name, shape, dt=F32):
            return nc.dram_tensor(name, shape, dt, kind="Internal").ap()

        ps = ctx.enter_context(nc.psum_tensor("ps", [P, 8, 512], F32))

        q_hi, q_lo = dram("q_hi", (B * D, S)), dram("q_lo", (B * D, S))
        k_hi, k_lo = dram("k_hi", (B * P, S)), dram("k_lo", (B * P, S))
        v_sc = dram("v_sc", (B * HKV * P, QT * DH))
        xq_hi, xq_lo = dram("xq_hi", (B * D, S)), dram("xq_lo", (B * D, S))
        xk_hi, xk_lo = dram("xk_hi", (B * NG * D, GK)), dram("xk_lo", (B * NG * D, GK))
        xv_sc = dram("xv_sc", (B * NG * H * P, 2 * DH))
        mask_sc = dram("mask_sc", (T, SK), BF16)
        num_sc = [dram(f"num_sc{a}", (D, T)) for a in range(2)]
        den_sc = [dram(f"den_sc{a}", (H, T)) for a in range(2)]
        rec_sc = [dram(f"rec_sc{a}", (H, T)) for a in range(2)]
        x_sc = [dram(f"x_sc{a}", (T, D)) for a in range(2)]

        xt = sb("xt", [P, KC, T])
        W = [sb(f"W{n}", [P, KC, D]) for n in range(5)]
        bq_s, bk_s = sb("bq_s", [P, KC]), sb("bk_s", [P, 1])
        bv_s = sb("bv_s", [P, P])
        xbq_s, xbk_s = sb("xbq_s", [P, KC]), sb("xbk_s", [P, KC])
        xbv_s = sb("xbv_s", [P, D])
        bo_s = [sb(f"bo_s{a}", [P, D]) for a in range(2)]
        rw_s, rb_s, eb_s = sb("rw_s", [P, KC, E]), sb("rb_s", [P, E]), sb("eb_s", [E, D])
        ident = sb("ident", [P, P])
        neg_ident = sb("neg_ident", [P, P], BF16)
        iota8 = sb("iota8", [P, E])
        qst = sb("qst", [97, NB, S], F32R)
        kst = sb("kst", [97, NB, S], F32R)
        vst = sb("vst", [P, NB, QT, 2 * DH])
        kx = sb("kx", [97, GK], F32R)
        vx = sb("vx", [P, 2, 2 * DH])
        mx = sb("mx", [P, QT, GK], BF16)
        mask0 = sb("mask0", [P, QT, GK], BF16)
        probs = sb("probs", [P, 2, S])
        hi = sb("hi", [P, 2, 512], F32R)
        lo = sb("lo", [P, 2, 512], F32R)
        m_part = sb("m_part", [P, QT, 2])
        m_rest = sb("m_rest", [P, QT])
        m_slot = sb("m_slot", [P, QT])
        m_fin = sb("m_fin", [P, 2, QT])
        m_row = sb("m_row", [QT, P], F32R)
        o_stage = sb("o_stage", [P, 2, 512])
        big = sb("big", [P, 10240])
        mask_i = big[:, 0:4096].bitcast(I32).rearrange("p (n k) -> p n k", n=2)
        mask_b = big[:, 4096:6144].bitcast(BF16).rearrange("p (n k) -> p n k", n=2)
        v_stage = big[:, 6144:7168].rearrange("p (n c) -> p n c", n=2)
        cx = big[:, 0:1024].rearrange("p (k t) -> p k t", k=KC)
        cv_stage = big[:, 1024:2048].rearrange("p (c n) -> p c n", c=2)
        onum = big[:, 0:2048].rearrange("p (c t) -> p c t", c=KC)
        orec = big[:, 2048:4096].rearrange("p (c t) -> p c t", c=KC)
        xres = big[:, 4096:6144].rearrange("p (i n) -> p i n", i=4)
        xnew = big[:, 6144:8192].rearrange("p (i n) -> p i n", i=4)
        den_s = big[:, 8192:8448]
        y = big[:, 0:8192].rearrange("p (i n) -> p i n", i=NT)
        wselT = big[0:E, 8192:10240].rearrange("p (i t) -> p i t", i=NT)
        hi4 = hi[:, :, :].rearrange("p a b -> p (a b)").rearrange("p (m t) -> p m t", m=4)
        lo4 = lo[:, :, :].rearrange("p a b -> p (a b)").rearrange("p (m t) -> p m t", m=4)
        grp = sb("grp", [P, B, QT, NG + 1])
        grp_m = sb("grp_m", [P, B, NG + 1])
        grp_r = sb("grp_r", [P, B, NG + 1])
        fl = sb("fl", [1, 8, NG])
        tbl = sb("tbl", [1, 4], I32)
        st = sb("st", [P, 4, 6])
        mv = sb("mv", [P, 4, 2])
        sd = sb("sd", [P, 4, 2])
        lg = sb("lg", [P, NT, E])
        ex = sb("ex", [P, NT, E])
        mx8 = sb("mx8", [P, NT, 8])
        ix8 = sb("ix8", [P, NT, 8], U32)
        nmx = sb("nmx", [P, NT])
        ssum = sb("ssum", [P, NT])
        gate = sb("gate", [P, NT])
        ixf = sb("ixf", [P, NT])
        wsel = sb("wsel", [P, NT, E])
        eps_s = sb("eps_s", [P, 1])

        names = """consts w_self xt0 xt1 xt2 xt3 bias w_out w_xq w_xk w_xv w_xo
            pj_mm pj_hi pj_done pj_st0 pj_st1 pv_st0 pv_st1
            mask_in0 mask_in1 mask_eq mask_red mask_st0 mask_st1 grp_ok grp_all flag tbl_ok
            s_stk0 s_stk1 s_stk2 s_stk3 s_unit s_score s_exp s_pv s_acc s_amm s_amax s_afin s_at s_arow s_mrow s_out0 s_out1
            c_stk0 c_stk1 c_stk2 c_stk3 c_unit c_score c_exp c_pv c_acc c_amm c_amax c_afin c_at c_arow c_mrow c_out0 c_out1 c_mask
            r_den0 r_rec0 r_out0 r_den1 r_rec1 r_out1
            o_num0 o_num1 o_ready0 o_ready1 o_x0 o_x1 o_xb0 o_xb1 o_mm0 o_mm1 o_add0 o_add1 o_st0 o_st1 o_var0 o_var1
            o_sd0 o_sd1 o_rs0 o_rs1 o_y0 o_y1 o_yst0 o_yst1 o_tr0 o_tr1 o_xt0 o_xt1
            cq_st0 cq_st1 passed
            f_w0 f_w1 f_w2 f_w3 f_w4 f_lg f_l f_mx f_ex f_ix f_g f_wt f_wtc f_bmm f_y f_mm f_acc f_st f_var f_sd f_rs f_n f_out f_x""".split()
        s = {n: sem(n) for n in names}
        kv = [{n: sem(f"{n}_kv{i}") for n in "ctx mm hi done st".split()} for i in range(3)]
        rest = [{n: sem(f"{n}_rest{b}") for n in "load free amm amax top score exp pv".split()} for b in range(B)]
        block = ctx.enter_context(nc.Block())

        JOBS = [(t, kind) for t in range(T // 512) for kind in ("k", "v", 0, 1, 2, 3)]
        HEADJOBS = [j for j, (_, kind) in enumerate(JOBS) if kind != "v"]

        @block.sync
        def _(sp):
            sp.dma_start(W[1][:, :, 0:P], wkT.rearrange("(k p) n -> p k n", p=P)).then_inc(s["w_self"], 16)
            sp.dma_start(xt[:, :, 0:512], xT[:, 0:512].rearrange("(k p) t -> p k t", p=P)).then_inc(s["xt0"], 16)
            sp.dma_start(W[1][:, :, P:2 * P], wvT.rearrange("(k p) n -> p k n", p=P)).then_inc(s["w_self"], 16)
            sp.dma_start(W[0][:, :, :], wqT.rearrange("(k p) n -> p k n", p=P)).then_inc(s["w_self"], 16)
            for dst, src in ((bq_s, bq), (bk_s, bk), (xbq_s, xbq), (xbk_s, xbk), (eb_s, eb)):
                sp.dma_start(dst[:, :], src).then_inc(s["bias"], 16)
            for dst, src in ((bv_s, bv), (xbv_s, xbv), (bo_s[0], bo), (bo_s[1], xbo), (rb_s, rb)):
                sp.dma_start(dst[:, :], src.broadcast_to([P, src.shape[1]])).then_inc(s["bias"], 16)
            sp.dma_start(rw_s[:, :, :], rw.rearrange("(k p) e -> p k e", p=P)).then_inc(s["bias"], 16)
            for t in range(1, 4):
                sp.dma_start(xt[:, :, t * 512:(t + 1) * 512],
                             xT[:, t * 512:(t + 1) * 512].rearrange("(k p) t -> p k t", p=P)).then_inc(s[f"xt{t}"], 16)
            sp.dma_start(W[2][:, :, :], woT.rearrange("(k p) n -> p k n", p=P)).then_inc(s["w_out"], 16)
            sp.dma_start(W[3][:, :, :], xwqT.rearrange("(k p) n -> p k n", p=P)).then_inc(s["w_xq"], 16)
            sp.dma_start(W[4][:, :, :], xwoT.rearrange("(k p) n -> p k n", p=P)).then_inc(s["w_xo"], 16)
            hj = vj = 0
            for j, (t, kind) in enumerate(JOBS):
                b, c0 = t // 2, (t % 2) * 512
                sp.wait_ge(s["pj_done"], j + 1)
                if kind == "v":
                    for i in range(4):
                        sp.dma_start(v_sc[b * HKV * P:(b + 1) * HKV * P, ((t % 2) * 4 + i) * DH:((t % 2) * 4 + i + 1) * DH]
                                     .rearrange("(h p) d -> p h d", p=P),
                                     v_stage[:, vj % 2, i * P:(i + 1) * P].rearrange("p (h d) -> p h d", h=HKV))\
                          .then_inc(s[f"pv_st{vj % 2}"], 16)
                    vj += 1
                else:
                    rows = slice(b * P, (b + 1) * P) if kind == "k" else slice(b * D + kind * P, b * D + (kind + 1) * P)
                    dst_hi, dst_lo = (k_hi, k_lo) if kind == "k" else (q_hi, q_lo)
                    sp.dma_start(dst_hi[rows, c0:c0 + 512], hi[:, hj % 2, :].bitcast(F32)).then_inc(s[f"pj_st{hj % 2}"], 16)
                    sp.dma_start(dst_lo[rows, c0:c0 + 512], lo[:, hj % 2, :].bitcast(F32)).then_inc(s[f"pj_st{hj % 2}"], 16)
                    hj += 1
            for n in range(2):
                sp.wait_ge(s[f"pj_st{n}"], 32 * hj // 2)
                sp.wait_ge(s[f"pv_st{n}"], 64 * vj // 2)

            def load_head(pre, buf, qrow, krow, vrow, q, k, v, nk):
                for dst, src in ((0, q[0]), (1, q[0]), (2, q[1])):
                    sp.dma_start(qst[32 * dst:32 * dst + 32, buf, :].bitcast(F32), src[ds(qrow, DH), :])\
                      .then_inc(s[f"{pre}_stk{buf}"], 16)
                for dst, src in ((0, k[0]), (1, k[1]), (2, k[0])):
                    sp.dma_start(kst[32 * dst:32 * dst + 32, buf, 0:nk].bitcast(F32), src[ds(krow, DH), 0:nk])\
                      .then_inc(s[f"{pre}_stk{buf}"], 16)
                sp.dma_start(vst[:, buf, 0:nk // P, 0:DH], v[ds(vrow, P), 0:(nk // P) * DH]
                             .rearrange("p (c d) -> p c d", d=DH)).then_inc(s[f"{pre}_stk{buf}"], 16)

            def row_of_maxima(pre, buf, n):
                sp.wait_ge(s[f"{pre}_arow"], n + 2)
                sp.dma_start(qst[96:97, buf, :].rearrange("o (t c) -> o t c", t=QT).bitcast(F32),
                             m_row[:, :].bitcast(F32)).then_inc(s[f"{pre}_mrow"], 16)

            def self_load(u4, g):
                load_head("s", g, u4 * 128 + g * 32, u4 * 32, u4 * 128, (q_hi, q_lo), (k_hi, k_lo), v_sc, S)

            for g in range(3):
                self_load(0, g)
            row_of_maxima("s", 0, 0)

            def self_units(j, last=False):
                for g in range(4):
                    if not (last and g > 0):
                        sp.wait_ge(s["s_unit"], 4 * j + g + 1)
                        sp.sem_inc(s["passed"], 1)
                        self_load(j + (g + 3) // 4, (g + 3) % 4)
                    if not (last and g == 3):
                        row_of_maxima("s", (g + 1) % 4, 4 * j + g + 1)

            with sp.Fori(0, 7) as j:
                self_units(j)
            self_units(7, last=True)

            sp.wait_ge(s["pj_mm"], len(JOBS))
            sp.dma_start(W[0][:, :, :], xwkT.rearrange("(k p) n -> p k n", p=P)).then_inc(s["w_xk"], 16)
            sp.dma_start(W[1][:, :, :], xwvT.rearrange("(k p) n -> p k n", p=P)).then_inc(s["w_xv"], 16)

            def out_stage(a):
                pre, units = ("s", 32) if a == 0 else ("c", 32)
                for n in range(2):
                    sp.wait_ge(s[f"{pre}_out{n}"], 64 * units // 2 + 64)
                sp.dma_start(den_s, den_sc[a].rearrange("h (c t) -> (h c) t", c=8)).then_inc(s[f"r_den{a}"], 16)
                sp.wait_ge(s[f"r_rec{a}"], 1)
                sp.dma_start(rec_sc[a].rearrange("h (c t) -> (h c) t", c=8), den_s).then_inc(s[f"r_out{a}"], 16)
                sp.wait_ge(s[f"r_out{a}"], 16)
                res = x if a == 0 else x_sc[0]
                for t in range(4):
                    if t:
                        sp.wait_ge(s[f"o_mm{a}"], 4 * t)
                    sp.dma_start(onum, num_sc[a][:, t * 512:(t + 1) * 512].rearrange("(c p) t -> p c t", p=P))\
                      .then_inc(s[f"o_num{a}"], 16)
                    for hh in range(4):
                        src = rec_sc[a][hh:H:4, t * 512:(t + 1) * 512]
                        sp.dma_start(orec[32 * hh:32 * hh + 32, :, :],
                                     src.rearrange("(o c) t -> o c t", o=1).broadcast_to([32, KC, 512]))\
                          .then_inc(s[f"o_num{a}"], 16)
                    if t:
                        sp.wait_ge(s[f"o_add{a}"], 4 * t)
                    sp.dma_start(xres, res[t * 512:(t + 1) * 512, :].rearrange("(i p) n -> p i n", p=P))\
                      .then_inc(s[f"o_x{a}"], 16)
                    sp.wait_ge(s[f"o_y{a}"], 4 * t + 4)
                    sp.dma_start(x_sc[a][t * 512:(t + 1) * 512, :].rearrange("(i p) n -> p i n", p=P), xnew)\
                      .then_inc(s[f"o_yst{a}"], 16)
                sp.wait_ge(s[f"o_yst{a}"], 64)

            for n in range(2):
                sp.wait_ge(s[f"mask_st{n}"], 16 * NT // 2)
            out_stage(0)

            for j in range(16):
                t, m = j // 4, j % 4
                sp.wait_ge(s["pj_done"], len(JOBS) + j + 1)
                rows, cols = slice((t // 2) * D + m * P, (t // 2) * D + (m + 1) * P), slice((t % 2) * 512, (t % 2) * 512 + 512)
                sp.dma_start(xq_hi[rows, cols], hi[:, j % 2, :].bitcast(F32)).then_inc(s[f"cq_st{j % 2}"], 16)
                sp.dma_start(xq_lo[rows, cols], lo[:, j % 2, :].bitcast(F32)).then_inc(s[f"cq_st{j % 2}"], 16)
            for n in range(2):
                sp.wait_ge(s[f"cq_st{n}"], 32 * 8)

            sp.wait_ge(s["tbl_ok"], 1)
            dense = [sp.value_load(tbl[0:1, b:b + 1], min_val=0, max_val=1) for b in range(B)]
            group = [sp.value_load(tbl[0:1, 2 + b:3 + b], min_val=0, max_val=NG - 1) for b in range(B)]

            def context_slot(k, n, b, slot, g):
                sp.wait_ge(k["done"], 6 * n + 1)
                sp.sem_inc(s["passed"], 1)
                sp.dma_start(cx, ctxT[:, ds(g * GK + b * SK, GK)].rearrange("(k p) t -> p k t", p=P)).then_inc(k["ctx"], 16)
                sp.wait_ge(k["done"], 6 * n + 7)
                sp.sem_inc(s["passed"], 1)
                for dst, src in ((xk_hi, hi4), (xk_lo, lo4)):
                    sp.dma_start(dst[ds(slot * D + b * NG * D, D), :].rearrange("(m p) t -> p m t", p=P), src.bitcast(F32))\
                      .then_inc(k["st"], 16)
                for c in range(2):
                    sp.dma_start(xv_sc[ds(slot * H * P + b * NG * H * P, H * P), c * DH:(c + 1) * DH].rearrange("(h p) d -> p h d", p=P),
                                 cv_stage[:, c, :].rearrange("p (h d) -> p h d", d=DH)).then_inc(k["st"], 16)
                sp.wait_ge(k["st"], 64 * n + 128)
                sp.sem_inc(s["passed"], 1)

            for b in range(B):
                context_slot(kv[2], b, b, 0, group[b])
            for b in range(B):
                with sp.If(dense[b]):
                    with sp.Fori(1, NG) as g:
                        context_slot(kv[b], g - 1, b, g, g)

            def cross_load(b, row4, g):
                load_head("c", g, b * D + row4 * 128 + g * 32, b * NG * D + row4 * 128 + g * 32,
                          b * NG * H * P + row4 * 4 * P + g * P, (xq_hi, xq_lo), (xk_hi, xk_lo), xv_sc, GK)

            def rest_loads(b, n, h):
                r = rest[b]
                with sp.If(dense[b]):
                    with sp.Fori(1, NG) as slot:
                        sp.wait_ge(r["free"], n + slot)
                        sp.sem_inc(s["passed"], 1)
                        row = slot * D + (b * NG * D + h * DH)
                        for dst, src in ((0, xk_hi), (1, xk_lo), (2, xk_hi)):
                            sp.dma_start(kx[32 * dst:32 * dst + 32, :].bitcast(F32), src[ds(row, DH), :]).then_inc(r["load"], 16)
                        sp.dma_start(vx[:, :, 0:DH], xv_sc[ds(slot * H * P + (b * NG * H * P + h * P), P), :]
                                     .rearrange("p (c d) -> p c d", d=DH)).then_inc(r["load"], 16)
                        sp.dma_start(mx[:, :, :], mask_sc[b * S:(b + 1) * S, ds(slot * GK, GK)]
                                     .rearrange("(i p) k -> p i k", p=P)).then_inc(r["load"], 16)

            for b in range(B):
                if b == 0:
                    for g in range(3):
                        cross_load(0, 0, g)
                else:
                    sp.wait_ge(s["c_unit"], 16 * b + 1)
                sp.dma_start(mask0[:, :, :], mask_sc[b * S:(b + 1) * S, ds(group[b] * GK, GK)]
                             .rearrange("(i p) k -> p i k", p=P)).then_inc(s["c_mask"], 16)
                rest_loads(b, 0, 0)
                rest_loads(b, 7, 1)
                row_of_maxima("c", 0, 16 * b)

                def cross_units(j, last=False):
                    for g in range(4):
                        n = 14 + 14 * (4 * j + g)
                        if last and g == 3:
                            n = n - 7
                        if not (last and g > 0 and b == B - 1):
                            sp.wait_ge(s["c_unit"], 16 * b + 4 * j + g + 1)
                            sp.sem_inc(s["passed"], 1)
                            if last and g > 0:
                                cross_load(b + 1, 0, g - 1)
                            else:
                                cross_load(b, j + (g + 3) // 4, (g + 3) % 4)
                        if not (last and g >= 2):
                            rest_loads(b, n, 4 * j + g + 2)
                        if not (last and g == 3):
                            row_of_maxima("c", (g + 1) % 4, 16 * b + 4 * j + g + 1)
                        rest_loads(b, n if last and g >= 2 else n + 7, 4 * j + g)

                with sp.Fori(0, 3) as j:
                    cross_units(j)
                cross_units(3, last=True)

            for e in range(4):
                sp.dma_start(W[e][:, :, :], ew[e * D:(e + 1) * D, :].rearrange("(k p) n -> p k n", p=P)).then_inc(s[f"f_w{e}"], 16)
            out_stage(1)
            sp.dma_start(W[4][:, :, :], ew[4 * D:5 * D, :].rearrange("(k p) n -> p k n", p=P)).then_inc(s["f_w4"], 16)
            sp.wait_ge(s["o_tr1"], NT)
            sp.dma_start(y, x_sc[1].rearrange("(i p) n -> p i n", p=P)).then_inc(s["f_x"], 16)
            for e in range(5, E):
                sp.wait_ge(s["f_mm"], NT * (e - 4))
                sp.dma_start(W[e - 5][:, :, :], ew[e * D:(e + 1) * D, :].rearrange("(k p) n -> p k n", p=P))\
                  .then_inc(s[f"f_w{e - 5}"], 16)
            for i in range(NT):
                sp.wait_ge(s["f_n"], i + 1)
                sp.dma_start(out[i * P:(i + 1) * P, :], y[:, i, :]).then_inc(s["f_out"], 16)
            sp.wait_ge(s["f_out"], 16 * NT)

        @block.gpsimd
        def _(pool):
            nc.gpsimd.memset(ident[:, :], 0.0).then_inc(s["consts"], 1)
            nc.gpsimd.memset(neg_ident[:, :], 0.0).then_inc(s["consts"], 1)
            nc.gpsimd.memset(vst[:, :, :, :], 1.0).then_inc(s["consts"], 1)
            nc.gpsimd.memset(vx[:, :, :], 1.0).then_inc(s["consts"], 1)
            pool.wait_ge(s["consts"], 4)
            nc.gpsimd.memset(kst[96:97, :, :].bitcast(F32), -1.0).then_inc(s["consts"], 1)
            pool.wait_ge(s["consts"], 5)
            nc.gpsimd.memset(kx[96:97, :].bitcast(F32), -1.0).then_inc(s["consts"], 1)
            pool.wait_ge(s["consts"], 6)
            nc.gpsimd.memset(eps_s[:, :], EPS).then_inc(s["consts"], 1)
            pool.wait_ge(s["consts"], 7)
            nc.gpsimd.affine_select(out=ident[:, :], in_=ident[:, :], compare_op=ALU.not_equal, fill=1.0, base=0,
                                    pattern=[[-1, P]], channel_multiplier=1).then_inc(s["consts"], 1)
            nc.gpsimd.affine_select(out=neg_ident[:, :], in_=neg_ident[:, :], compare_op=ALU.not_equal, fill=MASKED, base=0,
                                    pattern=[[-1, P]], channel_multiplier=1).then_inc(s["consts"], 1)
            nc.gpsimd.iota(iota8[:, :], pattern=[[1, E]], base=0, channel_multiplier=0,
                           allow_small_or_imprecise_dtypes=True).then_inc(s["consts"], 1)
            for i in range(NT + 1):
                if i < NT:
                    if i >= 2:
                        pool.wait_ge(s["mask_eq"], i - 1)
                    pool.dma_start(mask_i[:, i % 2, :], mask[i * P:(i + 1) * P, :]).then_inc(s[f"mask_in{i % 2}"], 16)
                if i >= 1:
                    pool.wait_ge(s["mask_eq"], i)
                    pool.dma_start(mask_sc[(i - 1) * P:i * P, :], mask_b[:, (i - 1) % 2, :]).then_inc(s[f"mask_st{(i - 1) % 2}"], 16)
            for n in range(2):
                pool.wait_ge(s[f"mask_st{n}"], 16 * NT // 2)
            pool.wait_ge(s["grp_ok"], 1)
            nc.gpsimd.partition_all_reduce(grp_r[:, :, :].rearrange("p b g -> p (b g)"),
                                           grp_m[:, :, :].rearrange("p b g -> p (b g)"), P, RMAX).then_inc(s["grp_all"], 1)
            for a in range(2):
                for t in range(4):
                    pool.wait_ge(s[f"o_x{a}"], 16 * t + 16)
                    if a == 0 and t == 0:
                        pool.wait_ge(s["bias"], 16 * 11)
                    for i in range(4):
                        nc.gpsimd.tensor_tensor(xres[:, i, :], xres[:, i, :], bo_s[a][:, :], ALU.add).then_inc(s[f"o_xb{a}"], 1)

        @block.scalar
        def _(act):
            for n in range(2):
                act.sem_inc(s[f"s_out{n}"], 64)
                act.sem_inc(s[f"c_out{n}"], 64)
            for pre in "sc":
                act.sem_inc(s[f"{pre}_exp"], 2)
                act.sem_inc(s[f"{pre}_acc"], 1)
                act.sem_inc(s[f"{pre}_arow"], 1)
                act.sem_inc(s[f"{pre}_mrow"], 16)
            act.wait_ge(s["bias"], 16 * 11)
            for n, j in enumerate(HEADJOBS):
                t, kind = JOBS[j]
                act.wait_ge(s["pj_mm"], j + 1)
                if n >= 2:
                    act.wait_ge(s[f"pj_st{n % 2}"], 32 * (n // 2))
                bias = bk_s[:, 0:1] if kind == "k" else bq_s[:, kind:kind + 1]
                nc.scalar.activation(hi[:, n % 2, :], ps[:, j % 8, :], ACT.Identity, bias=bias).then_inc(s["pj_hi"], 1)

            def copy_maxima(pre, n):
                act.wait_ge(s[f"{pre}_at"], n + 3)
                act.wait_ge(s[f"{pre}_mrow"], 16 * n + 16)
                nc.scalar.activation(m_row[:, :], ps[0:QT, BANK_T, 0:P], ACT.Copy).then_inc(s[f"{pre}_arow"], 1)

            def exps(pre, n, c):
                act.wait_ge(s[f"{pre}_score"], n + 1)
                act.wait_ge(s[f"{pre}_pv"], n + 1)
                nc.scalar.activation(probs[:, c % 2, :].rearrange("p (a b) -> p a b", a=2),
                                     ps[:, BANK_S + 2 * (c % 2):BANK_S + 2 * (c % 2) + 2, :],
                                     ACT.Exp, scale=SCALE).then_inc(s[f"{pre}_exp"], 1)

            def store_unit(pre, a, u, uses, row, col, par):
                act.wait_ge(s[f"{pre}_unit"], u + 2)
                act.wait_ge(s[f"{pre}_out{par}"], 64 * uses + 64)
                nc.scalar.activation(o_stage[:, par, :], ps[:, BANK_O, :], ACT.Copy).then_inc(s[f"{pre}_acc"], 1)
                act.wait_ge(s[f"{pre}_acc"], u + 2)
                for half in range(2):
                    cols = slice(col + half * 512, col + half * 512 + 512)
                    act.dma_start(num_sc[a][ds(row * DH, DH), cols], o_stage[64 * half:64 * half + DH, par, :])\
                       .then_inc(s[f"{pre}_out{par}"], 16)
                    act.dma_start(den_sc[a][ds(row, 1), cols], o_stage[64 * half + DH:64 * half + DH + 1, par, :])\
                       .then_inc(s[f"{pre}_out{par}"], 16)

            copy_maxima("s", 0)
            for b in range(B):
                def self_units(j, last=False):
                    for g in range(4):
                        u = 16 * b + 4 * j + g
                        for c in range(QT):
                            if c == 2 and not (last and g == 3 and b == B - 1):
                                copy_maxima("s", u + 1)
                            exps("s", 8 * u + c, c)
                        store_unit("s", 0, u, 8 * b + 2 * j + g // 2, 4 * j + g, b * S, g % 2)

                with act.Fori(0, 3) as j:
                    self_units(j)
                self_units(3, last=True)

            def norm_stage(a):
                for t in range(4):
                    for i in range(4):
                        act.wait_ge(s[f"o_var{a}"], 4 * t + i + 1)
                        nc.scalar.activation(sd[:, i, 0:1], mv[:, i, 1:2], ACT.Sqrt, bias=eps_s[:, 0:1]).then_inc(s[f"o_sd{a}"], 1)
                    for i in range(4):
                        act.wait_ge(s[f"o_tr{a}"], 4 * t + i + 1)
                        n = 4 * t + i
                        nc.scalar.activation(xt[:, :, n * P:(n + 1) * P], ps[:, 4 + n % 4, :].rearrange("p (k t) -> p k t", k=KC),
                                             ACT.Copy).then_inc(s[f"o_xt{a}"], 1)

            norm_stage(0)

            for j in range(16):
                act.wait_ge(s["pj_mm"], len(JOBS) + j + 1)
                if j >= 2:
                    act.wait_ge(s[f"cq_st{j % 2}"], 32 * (j // 2))
                nc.scalar.activation(hi[:, j % 2, :], ps[:, j % 8, :], ACT.Identity, bias=xbq_s[:, j % 4:j % 4 + 1]).then_inc(s["pj_hi"], 1)

            act.wait_ge(s["tbl_ok"], 1)
            dense = [act.value_load(tbl[0:1, b:b + 1], min_val=0, max_val=1) for b in range(B)]
            for n in range(2):
                act.wait_ge(s[f"cq_st{n}"], 32 * 8)

            def context_slot(k, n):
                for m in range(4):
                    act.wait_ge(k["mm"], 6 * n + m + 1)
                    act.wait_ge(k["st"], 64 * n + 64)
                    nc.scalar.activation(hi4[:, m, :], ps[:, m, 0:GK], ACT.Identity, bias=xbk_s[:, m:m + 1]).then_inc(k["hi"], 1)

            for b in range(B):
                context_slot(kv[2], b)
            for b in range(B):
                with act.If(dense[b]):
                    with act.Fori(0, NG - 1) as n:
                        context_slot(kv[b], n)

            for b in range(B):
                copy_maxima("c", 16 * b)

                def cross_units(j, last=False):
                    for g in range(4):
                        u = 4 * j + g
                        n = 16 * b + u
                        exps("c", 2 * n, 0)
                        exps("c", 2 * n + 1, 1)
                        if not (last and g == 3):
                            copy_maxima("c", n + 1)
                        r = rest[b]
                        with act.If(dense[b]):
                            act.wait_ge(s["c_pv"], 2 * n + 3)
                            with act.Fori(0, NG - 1) as sl:
                                for c in range(2):
                                    act.wait_ge(r["score"], 14 * u + sl * 2 + c + 1)
                                    act.wait_ge(r["pv"], 14 * u + sl * 2 + c + 1)
                                    nc.scalar.activation(probs[:, 0, :].rearrange("p (a b) -> p a b", a=2),
                                                         ps[:, BANK_S:BANK_S + 2, :], ACT.Exp, scale=SCALE).then_inc(r["exp"], 1)
                            act.wait_ge(r["pv"], 14 * u + 15)
                            act.sem_inc(s["passed"], 1)
                        store_unit("c", 1, n, 8 * b + 2 * j + g // 2, 4 * j + g, b * S, g % 2)

                with act.Fori(0, 3) as j:
                    cross_units(j)
                cross_units(3, last=True)
            norm_stage(1)

            for i in range(NT):
                act.wait_ge(s["f_mx"], i + 1)
                nc.scalar.activation(ex[:, i, :], lg[:, i, :], ACT.Exp, bias=nmx[:, i:i + 1],
                                     accum_out=ssum[:, i:i + 1]).then_inc(s["f_ex"], 1)
            for i in range(NT):
                act.wait_ge(s["f_wt"], i + 1)
                nc.scalar.activation(wselT[:, i, :], ps[0:E, i % 2, 0:P], ACT.Copy).then_inc(s["f_wtc"], 1)
            for i in range(NT):
                act.wait_ge(s["f_var"], i + 1)
                nc.scalar.activation(sd[:, i % 4, 0:1], mv[:, i % 4, 1:2], ACT.Sqrt, bias=eps_s[:, 0:1]).then_inc(s["f_sd"], 1)

        @block.tensor
        def _(pe):
            for pre in "sc":
                pe.sem_inc(s[f"{pre}_unit"], 1)
                pe.sem_inc(s[f"{pre}_pv"], 2)
                pe.sem_inc(s[f"{pre}_at"], 2)
            for r in rest:
                pe.sem_inc(r["free"], 1)
                pe.sem_inc(r["pv"], 1)
            mm = nc.tensor.matmul
            for j, (t, kind) in enumerate(JOBS):
                if j >= 8:
                    pe.wait_ge(s["pj_done"], j - 7)
                if j == 0:
                    pe.wait_ge(s["w_self"], 48)
                if kind == "k":
                    pe.wait_ge(s[f"xt{t}"], 16)
                if kind == "v":
                    for i in range(4):
                        for k in range(KC):
                            last = mm(ps[:, j % 8, i * P:(i + 1) * P], xt[:, k, t * 512 + i * P:t * 512 + (i + 1) * P],
                                      W[1][:, k, P:2 * P], start=(k == 0), stop=(k == KC - 1))
                else:
                    for k in range(KC):
                        w = W[1][:, k, 0:P] if kind == "k" else W[0][:, k, kind * P:(kind + 1) * P]
                        last = mm(ps[:, j % 8, :], w, xt[:, k, t * 512:(t + 1) * 512], start=(k == 0), stop=(k == KC - 1))
                last.then_inc(s["pj_mm"], 1)

            def scores(bank, st_buf, q_buf, c, masked=None):
                for half in range(2):
                    cols = slice(half * 512, half * 512 + 512)
                    last = mm(ps[:, bank + half, :], st_buf[:, c * P:(c + 1) * P], qst[:, q_buf, cols],
                              start=True, stop=True)
                    if masked is not None:
                        for i in range(4):
                            last = mm(ps[:, bank + half, i * P:(i + 1) * P], masked[:, 4 * half + i, c * P:(c + 1) * P],
                                      neg_ident[:, :], start=False, stop=True, skip_group_check=True)
                return last

            def weighted(v_buf, par, first, stop):
                for half in range(2):
                    last = mm(ps[64 * half:64 * half + 64, BANK_O, :], v_buf, probs[:, par, half * 512:half * 512 + 512],
                              start=first, stop=stop, skip_group_check=True)
                return last

            def transpose_maxima(pre, n, par):
                pe.wait_ge(s[f"{pre}_afin"], n + 2)
                pe.wait_ge(s[f"{pre}_arow"], n + 1)
                nc.tensor.transpose(ps[0:QT, BANK_T, 0:P], m_fin[:, par, :], ident[:, :]).then_inc(s[f"{pre}_at"], 1)

            def self_max(n, buf, i):
                for half in range(2):
                    pe.wait_ge(s["s_amax"], 16 * n + 2 * i + half + 1)
                    mm(ps[:, BANK_A + half, :], qst[0:96, buf, i * P:(i + 1) * P],
                       kst[0:96, buf, half * 512:half * 512 + 512], start=True, stop=True).then_inc(s["s_amm"], 1)

            pe.wait_ge(s["consts"], 10)
            pe.wait_ge(s["pj_done"], len(JOBS))
            for n in range(2):
                pe.wait_ge(s[f"s_stk{n}"], STK)
                for i in range(QT):
                    self_max(n, n, i)
            transpose_maxima("s", 0, 0)

            def self_units(j, last=False):
                for g in range(4):
                    u = 4 * j + g
                    ahead = not (last and g >= 2)
                    buf2 = (g + 2) % 4
                    pe.wait_ge(s["s_mrow"], 16 * u + 32)
                    for c in range(QT + 1):
                        if c < QT:
                            pe.wait_ge(s["s_exp"], 8 * u + c + 1)
                            scores(BANK_S + 2 * (c % 2), kst[:, g, :], g, c).then_inc(s["s_score"], 1)
                        if c == 2 and not (last and g == 3):
                            transpose_maxima("s", u + 1, (g + 1) % 2)
                        if c >= 1:
                            if c == 1:
                                pe.wait_ge(s["s_acc"], u + 1)
                            pe.wait_ge(s["s_exp"], 8 * u + c + 2)
                            weighted(vst[:, g, c - 1, :], (c - 1) % 2, c == 1, c == QT).then_inc(s["s_pv"], 1)
                        if ahead and c < QT:
                            if c == 0:
                                pe.wait_ge(s[f"s_stk{buf2}"], STK * (j + (g + 2) // 4) + STK)
                            self_max(u + 2, buf2, c)
                    pe.wait_ge(s["s_pv"], 8 * u + 10)
                    pe.sem_inc(s["s_unit"], 1)

            with pe.Fori(0, 7) as j:
                self_units(j)
            self_units(7, last=True)

            def out_stage(a, w):
                if a == 0:
                    pe.wait_ge(s["w_out"], 16)
                    pe.wait_ge(s["s_acc"], 33)
                else:
                    pe.wait_ge(s["w_xo"], 16)
                    pe.wait_ge(s["c_acc"], 33)

                def turn(t):
                    for i in range(4):
                        n = 4 * t + i
                        pe.wait_ge(s[f"o_y{a}"], n + 1)
                        if n >= 4:
                            pe.wait_ge(s[f"o_xt{a}"], n - 3)
                        for k in range(KC):
                            last = nc.tensor.transpose(ps[:, 4 + n % 4, k * P:(k + 1) * P], xnew[:, i, k * P:(k + 1) * P], ident[:, :])
                        last.then_inc(s[f"o_tr{a}"], 1)

                for t in range(4):
                    pe.wait_ge(s[f"o_ready{a}"], t + 1)
                    for i in range(4):
                        n = 4 * t + i
                        if n >= 4:
                            pe.wait_ge(s[f"o_add{a}"], n - 3)
                        for k in range(KC):
                            last = mm(ps[:, n % 4, :], onum[:, k, i * P:(i + 1) * P], w[:, k, :], start=(k == 0), stop=(k == KC - 1))
                        last.then_inc(s[f"o_mm{a}"], 1)
                    turn(t)

            out_stage(0, W[2])
            pe.wait_ge(s["w_xq"], 16)
            pe.wait_ge(s["o_xt0"], 16)
            for j in range(16):
                if j >= 8:
                    pe.wait_ge(s["pj_done"], len(JOBS) + j - 7)
                for k in range(KC):
                    last = mm(ps[:, j % 8, :], W[3][:, k, (j % 4) * P:(j % 4 + 1) * P], xt[:, k, (j // 4) * 512:(j // 4 + 1) * 512],
                              start=(k == 0), stop=(k == KC - 1))
                last.then_inc(s["pj_mm"], 1)

            pe.wait_ge(s["tbl_ok"], 1)
            dense = [pe.value_load(tbl[0:1, b:b + 1], min_val=0, max_val=1) for b in range(B)]
            pe.wait_ge(s["w_xk"], 16)
            pe.wait_ge(s["w_xv"], 16)
            pe.wait_ge(s["pj_done"], len(JOBS) + 16)

            def context_slot(k_, n):
                pe.wait_ge(k_["ctx"], 16 * n + 16)
                for m in range(4):
                    for k in range(KC):
                        last = mm(ps[:, m, 0:GK], W[0][:, k, m * P:(m + 1) * P], cx[:, k, :], start=(k == 0), stop=(k == KC - 1))
                    last.then_inc(k_["mm"], 1)
                for c in range(2):
                    for k in range(KC):
                        last = mm(ps[:, 4 + c, :], cx[:, k, c * P:(c + 1) * P], W[1][:, k, :], start=(k == 0), stop=(k == KC - 1))
                    last.then_inc(k_["mm"], 1)

            for b in range(B):
                context_slot(kv[2], b)
            for b in range(B):
                with pe.If(dense[b]):
                    with pe.Fori(0, NG - 1) as n:
                        context_slot(kv[b], n)
                        pe.wait_ge(kv[b]["done"], n * 6 + 7)
                        pe.sem_inc(s["passed"], 1)
            pe.wait_ge(kv[2]["done"], 13)

            def max_pair(bank, q_buf, keys, masked, f):
                for i in range(2):
                    mm(ps[:, bank, i * GK:(i + 1) * GK], qst[0:96, q_buf, (2 * f + i) * P:(2 * f + i + 1) * P], keys,
                       start=(i == 0), stop=True, skip_group_check=True)
                for i in range(2):
                    last = mm(ps[:, bank, i * GK:(i + 1) * GK], neg_ident[:, :], masked[:, 2 * f + i, :],
                              start=False, stop=True, skip_group_check=True)
                return last

            def cross_max(b, a, buf, n):
                r = rest[b]
                with pe.If(dense[b]):
                    pe.wait_ge(s["c_amax"], 64 * b + a * 4 + 2)
                    pe.sem_inc(s["passed"], 1)
                    with pe.Fori(0, NG - 1) as sl:
                        pe.wait_ge(r["load"], sl * 80 + n * 80 + 80)
                        for f in range(4):
                            pe.wait_ge(r["amax"], a * 28 + sl * 4 + f + 1)
                            last = max_pair(BANK_A, buf, kx[0:96, :], mx, f)
                            last.then_inc(r["amm"], 1)
                        pe.wait_ge(r["amm"], a * 28 + sl * 4 + 4)
                        pe.sem_inc(r["free"], 1)
                    pe.wait_ge(r["amax"], a * 28 + 29)
                    pe.sem_inc(s["passed"], 1)
                for f in range(4):
                    pe.wait_ge(s["c_amax"], 64 * b + a * 4 + f + 1)
                    max_pair(BANK_A + f % 2, buf, kst[0:96, buf, 0:GK], mask0, f).then_inc(s["c_amm"], 1)

            for b in range(B):
                pe.wait_ge(s["c_mask"], 16 * b + 16)
                for n in range(2):
                    pe.wait_ge(s[f"c_stk{n}"], STK * (4 * b + 1))
                    cross_max(b, n, n, 7 * n)
                transpose_maxima("c", 16 * b, 0)

                def cross_units(j, last=False):
                    for g in range(4):
                        u = 4 * j + g
                        n = 16 * b + u
                        before = 14 + 14 * u
                        if last and g == 3:
                            before = before - 7
                        ahead = not (last and g >= 2)
                        buf2 = (g + 2) % 4
                        pe.wait_ge(s["c_mrow"], 16 * n + 32)
                        for c in range(2):
                            pe.wait_ge(s["c_exp"], 2 * n + c + 1)
                            scores(BANK_S + 2 * c, kst[:, g, :], g, c, masked=mask0).then_inc(s["c_score"], 1)
                        if ahead:
                            pe.wait_ge(s[f"c_stk{buf2}"], STK * (4 * b + j + (g + 2) // 4) + STK)
                            cross_max(b, u + 2, buf2, before)
                        if not (last and g == 3):
                            transpose_maxima("c", n + 1, (g + 1) % 2)
                        pe.wait_ge(s["c_acc"], n + 1)
                        pe.wait_ge(s["c_exp"], 2 * n + 3)
                        weighted(vst[:, g, 0, :], 0, True, True).then_inc(s["c_pv"], 1)
                        r = rest[b]
                        taken = before + 7 if ahead else before
                        with pe.If(dense[b]):
                            with pe.Fori(0, NG - 1) as sl:
                                pe.wait_ge(r["load"], sl * 80 + taken * 80 + 80)
                                for c in range(2):
                                    scores(BANK_S, kx, g, c, masked=mx).then_inc(r["score"], 1)
                                    pe.wait_ge(r["exp"], 14 * u + sl * 2 + c + 1)
                                    weighted(vx[:, c, :], 0, False, True).then_inc(r["pv"], 1)
                                pe.wait_ge(r["pv"], 14 * u + sl * 2 + 3)
                                pe.sem_inc(r["free"], 1)
                        pe.wait_ge(s["c_exp"], 2 * n + 4)
                        weighted(vst[:, g, 1, :], 1, False, True).then_inc(s["c_pv"], 1)
                        pe.wait_ge(s["c_pv"], 2 * n + 4)
                        pe.sem_inc(s["c_unit"], 1)

                with pe.Fori(0, 3) as j:
                    cross_units(j)
                cross_units(3, last=True)
            out_stage(1, W[4])

            pe.wait_ge(s["o_xt1"], 16)
            for i in range(NT):
                for k in range(KC):
                    last = mm(ps[:, 0, i * E:(i + 1) * E], xt[:, k, i * P:(i + 1) * P], rw_s[:, k, :],
                              start=(i == 0 and k == 0), stop=(k == KC - 1), skip_group_check=True)
            last.then_inc(s["f_lg"], 1)
            pe.wait_ge(s["f_l"], 1)
            for i in range(NT):
                pe.wait_ge(s["f_g"], i + 1)
                if i >= 2:
                    pe.wait_ge(s["f_wtc"], i - 1)
                nc.tensor.transpose(ps[0:E, i % 2, 0:P], wsel[:, i, :], ident[:, :]).then_inc(s["f_wt"], 1)
            for i in range(NT):
                pe.wait_ge(s["f_wtc"], i + 1)
                if i >= 4:
                    pe.wait_ge(s["f_y"], i - 3)
                mm(ps[:, 4 + i % 4, :], wselT[:, i, :], eb_s[:, :], start=True, stop=True).then_inc(s["f_bmm"], 1)
            for e in range(E):
                pe.wait_ge(s[f"f_w{e % 5}"], 16 * (e // 5 + 1))
                for i in range(NT):
                    n = NT * e + i
                    if n < 4:
                        pe.wait_ge(s["f_wtc"], NT)
                    if n >= 4:
                        pe.wait_ge(s["f_acc"], n - 3)
                    for k in range(KC):
                        last = mm(ps[:, n % 4, :], xt[:, k, i * P:(i + 1) * P], W[e % 5][:, k, :], start=(k == 0), stop=(k == KC - 1))
                    last.then_inc(s["f_mm"], 1)

        @block.vector
        def _(dve):
            for pre in "sc":
                dve.sem_inc(s[f"{pre}_amax"], 2)
                dve.sem_inc(s[f"{pre}_afin"], 1)
            for k in kv:
                dve.sem_inc(k["done"], 1)
                dve.sem_inc(k["st"], 64)
            for r in rest:
                dve.sem_inc(r["amax"], 1)
            dve.wait_ge(s["bias"], 16 * 11)
            tile = [0]

            def mask_tile():
                i = tile[0]
                tile[0] += 1
                dve.wait_ge(s[f"mask_in{i % 2}"], 16 * (i // 2 + 1))
                if i >= 2:
                    dve.wait_ge(s[f"mask_st{i % 2}"], 16 * (i // 2))
                    dve.wait_ge(s["mask_red"], i - 1)
                nc.vector.tensor_scalar(mask_b[:, i % 2, :], mask_i[:, i % 2, :], 1.0, None, ALU.is_equal).then_inc(s["mask_eq"], 1)
                dve.wait_ge(s["mask_eq"], i + 1)
                nc.vector.tensor_reduce(grp[:, i // QT, i % QT, 0:NG], mask_b[:, i % 2, :].rearrange("p (g k) -> p g k", g=NG),
                                        AX.X, ALU.min).then_inc(s["mask_red"], 1)

            n = v = 0
            for j, (t, kind) in enumerate(JOBS):
                if kind == "v":
                    dve.wait_ge(s["pj_mm"], j + 1)
                    if v >= 2:
                        dve.wait_ge(s[f"pv_st{v % 2}"], 64 * (v // 2))
                    nc.vector.tensor_tensor(v_stage[:, v % 2, :].rearrange("p (i n) -> p i n", i=4),
                                            ps[:, j % 8, :].rearrange("p (i n) -> p i n", i=4),
                                            bv_s[:, :].rearrange("p (o n) -> p o n", o=1).broadcast_to([P, 4, P]),
                                            ALU.add).then_inc(s["pj_done"], 1)
                    v += 1
                else:
                    dve.wait_ge(s["pj_hi"], n + 1)
                    if n >= 2:
                        dve.wait_ge(s[f"pj_st{n % 2}"], 32 * (n // 2))
                    bias = bk_s[:, 0:1] if kind == "k" else bq_s[:, kind:kind + 1]
                    nc.vector.scalar_tensor_tensor(out=lo[:, n % 2, :], in0=ps[:, j % 8, :], scalar=bias,
                                                   in1=hi[:, n % 2, :].bitcast(F32), op0=ALU.add, op1=ALU.subtract)\
                      .then_inc(s["pj_done"], 1)
                    n += 1
                if j >= 4 and tile[0] < NT:
                    mask_tile()
            while tile[0] < NT:
                mask_tile()
            dve.wait_ge(s["mask_red"], NT)
            step = [0]

            def flag(ins):
                step[0] += 1
                ins.then_inc(s["flag"], 1)
                dve.wait_ge(s["flag"], step[0])

            flag(nc.vector.tensor_reduce(grp[:, :, :, NG], grp[:, :, :, 0:NG], AX.X, ALU.min))
            flag(nc.vector.tensor_scalar(grp[:, :, :, 0:NG], grp[:, :, :, 0:NG], -1.0, 1.0, ALU.mult, ALU.add))
            nc.vector.tensor_reduce(grp_m[:, :, :], grp[:, :, :, :].rearrange("p b i g -> p b g i"), AX.X, ALU.max)\
              .then_inc(s["grp_ok"], 1)

            def final_max(pre, n, par, src):
                dve.wait_ge(s[f"{pre}_at"], n + 1)
                if pre == "s":
                    nc.vector.tensor_reduce(m_fin[:, par, :], m_part[:, :, :], AX.X, ALU.max).then_inc(s["s_afin"], 1)
                else:
                    nc.vector.tensor_tensor(m_fin[:, par, :], m_slot[:, :], m_rest[:, :], ALU.max).then_inc(s["c_afin"], 1)

            def self_max(n, par):
                dve.wait_ge(s["s_afin"], n + 1)
                for k in range(2 * QT):
                    dve.wait_ge(s["s_amm"], 16 * n + k + 1)
                    nc.vector.reduce_max(m_part[:, k // 2, k % 2:k % 2 + 1], ps[:, BANK_A + k % 2, :], AX.X).then_inc(s["s_amax"], 1)
                dve.wait_ge(s["s_amax"], 16 * n + 18)
                final_max("s", n, par, None)

            with dve.Fori(0, 16) as j:
                self_max(2 * j, 0)
                self_max(2 * j + 1, 1)

            def out_stage(a):
                dve.wait_ge(s[f"r_den{a}"], 16)
                nc.vector.reciprocal(den_s, den_s).then_inc(s[f"r_rec{a}"], 1)
                for t in range(4):
                    dve.wait_ge(s[f"o_num{a}"], 80 * (t + 1))
                    nc.vector.tensor_tensor(onum, onum, orec, ALU.mult).then_inc(s[f"o_ready{a}"], 1)
                    if t:
                        dve.wait_ge(s[f"o_yst{a}"], 16 * t)
                        dve.wait_ge(s[f"o_tr{a}"], 4 * t)
                    for i in range(4):
                        n = 4 * t + i
                        dve.wait_ge(s[f"o_mm{a}"], n + 1)
                        dve.wait_ge(s[f"o_xb{a}"], n + 1)
                        nc.vector.tensor_tensor(xnew[:, i, :], ps[:, n % 4, :], xres[:, i, :], ALU.add).then_inc(s[f"o_add{a}"], 1)
                        dve.wait_ge(s[f"o_add{a}"], n + 1)
                        nc.vector.bn_stats(st[:, i, :], xnew[:, i, :]).then_inc(s[f"o_st{a}"], 1)
                        dve.wait_ge(s[f"o_st{a}"], n + 1)
                        nc.vector.bn_aggr(mv[:, i, :], st[:, i, :]).then_inc(s[f"o_var{a}"], 1)
                    for i in range(4):
                        n = 4 * t + i
                        dve.wait_ge(s[f"o_sd{a}"], n + 1)
                        nc.vector.reciprocal(sd[:, i, 1:2], sd[:, i, 0:1]).then_inc(s[f"o_rs{a}"], 1)
                        dve.wait_ge(s[f"o_rs{a}"], n + 1)
                        nc.vector.tensor_scalar(xnew[:, i, :], xnew[:, i, :], mv[:, i, 0:1], sd[:, i, 1:2],
                                                ALU.subtract, ALU.mult).then_inc(s[f"o_y{a}"], 1)

            out_stage(0)
            for j in range(16):
                dve.wait_ge(s["pj_hi"], len(HEADJOBS) + j + 1)
                if j >= 2:
                    dve.wait_ge(s[f"cq_st{j % 2}"], 32 * (j // 2))
                nc.vector.scalar_tensor_tensor(out=lo[:, j % 2, :], in0=ps[:, j % 8, :], scalar=xbq_s[:, j % 4:j % 4 + 1],
                                               in1=hi[:, j % 2, :].bitcast(F32), op0=ALU.add, op1=ALU.subtract)\
                  .then_inc(s["pj_done"], 1)

            dve.wait_ge(s["grp_all"], 1)
            for b in range(B):
                g = grp_r[0:1, b, :]
                flag(nc.vector.reduce_sum(fl[:, b, 0:1], g[:, 0:NG], AX.X))
                flag(nc.vector.tensor_scalar(fl[:, b, 1:2], g[:, NG:NG + 1], 2.0, fl[:, b, 0:1], ALU.mult, ALU.add))
                flag(nc.vector.tensor_scalar(fl[:, b, 2:3], fl[:, b, 1:2], 1.5, None, ALU.is_gt))
                flag(nc.vector.tensor_tensor(fl[:, 2 + b, :], g[:, 0:NG], iota8[0:1, :], ALU.mult))
                flag(nc.vector.reduce_max(fl[:, b, 3:4], fl[:, 2 + b, :], AX.X))
                flag(nc.vector.tensor_scalar(fl[:, b, 4:5], fl[:, b, 2:3], -1.0, 1.0, ALU.mult, ALU.add))
                flag(nc.vector.tensor_tensor(fl[:, b, 5:6], fl[:, b, 4:5], fl[:, b, 3:4], ALU.mult))
                flag(nc.vector.tensor_copy(tbl[:, b:b + 1], fl[:, b, 2:3]))
                flag(nc.vector.tensor_copy(tbl[:, 2 + b:3 + b], fl[:, b, 5:6]))
            dve.sem_inc(s["tbl_ok"], 1)
            dense = [dve.value_load(tbl[0:1, b:b + 1], min_val=0, max_val=1) for b in range(B)]

            for n in range(2):
                dve.wait_ge(s[f"cq_st{n}"], 32 * 8)

            def context_slot(k, n):
                for m in range(4):
                    dve.wait_ge(k["hi"], 4 * n + m + 1)
                    nc.vector.scalar_tensor_tensor(out=lo4[:, m, :], in0=ps[:, m, 0:GK], scalar=xbk_s[:, m:m + 1],
                                                   in1=hi4[:, m, :].bitcast(F32), op0=ALU.add, op1=ALU.subtract)\
                      .then_inc(k["done"], 1)
                for c in range(2):
                    dve.wait_ge(k["mm"], 6 * n + 5 + c)
                    nc.vector.tensor_tensor(cv_stage[:, c, :], ps[:, 4 + c, :], xbv_s[:, :], ALU.add).then_inc(k["done"], 1)

            for b in range(B):
                dve.wait_ge(kv[2]["st"], 64 * b + 64)
                context_slot(kv[2], b)
            for b in range(B):
                with dve.If(dense[b]):
                    with dve.Fori(0, NG - 1) as n:
                        dve.wait_ge(kv[b]["st"], n * 64 + 64)
                        context_slot(kv[b], n)

            def cross_max(b, a, par):
                r = rest[b]
                n = 16 * b + a
                with dve.If(dense[b]):
                    dve.wait_ge(s["c_afin"], n + 1)
                    dve.wait_ge(r["top"], 8 * a + 1)
                    nc.vector.memset(m_rest[:, :], MASKED).then_inc(r["top"], 1)
                    with dve.Fori(0, NG - 1) as sl:
                        dve.wait_ge(r["top"], a * 8 + sl + 2)
                        for f in range(4):
                            dve.wait_ge(r["amm"], a * 28 + sl * 4 + f + 1)
                            nc.vector.reduce_max(m_slot[:, 2 * f:2 * f + 2], ps[:, BANK_A, :].rearrange("p (i k) -> p i k", i=2), AX.X)\
                              .then_inc(r["amax"], 1)
                        dve.wait_ge(r["amax"], a * 28 + sl * 4 + 5)
                        nc.vector.tensor_tensor(m_rest[:, :], m_rest[:, :], m_slot[:, :], ALU.max).then_inc(r["top"], 1)
                    dve.wait_ge(r["top"], a * 8 + 9)
                    dve.sem_inc(s["passed"], 1)
                dve.wait_ge(s["c_afin"], n + 1)
                for f in range(4):
                    dve.wait_ge(s["c_amm"], 4 * n + f + 1)
                    nc.vector.reduce_max(m_slot[:, 2 * f:2 * f + 2], ps[:, BANK_A + f % 2, :].rearrange("p (i k) -> p i k", i=2), AX.X)\
                      .then_inc(s["c_amax"], 1)
                dve.wait_ge(s["c_amax"], 4 * n + 6)
                final_max("c", n, par, None)

            for b in range(B):
                dve.wait_ge(s["c_afin"], 16 * b + 1)
                nc.vector.memset(m_rest[:, :], MASKED).then_inc(rest[b]["top"], 1)
                dve.wait_ge(rest[b]["top"], 1)
                with dve.Fori(0, 8) as j:
                    cross_max(b, 2 * j, 0)
                    cross_max(b, 2 * j + 1, 1)
            out_stage(1)

            dve.wait_ge(s["f_lg"], 1)
            nc.vector.tensor_tensor(lg[:, :, :], ps[:, 0, 0:NT * E].rearrange("p (i e) -> p i e", i=NT),
                                    rb_s[:, :].rearrange("p (o e) -> p o e", o=1).broadcast_to([P, NT, E]), ALU.add).then_inc(s["f_l"], 1)
            dve.wait_ge(s["f_l"], 1)
            nc.vector.tensor_reduce(nmx[:, :], lg[:, :, :], AX.X, ALU.max, negate=True).then_inc(s["f_l"], 1)
            dve.wait_ge(s["f_l"], 2)
            dve.sem_inc(s["f_mx"], NT)
            for i in range(NT):
                dve.wait_ge(s["f_ex"], i + 1)
                nc.vector.max(mx8[:, i, :], ex[:, i, :]).then_inc(s["f_ix"], 1)
                dve.wait_ge(s["f_ix"], 2 * i + 1)
                nc.vector.max_index(ix8[:, i, :], mx8[:, i, :], ex[:, i, :]).then_inc(s["f_ix"], 1)
            dve.wait_ge(s["f_ix"], 2 * NT)
            nc.vector.reciprocal(ssum[:, :], ssum[:, :]).then_inc(s["f_ix"], 1)
            nc.vector.tensor_copy(ixf[:, :], ix8[:, :, 0]).then_inc(s["f_ix"], 1)
            dve.wait_ge(s["f_ix"], 2 * NT + 2)
            nc.vector.tensor_tensor(gate[:, :], ssum[:, :], mx8[:, :, 0], ALU.mult).then_inc(s["f_ix"], 1)
            dve.wait_ge(s["f_ix"], 2 * NT + 3)
            for i in range(NT):
                nc.vector.tensor_scalar(wsel[:, i, :], iota8[:, :], ixf[:, i:i + 1], gate[:, i:i + 1],
                                        ALU.is_equal, ALU.mult).then_inc(s["f_g"], 1)
            dve.wait_ge(s["f_x"], 16)
            for i in range(NT):
                dve.wait_ge(s["f_bmm"], i + 1)
                nc.vector.tensor_tensor(y[:, i, :], ps[:, 4 + i % 4, :], y[:, i, :], ALU.add).then_inc(s["f_y"], 1)
            dve.wait_ge(s["f_y"], NT)
            dve.wait_ge(s["f_g"], NT)
            for e in range(E):
                for i in range(NT):
                    n = NT * e + i
                    dve.wait_ge(s["f_mm"], n + 1)
                    if e:
                        dve.wait_ge(s["f_acc"], n - NT + 1)
                    nc.vector.scalar_tensor_tensor(out=y[:, i, :], in0=ps[:, n % 4, :], scalar=wsel[:, i, e:e + 1],
                                                   in1=y[:, i, :], op0=ALU.mult, op1=ALU.add).then_inc(s["f_acc"], 1)
            dve.wait_ge(s["f_acc"], NT * E)
            for i in range(NT):
                if i >= 4:
                    dve.wait_ge(s["f_n"], i - 3)
                nc.vector.bn_stats(st[:, i % 4, :], y[:, i, :]).then_inc(s["f_st"], 1)
                dve.wait_ge(s["f_st"], i + 1)
                nc.vector.bn_aggr(mv[:, i % 4, :], st[:, i % 4, :]).then_inc(s["f_var"], 1)
                dve.wait_ge(s["f_sd"], i + 1)
                nc.vector.reciprocal(sd[:, i % 4, 1:2], sd[:, i % 4, 0:1]).then_inc(s["f_rs"], 1)
                dve.wait_ge(s["f_rs"], i + 1)
                nc.vector.tensor_scalar(y[:, i, :], y[:, i, :], mv[:, i % 4, 0:1], sd[:, i % 4, 1:2],
                                        ALU.subtract, ALU.mult).then_inc(s["f_n"], 1)


def kernel(**inputs):
    import numpy as _np
    import concourse.bacc as _bacc
    from concourse import mybir as _mybir
    from concourse.bass_utils import run_bass_kernel_spmd as _run

    a = {k: _np.asarray(v) for k, v in inputs.items()}

    def column(v, n):
        return v.reshape(n, -1).T

    def turned(m):
        return m.reshape(-1, m.shape[-1]).T

    laid = {
        "x": a["x"].reshape(T, D), "xT": turned(a["x"]), "ctxT": turned(a["ctx_1024"]),
        "mask": a["mask_Bx1xSxS2_ik1"].reshape(T, SK),
        "wqT": a["L0_attn_wq"].T, "bq": column(a["L0_attn_bq"], KC), "wkT": a["L0_attn_wk"].T, "bk": column(a["L0_attn_bk"], 1),
        "wvT": a["L0_attn_wv"].T, "bv": a["L0_attn_bv"].reshape(1, -1), "woT": a["L0_attn_wo"].T, "bo": a["L0_attn_bo"].reshape(1, -1),
        "xwqT": a["L0_xattn_Wq"].T, "xbq": column(a["L0_xattn_bq"], KC), "xwkT": a["L0_xattn_Wk"].T, "xbk": column(a["L0_xattn_bk"], KC),
        "xwvT": a["L0_xattn_Wv"].T, "xbv": a["L0_xattn_bv"].reshape(1, -1), "xwoT": a["L0_xattn_Wo"].T, "xbo": a["L0_xattn_bo"].reshape(1, -1),
        "rw": a["L0_ffn_router_w"], "rb": a["L0_ffn_router_b"].reshape(1, -1),
        "ew": a["L0_ffn_expert_w"].reshape(E * D, D), "eb": a["L0_ffn_expert_b"],
    }
    nc = _bacc.Bacc("TRN2", target_bir_lowering=False, num_devices=1)
    arrays, args = {}, []
    for name, v in laid.items():
        v = _np.ascontiguousarray(v)
        arrays[f"{name}_dram"] = v
        args.append(nc.dram_tensor(f"{name}_dram", v.shape, _mybir.dt.from_np(v.dtype), kind="ExternalInput").ap())
    args.append(nc.dram_tensor("out_dram", (T, D), F32, kind="ExternalOutput").ap())
    decoder_layer(nc, *args)
    r = _run(nc, [arrays], core_ids=[0])
    return r.results[0]["out_dram"].reshape(B, S, D)
```

```python
from contextlib import ExitStack

import concourse.bass as bass
from concourse import mybir

F32 = mybir.dt.float32
F32R = mybir.dt.float32r
BF16 = mybir.dt.bfloat16
I32 = mybir.dt.int32
U32 = mybir.dt.uint32
ALU = mybir.AluOpType
ACT = mybir.ActivationFunctionType
AX = mybir.AxisListType
RMAX = bass.bass_isa.ReduceOp.max
ds = bass.ds

P = 128
B, S, D = 2, 1024, 512
SK = 2048
T = B * S
H, HKV, DH = 16, 4, 32
KC = D // P
GK = 256
NG = SK // GK
E = 8
XT = T // P + E - 1
R = 3 * DH
EPS = 1e-5
SCALE = float(DH) ** -0.5
MASKED = -float(2 ** 100)
QT = S // P
NT = T // P
NB = 4
STK = 3 * 16

BANK_S = 0
BANK_O = 4
BANK_A = 5
BANK_T = 7


def decoder_layer(nc, x, xT, ctxT, mask, wqT, bq, wkT, bk, wvT, bv, woT, bo,
                  xwqT, xbq, xwkT, xbk, xwvT, xbv, xwoT, xbo, rw, rb, ew, eb, out):
    with ExitStack() as ctx:
        def sb(name, shape, dt=F32):
            return ctx.enter_context(nc.sbuf_tensor(name, shape, dt))

        def sem(name):
            return ctx.enter_context(nc.semaphore(name))

        def dram(name, shape, dt=F32):
            return nc.dram_tensor(name, shape, dt, kind="Internal").ap()

        ps = ctx.enter_context(nc.psum_tensor("ps", [P, 8, 512], F32))

        q_sc, xq_sc = dram("q_sc", (B * H * R, S)), dram("xq_sc", (B * H * R, S))
        k_sc = dram("k_sc", (B * HKV * R, S))
        v_sc = dram("v_sc", (B * HKV * P, QT * DH))
        xk_sc = dram("xk_sc", (B * NG * H * R, GK))
        xv_sc = dram("xv_sc", (B * NG * H * P, 2 * DH))
        mask_sc = dram("mask_sc", (T, SK), BF16)
        att_sc = [dram(f"att_sc{a}", (B * H * P, 512)) for a in range(2)]
        rec_sc = [dram(f"rec_sc{a}", (B * H * 2, 512)) for a in range(2)]
        xs_sc, ys_sc = dram("xs_sc", (XT * P, D)), dram("ys_sc", (XT * P, D))
        x_sc = [dram(f"x_sc{a}", (T, D)) for a in range(2)]

        xw = sb("xw", [P, 5 * KC * D + KC * T])
        W = [xw[:, n * KC * D:(n + 1) * KC * D].rearrange("p (k n) -> p k n", k=KC) for n in range(5)]
        xt = xw[:, 5 * KC * D:].rearrange("p (k t) -> p k t", k=KC)
        bq_s, bk_s = sb("bq_s", [P, KC]), sb("bk_s", [P, 1])
        bv_s = sb("bv_s", [P, P])
        xbq_s, xbk_s = sb("xbq_s", [P, KC]), sb("xbk_s", [P, KC])
        xbv_s = sb("xbv_s", [P, D])
        bo_s = [sb(f"bo_s{a}", [P, D]) for a in range(2)]
        rw_s, rb_s, eb_s = sb("rw_s", [P, KC, E]), sb("rb_s", [P, E]), sb("eb_s", [E, D])
        ident = sb("ident", [P, P])
        neg_ident = sb("neg_ident", [P, P], BF16)
        iota8 = sb("iota8", [P, E])
        qst = sb("qst", [97, NB, S], F32R)
        kst = sb("kst", [97, NB, S], F32R)
        vst = sb("vst", [P, NB, QT, 2 * DH])
        kx = sb("kx", [97, GK], F32R)
        vx = sb("vx", [P, 2, 2 * DH])
        mx = sb("mx", [P, QT, GK], BF16)
        mask0 = sb("mask0", [P, QT, GK], BF16)
        probs = sb("probs", [P, 2, S])
        hi = sb("hi", [P, 2, 512], F32R)
        lo = sb("lo", [P, 2, 512], F32R)
        m_part = sb("m_part", [P, QT, 2])
        m_rest = sb("m_rest", [P, QT])
        m_slot = sb("m_slot", [P, QT])
        m_fin = sb("m_fin", [P, 2, QT])
        m_row = sb("m_row", [QT, P], F32R)
        o_stage = sb("o_stage", [P, 2, 512])
        big = sb("big", [P, 10240])
        mask_i = big[:, 0:4096].bitcast(I32).rearrange("p (n k) -> p n k", n=2)
        mask_b = big[:, 4096:6144].bitcast(BF16).rearrange("p (n k) -> p n k", n=2)
        v_stage = big[:, 6144:7168].rearrange("p (n c) -> p n c", n=2)
        cx = big[:, 0:1024].rearrange("p (k t) -> p k t", k=KC)
        cv_stage = big[:, 1024:2048].rearrange("p (c n) -> p c n", c=2)
        onum = [big[:, n * 1024:(n + 1) * 1024].rearrange("p (c t) -> p c t", c=KC) for n in range(2)]
        orec = [big[:, 2048 + n * 1024:3072 + n * 1024].rearrange("p (c t) -> p c t", c=KC) for n in range(2)]
        xres = [big[:, 4096 + n * 1024:5120 + n * 1024].rearrange("p (i n) -> p i n", i=2) for n in range(2)]
        xnew = [big[:, 6144 + n * 1024:7168 + n * 1024].rearrange("p (i n) -> p i n", i=2) for n in range(2)]
        den_s = big[:, 8192:8448]
        y = big[:, 0:8192].rearrange("p (i n) -> p i n", i=NT)
        wselT = vst[0:E, :, :, :].rearrange("p b c d -> p (b c d)").rearrange("p (i t) -> p i t", i=NT)
        xs = probs[:, :, :].rearrange("p a b -> p (a b)").rearrange("p (n t) -> p n t", n=4)
        xsT = big[:, 8192:9216].rearrange("p (n k t) -> p n k t", n=2, k=KC)
        hi4 = hi[:, :, :].rearrange("p a b -> p (a b)").rearrange("p (m t) -> p m t", m=4)
        lo4 = lo[:, :, :].rearrange("p a b -> p (a b)").rearrange("p (m t) -> p m t", m=4)
        grp = sb("grp", [P, B, QT, NG + 1])
        grp_m = sb("grp_m", [P, B, NG + 1])
        grp_r = sb("grp_r", [P, B, NG + 1])
        fl = sb("fl", [1, 8, NG])
        tbl = sb("tbl", [1, 4], I32)
        st = sb("st", [P, 4, 6])
        mv = sb("mv", [P, 4, 2])
        sd = sb("sd", [P, 4, 2])
        lg = sb("lg", [P, NT, E])
        ex = sb("ex", [P, NT, E])
        mx8 = sb("mx8", [P, NT, 8])
        ix8 = sb("ix8", [P, NT, 8], U32)
        top = sb("top", [P, NT])
        gate = sb("gate", [P, NT])
        ixf = sb("ixf", [P, NT])
        chosen = sb("chosen", [P, NT, E])
        wsel = sb("wsel", [P, NT, E])
        before = sb("before", [P, NT + 1, E])
        many = sb("many", [P, E, NT])
        tiles = sb("tiles", [P, E])
        first = sb("first", [P, E + 1])
        slotf = sb("slotf", [P, NT])
        slot_u = sb("slot_u", [P, NT], U32)
        tile_e = sb("tile_e", [1, XT, E])
        tile_f = sb("tile_f", [1, XT])
        tile_i = sb("tile_i", [1, XT], I32)
        steps = sb("steps", [P, NT])
        iotaT = sb("iotaT", [1, XT])
        earlier = sb("earlier", [P, P])
        ones = sb("ones", [P, P])
        zeros = sb("zeros", [P, D])
        eps_s = sb("eps_s", [P, 1])

        names = """consts w_self xt0 xt1 xt2 xt3 bias w_out w_xq w_xk w_xv w_xo
            pj_mm pj_hi pj_done pj_st0 pj_st1 pv_st0 pv_st1
            mask_in0 mask_in1 mask_eq mask_red mask_st0 mask_st1 grp_ok grp_all flag tbl_ok
            s_stk0 s_stk1 s_stk2 s_stk3 s_unit s_score s_exp s_pv s_acc s_amm s_amax s_afin s_at s_arow s_mrow s_out s_free
            c_stk0 c_stk1 c_stk2 c_stk3 c_unit c_score c_exp c_pv c_acc c_amm c_amax c_afin c_at c_arow c_mrow c_out c_free c_mask
            r_den r_rec r_out o_num0 o_num1 o_ready o_x0 o_x1 o_xb o_mm o_add o_st o_var o_sd o_rs o_y o_yst0 o_yst1 o_tr o_xt
            passed f_w f_lg f_l f_ex f_sel f_cum f_te f_wt f_wtc f_bmm f_y f_zero f_sc f_xs0 f_xs1 f_xs2 f_xs3 f_tr f_xc f_mm f_oc
            f_ga0 f_ga1 f_ga2 f_ga3 f_os0 f_os1 f_acc f_st f_var f_sd f_rs f_n f_out f_x""".split()
        s = {n: sem(n) for n in names}
        kv = [{n: sem(f"{n}_kv{i}") for n in "ctx mm hi done st".split()} for i in range(3)]
        rest = [{n: sem(f"{n}_rest{b}") for n in "load free amm amax top score exp pv".split()} for b in range(B)]
        block = ctx.enter_context(nc.Block())

        JOBS = [(t, kind) for t in range(T // 512) for kind in ("k", "v", 0, 1, 2, 3)]
        HEADJOBS = [j for j, (_, kind) in enumerate(JOBS) if kind != "v"]

        @block.sync
        def _(sp):
            sp.dma_start(W[1][:, :, 0:P], wkT.rearrange("(k p) n -> p k n", p=P)).then_inc(s["w_self"], 16)
            sp.dma_start(xt[:, :, 0:512], xT[:, 0:512].rearrange("(k p) t -> p k t", p=P)).then_inc(s["xt0"], 16)
            sp.dma_start(W[1][:, :, P:2 * P], wvT.rearrange("(k p) n -> p k n", p=P)).then_inc(s["w_self"], 16)
            sp.dma_start(W[0][:, :, :], wqT.rearrange("(k p) n -> p k n", p=P)).then_inc(s["w_self"], 16)
            for dst, src in ((bq_s, bq), (bk_s, bk), (xbq_s, xbq), (xbk_s, xbk), (eb_s, eb)):
                sp.dma_start(dst[:, :], src).then_inc(s["bias"], 16)
            for dst, src in ((bv_s, bv), (xbv_s, xbv), (bo_s[0], bo), (bo_s[1], xbo), (rb_s, rb)):
                sp.dma_start(dst[:, :], src.broadcast_to([P, src.shape[1]])).then_inc(s["bias"], 16)
            sp.dma_start(rw_s[:, :, :], rw.rearrange("(k p) e -> p k e", p=P)).then_inc(s["bias"], 16)
            for t in range(1, 4):
                sp.dma_start(xt[:, :, t * 512:(t + 1) * 512],
                             xT[:, t * 512:(t + 1) * 512].rearrange("(k p) t -> p k t", p=P)).then_inc(s[f"xt{t}"], 16)
            sp.dma_start(W[2][:, :, :], woT.rearrange("(k p) n -> p k n", p=P)).then_inc(s["w_out"], 16)
            sp.dma_start(W[3][:, :, :], xwqT.rearrange("(k p) n -> p k n", p=P)).then_inc(s["w_xq"], 16)
            sp.dma_start(W[4][:, :, :], xwoT.rearrange("(k p) n -> p k n", p=P)).then_inc(s["w_xo"], 16)
            def store_parts(dst, head, cols, high, low, keys, done):
                rows = dst[ds(head * R, 4 * R), cols].rearrange("(h c d) t -> c h d t", c=3, d=DH)
                for c, src in enumerate((high, low, high) if keys else (high, high, low)):
                    sp.dma_start(rows[c], src.bitcast(F32)).then_inc(done, 16)

            hj = vj = 0
            for j, (t, kind) in enumerate(JOBS):
                b, c0 = t // 2, (t % 2) * 512
                sp.wait_ge(s["pj_done"], j + 1)
                if kind == "v":
                    for i in range(4):
                        sp.dma_start(v_sc[b * HKV * P:(b + 1) * HKV * P, ((t % 2) * 4 + i) * DH:((t % 2) * 4 + i + 1) * DH]
                                     .rearrange("(h p) d -> p h d", p=P),
                                     v_stage[:, vj % 2, i * P:(i + 1) * P].rearrange("p (h d) -> p h d", h=HKV))\
                          .then_inc(s[f"pv_st{vj % 2}"], 16)
                    vj += 1
                else:
                    part, row = (k_sc, b * HKV) if kind == "k" else (q_sc, b * H + kind * 4)
                    store_parts(part, row, slice(c0, c0 + 512), hi[:, hj % 2, :], lo[:, hj % 2, :], kind == "k", s[f"pj_st{hj % 2}"])
                    hj += 1
            for n in range(2):
                sp.wait_ge(s[f"pj_st{n}"], 48 * hj // 2)
                sp.wait_ge(s[f"pv_st{n}"], 64 * vj // 2)

            def load_head(pre, buf, qrow, krow, vrow, q, k, v, nk):
                sp.dma_start(qst[0:R, buf, :].bitcast(F32), q[ds(qrow, R), :]).then_inc(s[f"{pre}_stk{buf}"], 16)
                sp.dma_start(kst[0:R, buf, 0:nk].bitcast(F32), k[ds(krow, R), :]).then_inc(s[f"{pre}_stk{buf}"], 16)
                sp.dma_start(vst[:, buf, 0:nk // P, 0:DH], v[ds(vrow, P), 0:(nk // P) * DH]
                             .rearrange("p (c d) -> p c d", d=DH)).then_inc(s[f"{pre}_stk{buf}"], 16)

            def row_of_maxima(pre, buf, n):
                sp.wait_ge(s[f"{pre}_arow"], n + 2)
                sp.dma_start(qst[96:97, buf, :].rearrange("o (t c) -> o t c", t=QT).bitcast(F32),
                             m_row[:, :].bitcast(F32)).then_inc(s[f"{pre}_mrow"], 16)

            def self_load(u4, g):
                load_head("s", g, u4 * (4 * R) + g * R, u4 * R, u4 * P, q_sc, k_sc, v_sc, S)

            for g in range(3):
                self_load(0, g)
            row_of_maxima("s", 0, 0)

            def self_units(j, last=False):
                for g in range(4):
                    if not (last and g > 0):
                        sp.wait_ge(s["s_unit"], 4 * j + g + 1)
                        sp.sem_inc(s["passed"], 1)
                        self_load(j + (g + 3) // 4, (g + 3) % 4)
                    if not (last and g == 3):
                        row_of_maxima("s", (g + 1) % 4, 4 * j + g + 1)

            with sp.Fori(0, 7) as j:
                self_units(j)
            self_units(7, last=True)

            sp.wait_ge(s["pj_mm"], len(JOBS))
            sp.dma_start(W[0][:, :, :], xwkT.rearrange("(k p) n -> p k n", p=P)).then_inc(s["w_xk"], 16)
            sp.dma_start(W[1][:, :, :], xwvT.rearrange("(k p) n -> p k n", p=P)).then_inc(s["w_xv"], 16)

            def out_stage(a):
                att = att_sc[a].rearrange("(b c h f r) t -> b h f r c t", b=B, c=KC, h=4, f=2)
                rec = rec_sc[a].rearrange("(b c h f) t -> b h f c t", b=B, c=KC, h=4)
                sp.wait_ge(s[f"{'sc'[a]}_out"], 16 * B * H)
                sp.dma_start(den_s,
                             att_sc[a].rearrange("(n r) (c t) -> r n c t", r=2 * DH, c=2)[DH]).then_inc(s["r_den"], 16)
                sp.wait_ge(s["r_rec"], a + 1)
                sp.dma_start(rec_sc[a].rearrange("n (c t) -> (n c) t", c=2), den_s).then_inc(s["r_out"], 16)
                sp.wait_ge(s["r_out"], 16 * a + 16)
                res = x if a == 0 else x_sc[0]

                def store(t):
                    sp.wait_ge(s["o_y"], NT * a + 2 * t + 2)
                    sp.dma_start(x_sc[a][t * 256:(t + 1) * 256, :].rearrange("(i p) n -> p i n", p=P), xnew[t % 2])\
                      .then_inc(s[f"o_yst{t % 2}"], 16)

                for t in range(8):
                    b, f, cols = t // 4, t // 2 % 2, slice(t % 2 * 256, t % 2 * 256 + 256)
                    if t >= 2:
                        sp.wait_ge(s["o_mm"], NT * a + 2 * t - 2)
                    for h in range(4):
                        sp.dma_start(onum[t % 2][DH * h:DH * h + DH, :, :], att[b, h, f, 0:DH, :, cols]).then_inc(s[f"o_num{t % 2}"], 16)
                        sp.dma_start(orec[t % 2][DH * h:DH * h + DH, :, :],
                                     rec[b, h, f, :, cols].rearrange("(o c) t -> o c t", o=1).broadcast_to([DH, KC, 256]))\
                          .then_inc(s[f"o_num{t % 2}"], 16)
                    if t >= 2:
                        sp.wait_ge(s["o_add"], NT * a + 2 * t - 2)
                    sp.dma_start(xres[t % 2], res[t * 256:(t + 1) * 256, :].rearrange("(i p) n -> p i n", p=P))\
                      .then_inc(s[f"o_x{t % 2}"], 16)
                    if t >= 3:
                        store(t - 3)
                for t in range(5, 8):
                    store(t)
                for n in range(2):
                    sp.wait_ge(s[f"o_yst{n}"], 64 * a + 64)

            for n in range(2):
                sp.wait_ge(s[f"mask_st{n}"], 16 * NT // 2)
            out_stage(0)

            for j in range(16):
                t, m = j // 4, j % 4
                sp.wait_ge(s["pj_done"], len(JOBS) + j + 1)
                store_parts(xq_sc, (t // 2) * H + m * 4, slice((t % 2) * 512, (t % 2) * 512 + 512), hi[:, j % 2, :], lo[:, j % 2, :],
                            False, s[f"pj_st{j % 2}"])
            for n in range(2):
                sp.wait_ge(s[f"pj_st{n}"], 48 * 18)

            sp.wait_ge(s["tbl_ok"], 1)
            dense = [sp.value_load(tbl[0:1, b:b + 1], min_val=0, max_val=1) for b in range(B)]
            group = [sp.value_load(tbl[0:1, 2 + b:3 + b], min_val=0, max_val=NG - 1) for b in range(B)]

            def context_slot(k, n, b, slot, g):
                sp.wait_ge(k["done"], 6 * n + 1)
                sp.sem_inc(s["passed"], 1)
                sp.dma_start(cx, ctxT[:, ds(g * GK + b * SK, GK)].rearrange("(k p) t -> p k t", p=P)).then_inc(k["ctx"], 16)
                sp.wait_ge(k["done"], 6 * n + 7)
                sp.sem_inc(s["passed"], 1)
                for m in range(4):
                    store_parts(xk_sc, slot * H + (b * NG * H + 4 * m), slice(0, GK), hi4[:, m, :], lo4[:, m, :], True, k["st"])
                for c in range(2):
                    sp.dma_start(xv_sc[ds(slot * H * P + b * NG * H * P, H * P), c * DH:(c + 1) * DH].rearrange("(h p) d -> p h d", p=P),
                                 cv_stage[:, c, :].rearrange("p (h d) -> p h d", d=DH)).then_inc(k["st"], 16)
                sp.wait_ge(k["st"], 224 * n + 448)
                sp.sem_inc(s["passed"], 1)

            for b in range(B):
                context_slot(kv[2], b, b, 0, group[b])
            for b in range(B):
                with sp.If(dense[b]):
                    with sp.Fori(1, NG) as g:
                        context_slot(kv[b], g - 1, b, g, g)

            def cross_load(b, row4, g):
                load_head("c", g, b * H * R + row4 * (4 * R) + g * R, b * NG * H * R + row4 * (4 * R) + g * R,
                          b * NG * H * P + row4 * 4 * P + g * P, xq_sc, xk_sc, xv_sc, GK)

            def rest_loads(b, n, h):
                r = rest[b]
                with sp.If(dense[b]):
                    with sp.Fori(1, NG) as slot:
                        sp.wait_ge(r["free"], n + slot)
                        sp.sem_inc(s["passed"], 1)
                        sp.dma_start(kx[0:R, :].bitcast(F32), xk_sc[ds(slot * H * R + (b * NG * H * R + h * R), R), :]).then_inc(r["load"], 16)
                        sp.dma_start(vx[:, :, 0:DH], xv_sc[ds(slot * H * P + (b * NG * H * P + h * P), P), :]
                                     .rearrange("p (c d) -> p c d", d=DH)).then_inc(r["load"], 16)
                        sp.dma_start(mx[:, :, :], mask_sc[b * S:(b + 1) * S, ds(slot * GK, GK)]
                                     .rearrange("(i p) k -> p i k", p=P)).then_inc(r["load"], 16)

            for b in range(B):
                if b == 0:
                    for g in range(3):
                        cross_load(0, 0, g)
                else:
                    sp.wait_ge(s["c_unit"], 16 * b + 1)
                sp.dma_start(mask0[:, :, :], mask_sc[b * S:(b + 1) * S, ds(group[b] * GK, GK)]
                             .rearrange("(i p) k -> p i k", p=P)).then_inc(s["c_mask"], 16)
                rest_loads(b, 0, 0)
                rest_loads(b, 7, 1)
                row_of_maxima("c", 0, 16 * b)

                def cross_units(j, last=False):
                    for g in range(4):
                        n = 14 + 14 * (4 * j + g)
                        if last and g == 3:
                            n = n - 7
                        if not (last and g > 0 and b == B - 1):
                            sp.wait_ge(s["c_unit"], 16 * b + 4 * j + g + 1)
                            sp.sem_inc(s["passed"], 1)
                            if last and g > 0:
                                cross_load(b + 1, 0, g - 1)
                            else:
                                cross_load(b, j + (g + 3) // 4, (g + 3) % 4)
                        if not (last and g >= 2):
                            rest_loads(b, n, 4 * j + g + 2)
                        if not (last and g == 3):
                            row_of_maxima("c", (g + 1) % 4, 16 * b + 4 * j + g + 1)
                        rest_loads(b, n if last and g >= 2 else n + 7, 4 * j + g)

                with sp.Fori(0, 3) as j:
                    cross_units(j)
                cross_units(3, last=True)

            def load_expert(e):
                sp.dma_start(xw[:, e * KC * D:(e + 1) * KC * D].rearrange("p (k n) -> p k n", k=KC),
                             ew[e * D:(e + 1) * D, :].rearrange("(k p) n -> p k n", p=P)).then_inc(s["f_w"], 16)

            for e in range(4):
                load_expert(e)
            out_stage(1)
            sp.wait_ge(s["o_tr"], 2 * NT)
            sp.dma_start(y, x_sc[1].rearrange("(i p) n -> p i n", p=P)).then_inc(s["f_x"], 16)
            load_expert(4)
            sp.wait_ge(s["f_lg"], 1)
            for e in range(5, E):
                load_expert(e)
            for n in range(XT):
                if n == 0:
                    sp.wait_ge(s["f_sc"], 16 * NT)
                if n >= 4:
                    sp.wait_ge(s["f_tr"], n - 3)
                sp.dma_start(xs[:, n % 4, :], xs_sc[n * P:(n + 1) * P, :]).then_inc(s[f"f_xs{n % 4}"], 16)
            for i in range(NT):
                sp.wait_ge(s["f_n"], i + 1)
                sp.dma_start(out[i * P:(i + 1) * P, :], y[:, i, :]).then_inc(s["f_out"], 16)
            sp.wait_ge(s["f_out"], 16 * NT)

        @block.gpsimd
        def _(pool):
            nc.gpsimd.memset(ident[:, :], 0.0).then_inc(s["consts"], 1)
            nc.gpsimd.memset(neg_ident[:, :], 0.0).then_inc(s["consts"], 1)
            nc.gpsimd.memset(vst[:, :, :, :], 1.0).then_inc(s["consts"], 1)
            nc.gpsimd.memset(vx[:, :, :], 1.0).then_inc(s["consts"], 1)
            pool.wait_ge(s["consts"], 4)
            nc.gpsimd.memset(kst[96:97, :, :].bitcast(F32), -1.0).then_inc(s["consts"], 1)
            pool.wait_ge(s["consts"], 5)
            nc.gpsimd.memset(kx[96:97, :].bitcast(F32), -1.0).then_inc(s["consts"], 1)
            pool.wait_ge(s["consts"], 6)
            nc.gpsimd.memset(eps_s[:, :], EPS).then_inc(s["consts"], 1)
            pool.wait_ge(s["consts"], 7)
            nc.gpsimd.affine_select(out=ident[:, :], in_=ident[:, :], compare_op=ALU.not_equal, fill=1.0, base=0,
                                    pattern=[[-1, P]], channel_multiplier=1).then_inc(s["consts"], 1)
            nc.gpsimd.affine_select(out=neg_ident[:, :], in_=neg_ident[:, :], compare_op=ALU.not_equal, fill=MASKED, base=0,
                                    pattern=[[-1, P]], channel_multiplier=1).then_inc(s["consts"], 1)
            nc.gpsimd.iota(iota8[:, :], pattern=[[1, E]], base=0, channel_multiplier=0,
                           allow_small_or_imprecise_dtypes=True).then_inc(s["consts"], 1)
            nc.gpsimd.iota(steps[:, :], pattern=[[P, NT]], base=0, channel_multiplier=0,
                           allow_small_or_imprecise_dtypes=True).then_inc(s["consts"], 1)
            nc.gpsimd.iota(iotaT[:, :], pattern=[[1, XT]], base=0, channel_multiplier=0,
                           allow_small_or_imprecise_dtypes=True).then_inc(s["consts"], 1)
            nc.gpsimd.memset(ones[:, :], 1.0).then_inc(s["consts"], 1)
            nc.gpsimd.memset(zeros[:, :], 0.0).then_inc(s["consts"], 1)
            pool.wait_ge(s["consts"], 14)
            nc.gpsimd.affine_select(out=earlier[:, :], in_=ones[:, :], compare_op=ALU.is_gt, fill=0.0, base=0,
                                    pattern=[[1, P]], channel_multiplier=-1).then_inc(s["consts"], 1)
            pool.dma_start(xs_sc.rearrange("(n p) d -> p n d", p=P),
                           zeros[:, :].rearrange("p (o d) -> p o d", o=1).broadcast_to([P, XT, D])).then_inc(s["f_zero"], 16)
            for i in range(NT + 1):
                if i < NT:
                    if i >= 2:
                        pool.wait_ge(s["mask_eq"], i - 1)
                    pool.dma_start(mask_i[:, i % 2, :], mask[i * P:(i + 1) * P, :]).then_inc(s[f"mask_in{i % 2}"], 16)
                if i >= 1:
                    pool.wait_ge(s["mask_eq"], i)
                    pool.dma_start(mask_sc[(i - 1) * P:i * P, :], mask_b[:, (i - 1) % 2, :]).then_inc(s[f"mask_st{(i - 1) % 2}"], 16)
            for n in range(2):
                pool.wait_ge(s[f"mask_st{n}"], 16 * NT // 2)
            pool.wait_ge(s["grp_ok"], 1)
            nc.gpsimd.partition_all_reduce(grp_r[:, :, :].rearrange("p b g -> p (b g)"),
                                           grp_m[:, :, :].rearrange("p b g -> p (b g)"), P, RMAX).then_inc(s["grp_all"], 1)
            for pre in "sc":
                pool.sem_inc(s[f"{pre}_free"], 2)

            def store_unit(pre, a, u, par):
                pool.wait_ge(s[f"{pre}_acc"], u + 2)
                pool.sem_inc(s["passed"], 1)
                pool.dma_start(att_sc[a][ds(u * P, P), :], o_stage[:, par, :]).then_inc(s[f"{pre}_out"], 16)
                pool.wait_ge(s[f"{pre}_out"], u * 16 + 16)
                pool.sem_inc(s[f"{pre}_free"], 1)

            with pool.Fori(0, 16) as j:
                for par in range(2):
                    store_unit("s", 0, 2 * j + par, par)

            def residuals(a):
                for t in range(8):
                    pool.wait_ge(s[f"o_x{t % 2}"], 64 * a + 16 * (t // 2) + 16)
                    for i in range(2):
                        nc.gpsimd.tensor_tensor(xres[t % 2][:, i, :], xres[t % 2][:, i, :], bo_s[a][:, :], ALU.add).then_inc(s["o_xb"], 1)

            pool.wait_ge(s["bias"], 16 * 11)
            residuals(0)
            with pool.Fori(0, 16) as j:
                for par in range(2):
                    store_unit("c", 1, 2 * j + par, par)
            residuals(1)

            pool.wait_ge(s["f_zero"], 16)
            pool.wait_ge(s["f_x"], 16)
            pool.wait_ge(s["f_te"], 1)
            for i in range(NT):
                nc.gpsimd.indirect_dma_start(xs_sc, bass.IndirectOffsetOnAxis(ap=slot_u[:, i:i + 1], axis=0), y[:, i, :], None)\
                  .then_inc(s["f_sc"], 16)
            for n in range(XT):
                pool.wait_ge(s["f_oc"], n + 1)
                pool.dma_start(ys_sc[n * P:(n + 1) * P, :], o_stage[:, n % 2, :]).then_inc(s[f"f_os{n % 2}"], 16)
            for n in range(2):
                pool.wait_ge(s[f"f_os{n}"], 16 * ((XT + 1 - n) // 2))
            for i in range(NT):
                if i == 0:
                    pool.wait_ge(s["f_tr"], XT)
                if i >= 4:
                    pool.wait_ge(s["f_acc"], i - 3)
                nc.gpsimd.indirect_dma_start(xs[:, i % 4, :], None, ys_sc, bass.IndirectOffsetOnAxis(ap=slot_u[:, i:i + 1], axis=0))\
                  .then_inc(s[f"f_ga{i % 4}"], 16)

        @block.scalar
        def _(act):
            for pre in "sc":
                act.sem_inc(s[f"{pre}_exp"], 2)
                act.sem_inc(s[f"{pre}_acc"], 1)
                act.sem_inc(s[f"{pre}_arow"], 1)
                act.sem_inc(s[f"{pre}_mrow"], 16)
            act.wait_ge(s["bias"], 16 * 11)
            for n, j in enumerate(HEADJOBS):
                t, kind = JOBS[j]
                act.wait_ge(s["pj_mm"], j + 1)
                if n >= 2:
                    act.wait_ge(s[f"pj_st{n % 2}"], 48 * (n // 2))
                bias = bk_s[:, 0:1] if kind == "k" else bq_s[:, kind:kind + 1]
                nc.scalar.activation(hi[:, n % 2, :], ps[:, j % 8, :], ACT.Identity, bias=bias).then_inc(s["pj_hi"], 1)

            def copy_maxima(pre, n):
                act.wait_ge(s[f"{pre}_at"], n + 3)
                act.wait_ge(s[f"{pre}_mrow"], 16 * n + 16)
                nc.scalar.activation(m_row[:, :], ps[0:QT, BANK_T, 0:P], ACT.Copy).then_inc(s[f"{pre}_arow"], 1)

            def exps(pre, n, c):
                act.wait_ge(s[f"{pre}_score"], n + 1)
                act.wait_ge(s[f"{pre}_pv"], n + 1)
                nc.scalar.activation(probs[:, c % 2, :].rearrange("p (a b) -> p a b", a=2),
                                     ps[:, BANK_S + 2 * (c % 2):BANK_S + 2 * (c % 2) + 2, :],
                                     ACT.Exp, scale=SCALE).then_inc(s[f"{pre}_exp"], 1)

            def unit_result(pre, u, par):
                act.wait_ge(s[f"{pre}_unit"], u + 2)
                act.wait_ge(s[f"{pre}_free"], u + 1)
                nc.scalar.activation(o_stage[:, par, :], ps[:, BANK_O, :], ACT.Copy).then_inc(s[f"{pre}_acc"], 1)

            copy_maxima("s", 0)
            for b in range(B):
                def self_units(j, last=False):
                    for g in range(4):
                        u = 16 * b + 4 * j + g
                        for c in range(QT):
                            if c == 2 and not (last and g == 3 and b == B - 1):
                                copy_maxima("s", u + 1)
                            exps("s", 8 * u + c, c)
                        unit_result("s", u, g % 2)

                with act.Fori(0, 3) as j:
                    self_units(j)
                self_units(3, last=True)

            def norm_stage(a):
                def turned(t):
                    for n in range(NT * a + 2 * t, NT * a + 2 * t + 2):
                        act.wait_ge(s["o_tr"], n + 1)
                        nc.scalar.activation(xt[:, :, n % NT * P:(n % NT + 1) * P],
                                             ps[:, 4 + n % 4, :].rearrange("p (k t) -> p k t", k=KC), ACT.Copy).then_inc(s["o_xt"], 1)

                for t in range(8):
                    act.wait_ge(s["o_var"], 16 * a + 2 * t + 2)
                    nc.scalar.activation(sd[:, t % 2 * 2:t % 2 * 2 + 2, 0], mv[:, t % 2 * 2:t % 2 * 2 + 2, 1], ACT.Sqrt,
                                         bias=eps_s[:, 0:1]).then_inc(s["o_sd"], 1)
                    if t:
                        turned(t - 1)
                turned(7)

            norm_stage(0)

            for j in range(16):
                act.wait_ge(s["pj_mm"], len(JOBS) + j + 1)
                if j >= 2:
                    act.wait_ge(s[f"pj_st{j % 2}"], 48 * (10 + j // 2))
                nc.scalar.activation(hi[:, j % 2, :], ps[:, j % 8, :], ACT.Identity, bias=xbq_s[:, j % 4:j % 4 + 1]).then_inc(s["pj_hi"], 1)

            act.wait_ge(s["tbl_ok"], 1)
            dense = [act.value_load(tbl[0:1, b:b + 1], min_val=0, max_val=1) for b in range(B)]
            for n in range(2):
                act.wait_ge(s[f"pj_st{n}"], 48 * 18)

            def context_slot(k, n):
                for m in range(4):
                    act.wait_ge(k["mm"], 6 * n + m + 1)
                    act.wait_ge(k["st"], 224 * n + 224)
                    nc.scalar.activation(hi4[:, m, :], ps[:, m, 0:GK], ACT.Identity, bias=xbk_s[:, m:m + 1]).then_inc(k["hi"], 1)

            for b in range(B):
                context_slot(kv[2], b)
            for b in range(B):
                with act.If(dense[b]):
                    with act.Fori(0, NG - 1) as n:
                        context_slot(kv[b], n)

            for b in range(B):
                copy_maxima("c", 16 * b)

                def cross_units(j, last=False):
                    for g in range(4):
                        u = 4 * j + g
                        n = 16 * b + u
                        exps("c", 2 * n, 0)
                        exps("c", 2 * n + 1, 1)
                        if not (last and g == 3):
                            copy_maxima("c", n + 1)
                        r = rest[b]
                        with act.If(dense[b]):
                            act.wait_ge(s["c_pv"], 2 * n + 3)
                            with act.Fori(0, NG - 1) as sl:
                                for c in range(2):
                                    act.wait_ge(r["score"], 14 * u + sl * 2 + c + 1)
                                    act.wait_ge(r["pv"], 14 * u + sl * 2 + c + 1)
                                    nc.scalar.activation(probs[:, 0, :].rearrange("p (a b) -> p a b", a=2),
                                                         ps[:, BANK_S:BANK_S + 2, :], ACT.Exp, scale=SCALE).then_inc(r["exp"], 1)
                            act.wait_ge(r["pv"], 14 * u + 15)
                            act.sem_inc(s["passed"], 1)
                        unit_result("c", n, g % 2)

                with act.Fori(0, 3) as j:
                    cross_units(j)
                cross_units(3, last=True)
            norm_stage(1)

            act.wait_ge(s["f_l"], 3)
            nc.scalar.activation(ex[:, :, :], lg[:, :, :], ACT.Exp).then_inc(s["f_ex"], 1)
            for i in range(NT):
                act.wait_ge(s["f_wt"], i + 1)
                nc.scalar.activation(wselT[:, i, :], ps[0:E, i % 2, 0:P], ACT.Copy).then_inc(s["f_wtc"], 1)
            for n in range(XT):
                act.wait_ge(s["f_tr"], n + 1)
                if n >= 2:
                    act.wait_ge(s["f_mm"], n - 1)
                nc.scalar.activation(xsT[:, n % 2, :, :], ps[:, 4 + n % 2, :].rearrange("p (k t) -> p k t", k=KC), ACT.Copy)\
                  .then_inc(s["f_xc"], 1)
            for q in range(4):
                act.wait_ge(s["f_var"], 4 * q + 4)
                nc.scalar.activation(sd[:, :, 0], mv[:, :, 1], ACT.Sqrt, bias=eps_s[:, 0:1]).then_inc(s["f_sd"], 1)

        @block.tensor
        def _(pe):
            for pre in "sc":
                pe.sem_inc(s[f"{pre}_unit"], 1)
                pe.sem_inc(s[f"{pre}_pv"], 2)
                pe.sem_inc(s[f"{pre}_at"], 2)
            for r in rest:
                pe.sem_inc(r["free"], 1)
                pe.sem_inc(r["pv"], 1)
            mm = nc.tensor.matmul
            for j, (t, kind) in enumerate(JOBS):
                if j >= 8:
                    pe.wait_ge(s["pj_done"], j - 7)
                if j == 0:
                    pe.wait_ge(s["w_self"], 48)
                if kind == "k":
                    pe.wait_ge(s[f"xt{t}"], 16)
                if kind == "v":
                    for i in range(4):
                        for k in range(KC):
                            last = mm(ps[:, j % 8, i * P:(i + 1) * P], xt[:, k, t * 512 + i * P:t * 512 + (i + 1) * P],
                                      W[1][:, k, P:2 * P], start=(k == 0), stop=(k == KC - 1))
                else:
                    for k in range(KC):
                        w = W[1][:, k, 0:P] if kind == "k" else W[0][:, k, kind * P:(kind + 1) * P]
                        last = mm(ps[:, j % 8, :], w, xt[:, k, t * 512:(t + 1) * 512], start=(k == 0), stop=(k == KC - 1))
                last.then_inc(s["pj_mm"], 1)

            def scores(bank, st_buf, q_buf, c, masked=None):
                for half in range(2):
                    cols = slice(half * 512, half * 512 + 512)
                    last = mm(ps[:, bank + half, :], st_buf[:, c * P:(c + 1) * P], qst[:, q_buf, cols],
                              start=True, stop=True)
                    if masked is not None:
                        for i in range(4):
                            last = mm(ps[:, bank + half, i * P:(i + 1) * P], masked[:, 4 * half + i, c * P:(c + 1) * P],
                                      neg_ident[:, :], start=False, stop=True, skip_group_check=True)
                return last

            def weighted(v_buf, par, first, stop):
                for half in range(2):
                    last = mm(ps[64 * half:64 * half + 64, BANK_O, :], v_buf, probs[:, par, half * 512:half * 512 + 512],
                              start=first, stop=stop, skip_group_check=True)
                return last

            def transpose_maxima(pre, n, par):
                pe.wait_ge(s[f"{pre}_afin"], n + 2)
                pe.wait_ge(s[f"{pre}_arow"], n + 1)
                nc.tensor.transpose(ps[0:QT, BANK_T, 0:P], m_fin[:, par, :], ident[:, :]).then_inc(s[f"{pre}_at"], 1)

            def self_max(n, buf, i):
                for half in range(2):
                    pe.wait_ge(s["s_amax"], 16 * n + 2 * i + half + 1)
                    mm(ps[:, BANK_A + half, :], qst[0:96, buf, i * P:(i + 1) * P],
                       kst[0:96, buf, half * 512:half * 512 + 512], start=True, stop=True).then_inc(s["s_amm"], 1)

            pe.wait_ge(s["consts"], 15)
            pe.wait_ge(s["pj_done"], len(JOBS))
            for n in range(2):
                pe.wait_ge(s[f"s_stk{n}"], STK)
                for i in range(QT):
                    self_max(n, n, i)
            transpose_maxima("s", 0, 0)

            def self_units(j, last=False):
                for g in range(4):
                    u = 4 * j + g
                    ahead = not (last and g >= 2)
                    buf2 = (g + 2) % 4
                    pe.wait_ge(s["s_mrow"], 16 * u + 32)
                    for c in range(QT + 1):
                        if c < QT:
                            pe.wait_ge(s["s_exp"], 8 * u + c + 1)
                            scores(BANK_S + 2 * (c % 2), kst[:, g, :], g, c).then_inc(s["s_score"], 1)
                        if c == 2 and not (last and g == 3):
                            transpose_maxima("s", u + 1, (g + 1) % 2)
                        if c >= 1:
                            if c == 1:
                                pe.wait_ge(s["s_acc"], u + 1)
                            pe.wait_ge(s["s_exp"], 8 * u + c + 2)
                            weighted(vst[:, g, c - 1, :], (c - 1) % 2, c == 1, c == QT).then_inc(s["s_pv"], 1)
                        if ahead and c < QT:
                            if c == 0:
                                pe.wait_ge(s[f"s_stk{buf2}"], STK * (j + (g + 2) // 4) + STK)
                            self_max(u + 2, buf2, c)
                    pe.wait_ge(s["s_pv"], 8 * u + 10)
                    pe.sem_inc(s["s_unit"], 1)

            with pe.Fori(0, 7) as j:
                self_units(j)
            self_units(7, last=True)

            def out_stage(a, w):
                if a == 0:
                    pe.wait_ge(s["w_out"], 16)
                    pe.wait_ge(s["s_acc"], 33)
                else:
                    pe.wait_ge(s["w_xo"], 16)
                    pe.wait_ge(s["c_acc"], 33)

                def turn(t):
                    for i in range(2):
                        n = NT * a + 2 * t + i
                        pe.wait_ge(s["o_y"], n + 1)
                        if 2 * t + i >= 4:
                            pe.wait_ge(s["o_xt"], n - 3)
                        for k in range(KC):
                            last = nc.tensor.transpose(ps[:, 4 + n % 4, k * P:(k + 1) * P], xnew[t % 2][:, i, k * P:(k + 1) * P], ident[:, :])
                        last.then_inc(s["o_tr"], 1)

                for t in range(8):
                    pe.wait_ge(s["o_ready"], 8 * a + t + 1)
                    for i in range(2):
                        n = NT * a + 2 * t + i
                        if 2 * t + i >= 4:
                            pe.wait_ge(s["o_add"], n - 3)
                        for k in range(KC):
                            last = mm(ps[:, n % 4, :], onum[t % 2][:, k, i * P:(i + 1) * P], w[:, k, :], start=(k == 0), stop=(k == KC - 1))
                        last.then_inc(s["o_mm"], 1)
                    if t >= 2:
                        turn(t - 2)
                turn(6)
                turn(7)

            out_stage(0, W[2])
            pe.wait_ge(s["w_xq"], 16)
            pe.wait_ge(s["o_xt"], NT)
            for j in range(16):
                if j >= 8:
                    pe.wait_ge(s["pj_done"], len(JOBS) + j - 7)
                for k in range(KC):
                    last = mm(ps[:, j % 8, :], W[3][:, k, (j % 4) * P:(j % 4 + 1) * P], xt[:, k, (j // 4) * 512:(j // 4 + 1) * 512],
                              start=(k == 0), stop=(k == KC - 1))
                last.then_inc(s["pj_mm"], 1)

            pe.wait_ge(s["tbl_ok"], 1)
            dense = [pe.value_load(tbl[0:1, b:b + 1], min_val=0, max_val=1) for b in range(B)]
            pe.wait_ge(s["w_xk"], 16)
            pe.wait_ge(s["w_xv"], 16)
            pe.wait_ge(s["pj_done"], len(JOBS) + 16)

            def context_slot(k_, n):
                pe.wait_ge(k_["ctx"], 16 * n + 16)
                for m in range(4):
                    for k in range(KC):
                        last = mm(ps[:, m, 0:GK], W[0][:, k, m * P:(m + 1) * P], cx[:, k, :], start=(k == 0), stop=(k == KC - 1))
                    last.then_inc(k_["mm"], 1)
                for c in range(2):
                    for k in range(KC):
                        last = mm(ps[:, 4 + c, :], cx[:, k, c * P:(c + 1) * P], W[1][:, k, :], start=(k == 0), stop=(k == KC - 1))
                    last.then_inc(k_["mm"], 1)

            for b in range(B):
                context_slot(kv[2], b)
            for b in range(B):
                with pe.If(dense[b]):
                    with pe.Fori(0, NG - 1) as n:
                        context_slot(kv[b], n)
                        pe.wait_ge(kv[b]["done"], n * 6 + 7)
                        pe.sem_inc(s["passed"], 1)
            pe.wait_ge(kv[2]["done"], 13)

            def max_pair(bank, q_buf, keys, masked, f):
                for i in range(2):
                    mm(ps[:, bank, i * GK:(i + 1) * GK], qst[0:96, q_buf, (2 * f + i) * P:(2 * f + i + 1) * P], keys,
                       start=(i == 0), stop=True, skip_group_check=True)
                for i in range(2):
                    last = mm(ps[:, bank, i * GK:(i + 1) * GK], neg_ident[:, :], masked[:, 2 * f + i, :],
                              start=False, stop=True, skip_group_check=True)
                return last

            def cross_max(b, a, buf, n):
                r = rest[b]
                with pe.If(dense[b]):
                    pe.wait_ge(s["c_amax"], 64 * b + a * 4 + 2)
                    pe.sem_inc(s["passed"], 1)
                    with pe.Fori(0, NG - 1) as sl:
                        pe.wait_ge(r["load"], sl * 48 + n * 48 + 48)
                        for f in range(4):
                            pe.wait_ge(r["amax"], a * 28 + sl * 4 + f + 1)
                            last = max_pair(BANK_A, buf, kx[0:96, :], mx, f)
                            last.then_inc(r["amm"], 1)
                        pe.wait_ge(r["amm"], a * 28 + sl * 4 + 4)
                        pe.sem_inc(r["free"], 1)
                    pe.wait_ge(r["amax"], a * 28 + 29)
                    pe.sem_inc(s["passed"], 1)
                for f in range(4):
                    pe.wait_ge(s["c_amax"], 64 * b + a * 4 + f + 1)
                    max_pair(BANK_A + f % 2, buf, kst[0:96, buf, 0:GK], mask0, f).then_inc(s["c_amm"], 1)

            for b in range(B):
                pe.wait_ge(s["c_mask"], 16 * b + 16)
                for n in range(2):
                    pe.wait_ge(s[f"c_stk{n}"], STK * (4 * b + 1))
                    cross_max(b, n, n, 7 * n)
                transpose_maxima("c", 16 * b, 0)

                def cross_units(j, last=False):
                    for g in range(4):
                        u = 4 * j + g
                        n = 16 * b + u
                        before = 14 + 14 * u
                        if last and g == 3:
                            before = before - 7
                        ahead = not (last and g >= 2)
                        buf2 = (g + 2) % 4
                        pe.wait_ge(s["c_mrow"], 16 * n + 32)
                        for c in range(2):
                            pe.wait_ge(s["c_exp"], 2 * n + c + 1)
                            scores(BANK_S + 2 * c, kst[:, g, :], g, c, masked=mask0).then_inc(s["c_score"], 1)
                        if ahead:
                            pe.wait_ge(s[f"c_stk{buf2}"], STK * (4 * b + j + (g + 2) // 4) + STK)
                            cross_max(b, u + 2, buf2, before)
                        if not (last and g == 3):
                            transpose_maxima("c", n + 1, (g + 1) % 2)
                        pe.wait_ge(s["c_acc"], n + 1)
                        pe.wait_ge(s["c_exp"], 2 * n + 3)
                        weighted(vst[:, g, 0, :], 0, True, True).then_inc(s["c_pv"], 1)
                        r = rest[b]
                        taken = before + 7 if ahead else before
                        with pe.If(dense[b]):
                            with pe.Fori(0, NG - 1) as sl:
                                pe.wait_ge(r["load"], sl * 48 + taken * 48 + 48)
                                for c in range(2):
                                    scores(BANK_S, kx, g, c, masked=mx).then_inc(r["score"], 1)
                                    pe.wait_ge(r["exp"], 14 * u + sl * 2 + c + 1)
                                    weighted(vx[:, c, :], 0, False, True).then_inc(r["pv"], 1)
                                pe.wait_ge(r["pv"], 14 * u + sl * 2 + 3)
                                pe.sem_inc(r["free"], 1)
                        pe.wait_ge(s["c_exp"], 2 * n + 4)
                        weighted(vst[:, g, 1, :], 1, False, True).then_inc(s["c_pv"], 1)
                        pe.wait_ge(s["c_pv"], 2 * n + 4)
                        pe.sem_inc(s["c_unit"], 1)

                with pe.Fori(0, 3) as j:
                    cross_units(j)
                cross_units(3, last=True)
            out_stage(1, W[4])

            pe.wait_ge(s["o_xt"], 2 * NT)
            for i in range(NT):
                for k in range(KC):
                    last = mm(ps[:, 0, i * E:(i + 1) * E], xt[:, k, i * P:(i + 1) * P], rw_s[:, k, :],
                              start=(i == 0 and k == 0), stop=(k == KC - 1), skip_group_check=True)
            last.then_inc(s["f_lg"], 1)
            pe.wait_ge(s["f_sel"], 1)
            mm(ps[:, 2, 0:NT * E], earlier[:, :], chosen[:, :, :].rearrange("p i e -> p (i e)"), start=True, stop=True).then_inc(s["f_cum"], 1)
            mm(ps[:, 3, 0:NT * E], ones[:, :], chosen[:, :, :].rearrange("p i e -> p (i e)"), start=True, stop=True).then_inc(s["f_cum"], 1)
            pe.wait_ge(s["f_sel"], 2)
            for i in range(NT):
                if i >= 2:
                    pe.wait_ge(s["f_wtc"], i - 1)
                nc.tensor.transpose(ps[0:E, i % 2, 0:P], wsel[:, i, :], ident[:, :]).then_inc(s["f_wt"], 1)
            for i in range(NT):
                pe.wait_ge(s["f_wtc"], i + 1)
                if i >= 2:
                    pe.wait_ge(s["f_y"], i - 1)
                mm(ps[:, 6 + i % 2, :], wselT[:, i, :], eb_s[:, :], start=True, stop=True).then_inc(s["f_bmm"], 1)

            def turn(n):
                pe.wait_ge(s[f"f_xs{n % 4}"], 16 * (n // 4) + 16)
                if n >= 2:
                    pe.wait_ge(s["f_xc"], n - 1)
                for k in range(KC):
                    last = nc.tensor.transpose(ps[:, 4 + n % 2, k * P:(k + 1) * P], xs[:, n % 4, k * P:(k + 1) * P], ident[:, :])
                last.then_inc(s["f_tr"], 1)

            pe.wait_ge(s["f_te"], 1)
            turn(0)
            turn(1)
            pe.wait_ge(s["f_w"], 16 * E)
            for n in range(XT):
                expert = pe.value_load(tile_i[0:1, n:n + 1], min_val=0, max_val=E - 1)
                pe.wait_ge(s["f_xc"], n + 1)
                if n >= 4:
                    pe.wait_ge(s["f_oc"], n - 3)
                for k in range(KC):
                    last = mm(ps[:, n % 4, :], xsT[:, n % 2, k, :], xw[:, ds(expert * (KC * D) + k * D, D)], start=(k == 0), stop=(k == KC - 1))
                last.then_inc(s["f_mm"], 1)
                if n + 2 < XT:
                    turn(n + 2)

        @block.vector
        def _(dve):
            for pre in "sc":
                dve.sem_inc(s[f"{pre}_amax"], 2)
                dve.sem_inc(s[f"{pre}_afin"], 1)
            for k in kv:
                dve.sem_inc(k["done"], 1)
                dve.sem_inc(k["st"], 224)
            for r in rest:
                dve.sem_inc(r["amax"], 1)
            dve.wait_ge(s["bias"], 16 * 11)
            tile = [0]

            def mask_tile():
                i = tile[0]
                tile[0] += 1
                dve.wait_ge(s[f"mask_in{i % 2}"], 16 * (i // 2 + 1))
                if i >= 2:
                    dve.wait_ge(s[f"mask_st{i % 2}"], 16 * (i // 2))
                    dve.wait_ge(s["mask_red"], i - 1)
                nc.vector.tensor_scalar(mask_b[:, i % 2, :], mask_i[:, i % 2, :], 1.0, None, ALU.is_equal).then_inc(s["mask_eq"], 1)
                dve.wait_ge(s["mask_eq"], i + 1)
                nc.vector.tensor_reduce(grp[:, i // QT, i % QT, 0:NG], mask_b[:, i % 2, :].rearrange("p (g k) -> p g k", g=NG),
                                        AX.X, ALU.min).then_inc(s["mask_red"], 1)

            n = v = 0
            for j, (t, kind) in enumerate(JOBS):
                if kind == "v":
                    dve.wait_ge(s["pj_mm"], j + 1)
                    if v >= 2:
                        dve.wait_ge(s[f"pv_st{v % 2}"], 64 * (v // 2))
                    nc.vector.tensor_tensor(v_stage[:, v % 2, :].rearrange("p (i n) -> p i n", i=4),
                                            ps[:, j % 8, :].rearrange("p (i n) -> p i n", i=4),
                                            bv_s[:, :].rearrange("p (o n) -> p o n", o=1).broadcast_to([P, 4, P]),
                                            ALU.add).then_inc(s["pj_done"], 1)
                    v += 1
                else:
                    dve.wait_ge(s["pj_hi"], n + 1)
                    if n >= 2:
                        dve.wait_ge(s[f"pj_st{n % 2}"], 48 * (n // 2))
                    bias = bk_s[:, 0:1] if kind == "k" else bq_s[:, kind:kind + 1]
                    nc.vector.scalar_tensor_tensor(out=lo[:, n % 2, :], in0=ps[:, j % 8, :], scalar=bias,
                                                   in1=hi[:, n % 2, :].bitcast(F32), op0=ALU.add, op1=ALU.subtract)\
                      .then_inc(s["pj_done"], 1)
                    n += 1
                if j >= 4 and tile[0] < NT:
                    mask_tile()
            while tile[0] < NT:
                mask_tile()
            dve.wait_ge(s["mask_red"], NT)
            step = [0]

            def flag(ins):
                step[0] += 1
                ins.then_inc(s["flag"], 1)
                dve.wait_ge(s["flag"], step[0])

            flag(nc.vector.tensor_reduce(grp[:, :, :, NG], grp[:, :, :, 0:NG], AX.X, ALU.min))
            flag(nc.vector.tensor_scalar(grp[:, :, :, 0:NG], grp[:, :, :, 0:NG], -1.0, 1.0, ALU.mult, ALU.add))
            nc.vector.tensor_reduce(grp_m[:, :, :], grp[:, :, :, :].rearrange("p b i g -> p b g i"), AX.X, ALU.max)\
              .then_inc(s["grp_ok"], 1)

            def final_max(pre, n, par, src):
                dve.wait_ge(s[f"{pre}_at"], n + 1)
                if pre == "s":
                    nc.vector.tensor_reduce(m_fin[:, par, :], m_part[:, :, :], AX.X, ALU.max).then_inc(s["s_afin"], 1)
                else:
                    nc.vector.tensor_tensor(m_fin[:, par, :], m_slot[:, :], m_rest[:, :], ALU.max).then_inc(s["c_afin"], 1)

            def self_max(n, par):
                dve.wait_ge(s["s_afin"], n + 1)
                for k in range(2 * QT):
                    dve.wait_ge(s["s_amm"], 16 * n + k + 1)
                    nc.vector.reduce_max(m_part[:, k // 2, k % 2:k % 2 + 1], ps[:, BANK_A + k % 2, :], AX.X).then_inc(s["s_amax"], 1)
                dve.wait_ge(s["s_amax"], 16 * n + 18)
                final_max("s", n, par, None)

            with dve.Fori(0, 16) as j:
                self_max(2 * j, 0)
                self_max(2 * j + 1, 1)

            def out_stage(a):
                dve.wait_ge(s["r_den"], 16 * a + 16)
                nc.vector.reciprocal(den_s, den_s).then_inc(s["r_rec"], 1)

                def sums(t):
                    if t >= 2:
                        dve.wait_ge(s[f"o_yst{t % 2}"], 64 * a + 16 * (t // 2))
                        dve.wait_ge(s["o_tr"], NT * a + 2 * t - 2)
                    for i in range(2):
                        n = NT * a + 2 * t + i
                        dve.wait_ge(s["o_mm"], n + 1)
                        dve.wait_ge(s["o_xb"], n + 1)
                        nc.vector.tensor_tensor(xnew[t % 2][:, i, :], ps[:, n % 4, :], xres[t % 2][:, i, :], ALU.add).then_inc(s["o_add"], 1)
                    for i in range(2):
                        n = NT * a + 2 * t + i
                        dve.wait_ge(s["o_add"], n + 1)
                        dve.wait_ge(s["o_y"], NT * a + 2 * t - 2) if t >= 2 else None
                        nc.vector.bn_stats(st[:, n % 4, :], xnew[t % 2][:, i, :]).then_inc(s["o_st"], 1)
                    for i in range(2):
                        n = NT * a + 2 * t + i
                        dve.wait_ge(s["o_st"], n + 1)
                        nc.vector.bn_aggr(mv[:, n % 4, :], st[:, n % 4, :]).then_inc(s["o_var"], 1)

                def norm(t):
                    lanes = slice(t % 2 * 2, t % 2 * 2 + 2)
                    dve.wait_ge(s["o_sd"], 8 * a + t + 1)
                    nc.vector.reciprocal(sd[:, lanes, 1], sd[:, lanes, 0]).then_inc(s["o_rs"], 1)
                    dve.wait_ge(s["o_rs"], 8 * a + t + 1)
                    for i in range(2):
                        n = NT * a + 2 * t + i
                        nc.vector.tensor_scalar(xnew[t % 2][:, i, :], xnew[t % 2][:, i, :], mv[:, n % 4, 0:1], sd[:, n % 4, 1:2],
                                                ALU.subtract, ALU.mult).then_inc(s["o_y"], 1)

                for t in range(9):
                    if t < 8:
                        dve.wait_ge(s[f"o_num{t % 2}"], 512 * a + 128 * (t // 2) + 128)
                        nc.vector.tensor_tensor(onum[t % 2], onum[t % 2], orec[t % 2], ALU.mult).then_inc(s["o_ready"], 1)
                    if t >= 1:
                        sums(t - 1)
                        norm(t - 1)

            out_stage(0)
            for j in range(16):
                dve.wait_ge(s["pj_hi"], len(HEADJOBS) + j + 1)
                if j >= 2:
                    dve.wait_ge(s[f"pj_st{j % 2}"], 48 * (10 + j // 2))
                nc.vector.scalar_tensor_tensor(out=lo[:, j % 2, :], in0=ps[:, j % 8, :], scalar=xbq_s[:, j % 4:j % 4 + 1],
                                               in1=hi[:, j % 2, :].bitcast(F32), op0=ALU.add, op1=ALU.subtract)\
                  .then_inc(s["pj_done"], 1)

            dve.wait_ge(s["grp_all"], 1)
            for b in range(B):
                g = grp_r[0:1, b, :]
                flag(nc.vector.reduce_sum(fl[:, b, 0:1], g[:, 0:NG], AX.X))
                flag(nc.vector.tensor_scalar(fl[:, b, 1:2], g[:, NG:NG + 1], 2.0, fl[:, b, 0:1], ALU.mult, ALU.add))
                flag(nc.vector.tensor_scalar(fl[:, b, 2:3], fl[:, b, 1:2], 1.5, None, ALU.is_gt))
                flag(nc.vector.tensor_tensor(fl[:, 2 + b, :], g[:, 0:NG], iota8[0:1, :], ALU.mult))
                flag(nc.vector.reduce_max(fl[:, b, 3:4], fl[:, 2 + b, :], AX.X))
                flag(nc.vector.tensor_scalar(fl[:, b, 4:5], fl[:, b, 2:3], -1.0, 1.0, ALU.mult, ALU.add))
                flag(nc.vector.tensor_tensor(fl[:, b, 5:6], fl[:, b, 4:5], fl[:, b, 3:4], ALU.mult))
                flag(nc.vector.tensor_copy(tbl[:, b:b + 1], fl[:, b, 2:3]))
                flag(nc.vector.tensor_copy(tbl[:, 2 + b:3 + b], fl[:, b, 5:6]))
            dve.sem_inc(s["tbl_ok"], 1)
            dense = [dve.value_load(tbl[0:1, b:b + 1], min_val=0, max_val=1) for b in range(B)]

            for n in range(2):
                dve.wait_ge(s[f"pj_st{n}"], 48 * 18)

            def context_slot(k, n):
                for m in range(4):
                    dve.wait_ge(k["hi"], 4 * n + m + 1)
                    nc.vector.scalar_tensor_tensor(out=lo4[:, m, :], in0=ps[:, m, 0:GK], scalar=xbk_s[:, m:m + 1],
                                                   in1=hi4[:, m, :].bitcast(F32), op0=ALU.add, op1=ALU.subtract)\
                      .then_inc(k["done"], 1)
                for c in range(2):
                    dve.wait_ge(k["mm"], 6 * n + 5 + c)
                    nc.vector.tensor_tensor(cv_stage[:, c, :], ps[:, 4 + c, :], xbv_s[:, :], ALU.add).then_inc(k["done"], 1)

            for b in range(B):
                dve.wait_ge(kv[2]["st"], 224 * b + 224)
                context_slot(kv[2], b)
            for b in range(B):
                with dve.If(dense[b]):
                    with dve.Fori(0, NG - 1) as n:
                        dve.wait_ge(kv[b]["st"], n * 224 + 224)
                        context_slot(kv[b], n)

            def cross_max(b, a, par):
                r = rest[b]
                n = 16 * b + a
                with dve.If(dense[b]):
                    dve.wait_ge(s["c_afin"], n + 1)
                    dve.wait_ge(r["top"], 8 * a + 1)
                    nc.vector.memset(m_rest[:, :], MASKED).then_inc(r["top"], 1)
                    with dve.Fori(0, NG - 1) as sl:
                        dve.wait_ge(r["top"], a * 8 + sl + 2)
                        for f in range(4):
                            dve.wait_ge(r["amm"], a * 28 + sl * 4 + f + 1)
                            nc.vector.reduce_max(m_slot[:, 2 * f:2 * f + 2], ps[:, BANK_A, :].rearrange("p (i k) -> p i k", i=2), AX.X)\
                              .then_inc(r["amax"], 1)
                        dve.wait_ge(r["amax"], a * 28 + sl * 4 + 5)
                        nc.vector.tensor_tensor(m_rest[:, :], m_rest[:, :], m_slot[:, :], ALU.max).then_inc(r["top"], 1)
                    dve.wait_ge(r["top"], a * 8 + 9)
                    dve.sem_inc(s["passed"], 1)
                dve.wait_ge(s["c_afin"], n + 1)
                for f in range(4):
                    dve.wait_ge(s["c_amm"], 4 * n + f + 1)
                    nc.vector.reduce_max(m_slot[:, 2 * f:2 * f + 2], ps[:, BANK_A + f % 2, :].rearrange("p (i k) -> p i k", i=2), AX.X)\
                      .then_inc(s["c_amax"], 1)
                dve.wait_ge(s["c_amax"], 4 * n + 6)
                final_max("c", n, par, None)

            for b in range(B):
                dve.wait_ge(s["c_afin"], 16 * b + 1)
                nc.vector.memset(m_rest[:, :], MASKED).then_inc(rest[b]["top"], 1)
                dve.wait_ge(rest[b]["top"], 1)
                with dve.Fori(0, 8) as j:
                    cross_max(b, 2 * j, 0)
                    cross_max(b, 2 * j + 1, 1)
            out_stage(1)

            def per_expert(v):
                return v.rearrange("p (o e) -> p o e", o=1).broadcast_to([P, NT, E])

            def per_token(v):
                return v.rearrange("p (i o) -> p i o", o=1).broadcast_to([P, NT, E])

            dve.wait_ge(s["f_lg"], 1)
            nc.vector.tensor_tensor(lg[:, :, :], ps[:, 0, 0:NT * E].rearrange("p (i e) -> p i e", i=NT), per_expert(rb_s[:, :]), ALU.add)\
              .then_inc(s["f_l"], 1)
            dve.wait_ge(s["f_l"], 1)
            nc.vector.reduce_max(top[:, :], lg[:, :, :], AX.X).then_inc(s["f_l"], 1)
            dve.wait_ge(s["f_l"], 2)
            nc.vector.tensor_tensor(lg[:, :, :], lg[:, :, :], per_token(top[:, :]), ALU.subtract).then_inc(s["f_l"], 1)
            dve.wait_ge(s["f_ex"], 1)
            for i in range(NT):
                ins = nc.vector.max(mx8[:, i, :], ex[:, i, :])
            flag(ins)
            for i in range(NT):
                ins = nc.vector.max_index(ix8[:, i, :], mx8[:, i, :], ex[:, i, :])
            flag(ins)
            flag(nc.vector.tensor_copy(ixf[:, :], ix8[:, :, 0]))
            nc.vector.tensor_tensor(chosen[:, :, :], per_expert(iota8[:, :]), per_token(ixf[:, :]), ALU.is_equal).then_inc(s["f_sel"], 1)
            flag(nc.vector.reduce_sum(gate[:, :], ex[:, :, :], AX.X))
            flag(nc.vector.reciprocal(gate[:, :], gate[:, :]))
            flag(nc.vector.tensor_tensor(gate[:, :], gate[:, :], mx8[:, :, 0], ALU.mult))
            dve.wait_ge(s["f_sel"], 1)
            nc.vector.tensor_tensor(wsel[:, :, :], chosen[:, :, :], per_token(gate[:, :]), ALU.mult).then_inc(s["f_sel"], 1)
            dve.wait_ge(s["f_cum"], 2)
            totals = ps[:, 3, 0:NT * E].rearrange("p (i e) -> p i e", i=NT)
            flag(nc.vector.memset(before[:, 0, :], 0.0))
            for i in range(NT):
                flag(nc.vector.tensor_tensor(before[:, i + 1, :], totals[:, i, :], before[:, i, :], ALU.add))
            flag(nc.vector.tensor_tensor(many[:, :, :], before[:, NT, :].rearrange("p (e o) -> p e o", o=1).broadcast_to([P, E, NT]),
                                         steps[:, :].rearrange("p (o k) -> p o k", o=1).broadcast_to([P, E, NT]), ALU.is_gt))
            flag(nc.vector.reduce_sum(tiles[:, :], many[:, :, :], AX.X))
            flag(nc.vector.memset(first[:, 0:1], 0.0))
            for e in range(E):
                flag(nc.vector.tensor_tensor(first[:, e + 1:e + 2], first[:, e:e + 1], tiles[:, e:e + 1], ALU.add))
            flag(nc.vector.tensor_tensor(tile_e[:, :, :], iotaT[:, :].rearrange("p (n o) -> p n o", o=1).broadcast_to([1, XT, E]),
                                         first[0:1, 0:E].rearrange("p (o e) -> p o e", o=1).broadcast_to([1, XT, E]), ALU.is_ge))
            flag(nc.vector.reduce_sum(tile_f[:, :], tile_e[:, :, :], AX.X))
            flag(nc.vector.tensor_scalar(tile_i[:, :], tile_f[:, :], -1.0, None, ALU.add))
            flag(nc.vector.tensor_scalar(first[:, :], first[:, :], float(P), None, ALU.mult))
            flag(nc.vector.tensor_tensor(lg[:, :, :], ps[:, 2, 0:NT * E].rearrange("p (i e) -> p i e", i=NT), before[:, 0:NT, :], ALU.add))
            flag(nc.vector.tensor_tensor(lg[:, :, :], lg[:, :, :], per_expert(first[:, 0:E]), ALU.add))
            flag(nc.vector.tensor_tensor(lg[:, :, :], lg[:, :, :], chosen[:, :, :], ALU.mult))
            flag(nc.vector.reduce_sum(slotf[:, :], lg[:, :, :], AX.X))
            nc.vector.tensor_copy(slot_u[:, :], slotf[:, :]).then_inc(s["f_te"], 1)
            dve.wait_ge(s["f_sc"], 16 * NT)
            for i in range(NT):
                dve.wait_ge(s["f_bmm"], i + 1)
                nc.vector.tensor_tensor(y[:, i, :], ps[:, 6 + i % 2, :], y[:, i, :], ALU.add).then_inc(s["f_y"], 1)
            for n in range(XT):
                dve.wait_ge(s["f_mm"], n + 1)
                if n >= 2:
                    dve.wait_ge(s[f"f_os{n % 2}"], 16 * (n // 2))
                nc.vector.tensor_copy(o_stage[:, n % 2, :], ps[:, n % 4, :]).then_inc(s["f_oc"], 1)
            for q in range(4):
                for i in range(4 * q, 4 * q + 4):
                    dve.wait_ge(s[f"f_ga{i % 4}"], 16 * (i // 4) + 16)
                    if i == 0:
                        dve.wait_ge(s["f_y"], NT)
                    nc.vector.scalar_tensor_tensor(out=y[:, i, :], in0=xs[:, i % 4, :], scalar=gate[:, i:i + 1],
                                                   in1=y[:, i, :], op0=ALU.mult, op1=ALU.add).then_inc(s["f_acc"], 1)
                if q:
                    dve.wait_ge(s["f_n"], 4 * q)
                for i in range(4 * q, 4 * q + 4):
                    dve.wait_ge(s["f_acc"], i + 1)
                    nc.vector.bn_stats(st[:, i % 4, :], y[:, i, :]).then_inc(s["f_st"], 1)
                for i in range(4 * q, 4 * q + 4):
                    dve.wait_ge(s["f_st"], i + 1)
                    nc.vector.bn_aggr(mv[:, i % 4, :], st[:, i % 4, :]).then_inc(s["f_var"], 1)
                dve.wait_ge(s["f_sd"], q + 1)
                nc.vector.reciprocal(sd[:, :, 1], sd[:, :, 0]).then_inc(s["f_rs"], 1)
                dve.wait_ge(s["f_rs"], q + 1)
                for i in range(4 * q, 4 * q + 4):
                    nc.vector.tensor_scalar(y[:, i, :], y[:, i, :], mv[:, i % 4, 0:1], sd[:, i % 4, 1:2],
                                            ALU.subtract, ALU.mult).then_inc(s["f_n"], 1)


def kernel(**inputs):
    import numpy as _np
    import concourse.bacc as _bacc
    from concourse import mybir as _mybir
    from concourse.bass_utils import run_bass_kernel_spmd as _run

    a = {k: _np.asarray(v) for k, v in inputs.items()}

    def column(v, n):
        return v.reshape(n, -1).T

    def turned(m):
        return m.reshape(-1, m.shape[-1]).T

    laid = {
        "x": a["x"].reshape(T, D), "xT": turned(a["x"]), "ctxT": turned(a["ctx_1024"]),
        "mask": a["mask_Bx1xSxS2_ik1"].reshape(T, SK),
        "wqT": a["L0_attn_wq"].T, "bq": column(a["L0_attn_bq"], KC), "wkT": a["L0_attn_wk"].T, "bk": column(a["L0_attn_bk"], 1),
        "wvT": a["L0_attn_wv"].T, "bv": a["L0_attn_bv"].reshape(1, -1), "woT": a["L0_attn_wo"].T, "bo": a["L0_attn_bo"].reshape(1, -1),
        "xwqT": a["L0_xattn_Wq"].T, "xbq": column(a["L0_xattn_bq"], KC), "xwkT": a["L0_xattn_Wk"].T, "xbk": column(a["L0_xattn_bk"], KC),
        "xwvT": a["L0_xattn_Wv"].T, "xbv": a["L0_xattn_bv"].reshape(1, -1), "xwoT": a["L0_xattn_Wo"].T, "xbo": a["L0_xattn_bo"].reshape(1, -1),
        "rw": a["L0_ffn_router_w"], "rb": a["L0_ffn_router_b"].reshape(1, -1),
        "ew": a["L0_ffn_expert_w"].reshape(E * D, D), "eb": a["L0_ffn_expert_b"],
    }
    nc = _bacc.Bacc("TRN2", target_bir_lowering=False, num_devices=1)
    arrays, args = {}, []
    for name, v in laid.items():
        v = _np.ascontiguousarray(v)
        arrays[f"{name}_dram"] = v
        args.append(nc.dram_tensor(f"{name}_dram", v.shape, _mybir.dt.from_np(v.dtype), kind="ExternalInput").ap())
    args.append(nc.dram_tensor("out_dram", (T, D), F32, kind="ExternalOutput").ap())
    decoder_layer(nc, *args)
    r = _run(nc, [arrays], core_ids=[0])
    return r.results[0]["out_dram"].reshape(B, S, D)
```

```python
from contextlib import ExitStack, nullcontext

import concourse.bass as bass
from concourse import mybir

F32 = mybir.dt.float32
F32R = mybir.dt.float32r
BF16 = mybir.dt.bfloat16
I32 = mybir.dt.int32
U32 = mybir.dt.uint32
ALU = mybir.AluOpType
ACT = mybir.ActivationFunctionType
AX = mybir.AxisListType
RMAX = bass.bass_isa.ReduceOp.max
ds = bass.ds

P = 128
B, S, D = 2, 1024, 512
SK = 2048
T = B * S
H, HKV, DH = 16, 4, 32
KC = D // P
GK = 256
NG = SK // GK
E = 8
XT = T // P + E - 1
ZT = -(-XT // 8)
R = 3 * DH
ROW = D + 4
XB, YB = 6, 4
EPS = 1e-5
SCALE = float(DH) ** -0.5
MASKED = -float(2 ** 100)
QT = S // P
NT = T // P
NB = 4
KV_ST = (4 * 3 + 2) * 16
STK = 3 * 16

BANK_S = 0
BANK_O = 4
BANK_A = 5
BANK_T = 7
BANK_L = 7
OUT_BANKS = ((2, 2), (4, 3))
BANK_Q = 4


def decoder_layer(nc, x, xT, ctxT, mask, wqT, bq, wkT, bk, wvT, bv, woT, bo,
                  xwqT, xbq, xwkT, xbk, xwvT, xbv, xwoT, xbo, rw, rb, ew, eb, out):
    with ExitStack() as ctx:
        def sb(name, shape, dt=F32):
            return ctx.enter_context(nc.sbuf_tensor(name, shape, dt))

        def sem(name):
            return ctx.enter_context(nc.semaphore(name))

        def dram(name, shape, dt=F32):
            return nc.dram_tensor(name, shape, dt, kind="Internal").ap()

        ps = ctx.enter_context(nc.psum_tensor("ps", [P, 8, 512], F32))

        q_sc, xq_sc = dram("q_sc", (B * H * R, S)), dram("xq_sc", (B * H * R, S))
        k_sc = dram("k_sc", (B * HKV * R, S))
        v_sc = dram("v_sc", (B * HKV * P, QT * DH))
        xk_sc = dram("xk_sc", (B * NG * H * R, GK))
        xv_sc = dram("xv_sc", (B * NG * H * P, 2 * DH))
        mask_sc = dram("mask_sc", (T, SK), BF16)
        att_sc = [dram(f"att_sc{a}", (B * H * P, 512)) for a in range(2)]
        rec_sc = [dram(f"rec_sc{a}", (B * H * 2, 512)) for a in range(2)]
        xs_sc = dram("xs_sc", (8 * ZT * P, ROW))
        eb_sc = dram("eb_sc", (2 * E, D))
        x_sc = dram("x_sc", (T, D))

        xw = sb("xw", [P, 5 * KC * D + KC * T])
        W = [xw[:, n * KC * D:(n + 1) * KC * D].rearrange("p (k n) -> p k n", k=KC) for n in range(5)]
        xt = xw[:, 5 * KC * D:].rearrange("p (k t) -> p k t", k=KC)
        bq_s, bk_s = sb("bq_s", [P, KC]), sb("bk_s", [P, 1])
        bv_s = sb("bv_s", [P, P])
        xbq_s, xbk_s = sb("xbq_s", [P, KC]), sb("xbk_s", [P, KC])
        xbv_s = sb("xbv_s", [P, D])
        bo_s = [sb(f"bo_s{a}", [P, D]) for a in range(2)]
        rw_s, rb_s, eb_in = sb("rw_s", [P, KC, E]), sb("rb_s", [P, E]), sb("eb_in", [E, D])
        ident = sb("ident", [P, P])
        neg_ident = sb("neg_ident", [P, P], BF16)
        iota8 = sb("iota8", [P, E])
        iota8_m = sb("iota8_m", [P, E])
        qst = sb("qst", [97, NB, S], F32R)
        kst = sb("kst", [97, NB, S], F32R)
        vst = sb("vst", [P, NB, QT, 2 * DH])
        den_s = sb("den_s", [P, B, P])
        kx = sb("kx", [97, GK], F32R)
        vx = sb("vx", [P, 2, 2 * DH])
        mx = sb("mx", [P, QT, GK], BF16)
        mask0 = sb("mask0", [P, QT, GK], BF16)
        probs = sb("probs", [P, 2, S])
        hi = sb("hi", [P, 2, 512], F32R)
        lo = sb("lo", [P, 2, 512], F32R)
        m_part = sb("m_part", [P, QT, 2])
        m_rest = sb("m_rest", [P, QT])
        m_slot = sb("m_slot", [P, QT])
        m_fin = sb("m_fin", [P, 2, QT])
        m_row = sb("m_row", [QT, P], F32R)
        o_stage = sb("o_stage", [P, 2, 512])
        big = sb("big", [P, 10240])
        mask_i = big[:, 0:4096].bitcast(I32).rearrange("p (n k) -> p n k", n=2)
        mask_b = big[:, 4096:6144].bitcast(BF16).rearrange("p (n k) -> p n k", n=2)
        v_stage = big[:, 6144:7168].rearrange("p (n c) -> p n c", n=2)
        cx = [big[:, 7168 + n * 1024:8192 + n * 1024].rearrange("p (k t) -> p k t", k=KC) for n in range(2)]
        cv_stage = big[:, 9216:10240].rearrange("p (c n) -> p c n", c=2)
        onum, orec, xres = ([[area[:, m * 2048 + n * 1024:m * 2048 + (n + 1) * 1024].rearrange("p (c t) -> p c t", c=c) for n in range(2)]
                             for area in (big, xw)] for m, c in enumerate((KC, KC, 2)))
        y = big[:, 0:NT * ROW].rearrange("p (i n) -> p i n", i=NT)
        xs = [area[:, n * ROW:(n + 1) * ROW] for area in (probs[:, :, :].rearrange("p a b -> p (a b)"),
                                                           vst[:, :, :, :].rearrange("p a b c -> p (a b c)")) for n in range(XB // 2)]
        ys = [area[:, :, :].rearrange("p a b -> p (a b)").bitcast(F32)[:, n * D:(n + 1) * D] for area in (mask0, mx) for n in range(YB // 2)]
        xsT = big[:, NT * ROW:NT * ROW + 2 * D].rearrange("p (n k t) -> p n k t", n=2, k=KC)
        xnew = [[big[:, 6144 + n % 2 * 1024:7168 + n % 2 * 1024].rearrange("p (i n) -> p i n", i=2) for n in range(NT // 2)],
                [y[:, 2 * n:2 * n + 2, 0:D] for n in range(NT // 2)]]
        lgT = probs[0:E, :, :].rearrange("p a b -> p (a b)")
        eb_s = qst[0:DH + 1, :, :].rearrange("p a b -> p (a b)")
        two_ones = sb("two_ones", [DH + 1, P], F32R)
        hi4 = hi[:, :, :].rearrange("p a b -> p (a b)").rearrange("p (m t) -> p m t", m=4)
        lo4 = lo[:, :, :].rearrange("p a b -> p (a b)").rearrange("p (m t) -> p m t", m=4)
        grp = sb("grp", [P, NT, NG + 1])
        grp_m = sb("grp_m", [P, B, NG + 1])
        grp_r = sb("grp_r", [P, B, NG + 1])
        fl = sb("fl", [1, 8, NG])
        tbl = sb("tbl", [1, 4], I32)
        st = sb("st", [P, 4, 6])
        mv = sb("mv", [P, 4, 2])
        sd = sb("sd", [P, 4, 2])
        lg = sb("lg", [P, NT, E])
        ex = sb("ex", [P, NT, E])
        top = sb("top", [P, NT])
        gate = sb("gate", [P, NT])
        ixf = sb("ixf", [P, NT])
        chosen = sb("chosen", [P, NT, E])
        scan = sb("scan", [P, 2, 2 * NT + 1, E])
        before = scan[:, 0, NT:, :]
        many = sb("many", [P, E, NT])
        scan_e = sb("scan_e", [P, 2, 2 * E + 1])
        first = scan_e[:, 1, E:]
        slotf = sb("slotf", [P, NT])
        slot_u = sb("slot_u", [P, NT], U32)
        tile_e = sb("tile_e", [1, XT, E])
        tile_f = sb("tile_f", [1, XT])
        tile_i = sb("tile_i", [1, XT], I32)
        tile_u = sb("tile_u", [1, XT], I32)
        number = sb("number", [P, NT], I32)
        steps = sb("steps", [P, NT])
        iotaT = sb("iotaT", [1, XT])
        earlier = sb("earlier", [P, P])
        ones = sb("ones", [P, P])
        zeros = sb("zeros", [P, ROW])
        eps_s = sb("eps_s", [P, 1])

        names = """consts w_k w_self xt0 xt1 xt2 xt3 bias w_out w_xq w_kv w_xo
            pj_mm pj_hi pj_done pj_st0 pj_st1 pv_st0 pv_st1
            mask_in0 mask_in1 mask_eq mask_red mask_st grp_ok grp_all flag tbl_ok
            s_stk0 s_stk1 s_stk2 s_stk3 s_score s_exp s_pv s_acc s_amm s_amax s_afin s_at s_arow s_mrow s_out s_free
            c_stk0 c_stk1 c_stk2 c_stk3 c_score c_exp c_pv c_acc c_amm c_amax c_afin c_at c_arow c_mrow c_out c_free c_mask
            r_den0 r_den1 r_rec r_out o_num0 o_num1 o_ready o_x0 o_x1 o_xb o_mm o_add o_st o_var o_sd o_rs o_y o_yst0 o_yst1 o_tr o_xt
            passed f_w f_lm f_lc f_lg f_l f_ex f_sel f_cum f_slot f_te f_ebz f_ebi f_ebs f_ebd f_zero f_sc f_xs0 f_xs1 f_xs2 f_xs3 f_xs4 f_xs5 f_tr f_xc f_mm
            f_os0 f_os1 f_os2 f_os3 f_acc f_st f_var f_sd f_rs f_n""".split()
        s = {n: sem(n) for n in names}
        kv = [{n: sem(f"{n}_kv{i}") for n in "ctx mm hi done st".split()} for i in range(4)]
        rest = [{n: sem(f"{n}_rest{b}") for n in "load free amm amax top score exp pv".split()} for b in range(B)]
        block = ctx.enter_context(nc.Block())

        JOBS = [(t, kind) for t in range(T // 512) for kind in ("k", "v", 0, 1, 2, 3)]
        HEADJOBS = [j for j, (_, kind) in enumerate(JOBS) if kind != "v"]
        QJOBS = 4 * (T // 512)

        def query_jobs(t):
            return range(max(2 * t - 8, 0), 2 * t - 6 if t < 9 else QJOBS) if t >= 4 else ()

        PJ_BANKS = BANK_A
        FIRST_MAX = 16
        FIRST_ROW = 21

        def used_tiles(eng):
            eng.wait_ge(s["f_te"], 1)
            return [None] * NT + [eng.value_load(tile_u[0:1, n:n + 1], min_val=0, max_val=1) for n in range(NT, XT)]

        def where_used(eng, used, n):
            return eng.If(used[n]) if n >= NT else nullcontext()

        @block.sync
        def _(sp):
            sp.dma_start(W[1][:, :, 0:P], wkT.rearrange("(k p) n -> p k n", p=P)).then_inc(s["w_k"], 16)
            sp.dma_start(xt[:, :, 0:512], xT[:, 0:512].rearrange("(k p) t -> p k t", p=P)).then_inc(s["xt0"], 16)
            sp.dma_start(W[1][:, :, P:2 * P], wvT.rearrange("(k p) n -> p k n", p=P)).then_inc(s["w_self"], 16)
            sp.dma_start(W[0][:, :, :], wqT.rearrange("(k p) n -> p k n", p=P)).then_inc(s["w_self"], 16)
            for dst, src in ((bq_s, bq), (bk_s, bk)):
                sp.dma_start(dst[:, :], src).then_inc(s["bias"], 16)
            sp.dma_start(bv_s[:, :], bv.broadcast_to([P, P])).then_inc(s["bias"], 16)
            for t in range(1, 4):
                sp.dma_start(xt[:, :, t * 512:(t + 1) * 512],
                             xT[:, t * 512:(t + 1) * 512].rearrange("(k p) t -> p k t", p=P)).then_inc(s[f"xt{t}"], 16)

            def store_parts(dst, head, cols, high, low, keys, done):
                rows = dst[ds(head * R, 4 * R), cols].rearrange("(h c d) t -> c h d t", c=3, d=DH)
                for c, src in enumerate((high, low, high) if keys else (high, high, low)):
                    sp.dma_start(rows[c], src.bitcast(F32)).then_inc(done, 16)

            def load_head(pre, buf, qrow, krow, vrow, q, k, v, nk):
                sp.dma_start(qst[0:R, buf, :].bitcast(F32), q[ds(qrow, R), :]).then_inc(s[f"{pre}_stk{buf}"], 16)
                sp.dma_start(kst[0:R, buf, 0:nk].bitcast(F32), k[ds(krow, R), :]).then_inc(s[f"{pre}_stk{buf}"], 16)
                sp.dma_start(vst[:, buf, 0:nk // P, 0:DH], v[ds(vrow, P), 0:(nk // P) * DH]
                             .rearrange("p (c d) -> p c d", d=DH)).then_inc(s[f"{pre}_stk{buf}"], 16)

            def row_of_maxima(pre, buf, n):
                sp.wait_ge(s[f"{pre}_arow"], n + 2)
                sp.dma_start(qst[96:97, buf, :].rearrange("o (t c) -> o t c", t=QT).bitcast(F32),
                             m_row[:, :].bitcast(F32)).then_inc(s[f"{pre}_mrow"], 16)

            hj = vj = 0
            for j, (t, kind) in enumerate(JOBS):
                b, c0 = t // 2, (t % 2) * 512
                sp.wait_ge(s["pj_done"], j + 1)
                if kind == "v":
                    for i in range(4):
                        sp.dma_start(v_sc[b * HKV * P:(b + 1) * HKV * P, ((t % 2) * 4 + i) * DH:((t % 2) * 4 + i + 1) * DH]
                                     .rearrange("(h p) d -> p h d", p=P),
                                     v_stage[:, vj % 2, i * P:(i + 1) * P].rearrange("p (h d) -> p h d", h=HKV))\
                          .then_inc(s[f"pv_st{vj % 2}"], 16)
                    vj += 1
                else:
                    part, row = (k_sc, b * HKV) if kind == "k" else (q_sc, b * H + kind * 4)
                    store_parts(part, row, slice(c0, c0 + 512), hi[:, hj % 2, :], lo[:, hj % 2, :], kind == "k", s[f"pj_st{hj % 2}"])
                    hj += 1
                if j == len(JOBS) // B - 1:
                    for n in range(2):
                        sp.wait_ge(s[f"pj_st{n}"], 48 * hj // 2)
                        sp.wait_ge(s[f"pv_st{n}"], 64 * vj // 2)
                    sp.wait_ge(s["consts"], 18)
                    for g in range(3):
                        load_head("s", g, g * R, 0, 0, q_sc, k_sc, v_sc, S)
                if j == FIRST_ROW + 1:
                    row_of_maxima("s", 0, 0)
            for dst, src in ((xbq_s, xbq), (xbk_s, xbk), (eb_in, eb)):
                sp.dma_start(dst[:, :], src).then_inc(s["bias"], 16)
            for dst, src in ((xbv_s, xbv), (bo_s[0], bo), (bo_s[1], xbo), (rb_s, rb)):
                sp.dma_start(dst[:, :], src.broadcast_to([P, src.shape[1]])).then_inc(s["bias"], 16)
            sp.dma_start(rw_s[:, :, :], rw.rearrange("(k p) e -> p k e", p=P)).then_inc(s["bias"], 16)
            for n in range(2):
                sp.wait_ge(s[f"pj_st{n}"], 48 * hj // 2)
                sp.wait_ge(s[f"pv_st{n}"], 64 * vj // 2)

            def self_load(u4, g):
                load_head("s", g, u4 * (4 * R) + g * R, u4 * R, u4 * P, q_sc, k_sc, v_sc, S)

            def self_units(j, last=False):
                for g in range(4):
                    if not (last and g > 0):
                        sp.wait_ge(s["s_pv"], 8 * (4 * j + g) + 2)
                        sp.sem_inc(s["passed"], 1)
                        self_load(j + (g + 3) // 4, (g + 3) % 4)
                    if not (last and g == 3):
                        row_of_maxima("s", (g + 1) % 4, 4 * j + g + 1)

            with sp.Fori(0, 5) as j:
                self_units(j)

            sp.wait_ge(s["pj_mm"], len(JOBS))
            for w, src, done in ((W[0], xwkT, "w_kv"), (W[1], xwvT, "w_kv"), (W[2], woT, "w_out"), (W[3], xwqT, "w_xq"), (W[4], xwoT, "w_xo")):
                sp.dma_start(w, src.rearrange("(k p) n -> p k n", p=P)).then_inc(s[done], 16)
            sp.wait_ge(s["tbl_ok"], 1)
            dense = [sp.value_load(tbl[0:1, b:b + 1], min_val=0, max_val=1) for b in range(B)]
            group = [sp.value_load(tbl[0:1, 2 + b:3 + b], min_val=0, max_val=NG - 1) for b in range(B)]

            def context_load(k, b, g, buf):
                sp.dma_start(cx[buf], ctxT[:, ds(g * GK + b * SK, GK)].rearrange("(k p) t -> p k t", p=P)).then_inc(k["ctx"], 16)

            def context_store(k, b, slot):
                for m in range(4):
                    store_parts(xk_sc, slot * H + (b * NG * H + 4 * m), slice(0, GK), hi4[:, m, :], lo4[:, m, :], True, k["st"])
                for c in range(2):
                    sp.dma_start(xv_sc[ds(slot * H * P + b * NG * H * P, H * P), c * DH:(c + 1) * DH].rearrange("(h p) d -> p h d", p=P),
                                 cv_stage[:, c, :].rearrange("p (h d) -> p h d", d=DH)).then_inc(k["st"], 16)

            for b in range(B):
                context_load(kv[2 + b], b, group[b], b)
            self_units(5)
            for b in range(B):
                sp.wait_ge(kv[2 + b]["done"], 7)
                context_store(kv[2 + b], b, 0)

            def sums_load(a, b):
                sp.wait_ge(s[f"{'sc'[a]}_out"], 16 * H * (b + 1))
                sp.dma_start(den_s[:, b, :], att_sc[a].rearrange("(b n r) (c t) -> b r n c t", b=B, r=2 * DH, c=4)[b, DH])\
                  .then_inc(s[f"r_den{b}"], 16)

            def sums_store(a, b):
                sp.wait_ge(s["r_rec"], 2 * a + b + 1)
                sp.dma_start(rec_sc[a].rearrange("(b n) (c t) -> b (n c) t", b=B, c=4)[b], den_s[:, b, :]).then_inc(s["r_out"], 16)
                sp.wait_ge(s["r_out"], 16 * (2 * a + b) + 16)

            sums_load(0, 0)
            self_units(6)
            sums_store(0, 0)
            self_units(7, last=True)

            def out_stage(a):
                att = att_sc[a].rearrange("(b c h f r) t -> b h f r c t", b=B, c=KC, h=4, f=2)
                rec = rec_sc[a].rearrange("(b c h f) t -> b h f c t", b=B, c=KC, h=4)
                res = x if a == 0 else x_sc

                def store(t):
                    sp.wait_ge(s["o_y"], NT * a + 2 * t + 2)
                    sp.dma_start(x_sc[t * 256:(t + 1) * 256, :].rearrange("(i p) n -> p i n", p=P), xnew[a][t])\
                      .then_inc(s[f"o_yst{t % 2}"], 16)

                def store_queries(t):
                    for j in query_jobs(t):
                        sp.wait_ge(s["pj_done"], len(JOBS) + j + 1)
                        store_parts(xq_sc, (j // 8) * H + j % 4 * 4, slice(j // 4 % 2 * 512, j // 4 % 2 * 512 + 512),
                                    hi[:, j % 2, :], lo[:, j % 2, :], False, s[f"pj_st{j % 2}"])

                for t in range(8):
                    b, f, cols = t // 4, t // 2 % 2, slice(t % 2 * 256, t % 2 * 256 + 256)
                    if t >= 2:
                        sp.wait_ge(s["o_mm"], NT * a + 2 * t - 2)
                    for h in range(4):
                        sp.dma_start(onum[a][t % 2][DH * h:DH * h + DH, :, :], att[b, h, f, 0:DH, :, cols]).then_inc(s[f"o_num{t % 2}"], 16)
                        sp.dma_start(orec[a][t % 2][DH * h:DH * h + DH, :, :],
                                     rec[b, h, f, :, cols].rearrange("(o c) t -> o c t", o=1).broadcast_to([DH, KC, 256]))\
                          .then_inc(s[f"o_num{t % 2}"], 16)
                    if a == 0:
                        store_queries(t - 2)
                    if t >= 2:
                        sp.wait_ge(s["o_add"], NT * a + 2 * t - 2)
                    sp.dma_start(xres[a][t % 2], res[t * 256:(t + 1) * 256, :].rearrange("(i p) n -> p i n", p=P))\
                      .then_inc(s[f"o_x{t % 2}"], 16)
                    if t == 1:
                        sums_load(a, 1)
                    if t == 2:
                        sums_store(a, 1)
                    if a == 0 and t >= 3:
                        store(t - 3)
                for t in range(5, 8) if a == 0 else ():
                    store_queries(t + 1)
                    if t == 6:
                        for n in range(2):
                            sp.wait_ge(s[f"pj_st{n}"], 48 * (10 + QJOBS // 2 // 2))
                        for b in range(B):
                            sp.wait_ge(kv[2 + b]["st"], 2 * KV_ST)
                        for g in range(3):
                            cross_load(0, 0, g)
                        mask_slot(0)
                    store(t)
                if a == 0:
                    store_queries(9)
                    for n in range(2):
                        sp.wait_ge(s[f"pj_st{n}"], 48 * (10 + QJOBS // 2))
                        sp.wait_ge(s[f"o_yst{n}"], 64)

            def cross_load(b, row4, g):
                load_head("c", g, b * H * R + row4 * (4 * R) + g * R, b * NG * H * R + row4 * (4 * R) + g * R,
                          b * NG * H * P + row4 * 4 * P + g * P, xq_sc, xk_sc, xv_sc, GK)

            def mask_slot(b):
                sp.dma_start(mask0[:, :, :], mask_sc[b * S:(b + 1) * S, ds(group[b] * GK, GK)]
                             .rearrange("(i p) k -> p i k", p=P)).then_inc(s["c_mask"], 16)

            out_stage(0)

            def context_rest(k, n, b, slot):
                sp.wait_ge(k["done"], 6 * n + 1)
                sp.sem_inc(s["passed"], 1)
                context_load(k, b, slot, 0)
                sp.wait_ge(k["done"], 6 * n + 7)
                sp.sem_inc(s["passed"], 1)
                context_store(k, b, slot)
                sp.wait_ge(k["st"], KV_ST * n + 2 * KV_ST)
                sp.sem_inc(s["passed"], 1)

            for b in range(B):
                with sp.If(dense[b]):
                    with sp.Fori(1, NG) as g:
                        context_rest(kv[b], g - 1, b, g)

            def rest_loads(b, n, h):
                r = rest[b]
                with sp.If(dense[b]):
                    with sp.Fori(1, NG) as slot:
                        sp.wait_ge(r["free"], n + slot)
                        sp.sem_inc(s["passed"], 1)
                        sp.dma_start(kx[0:R, :].bitcast(F32), xk_sc[ds(slot * H * R + (b * NG * H * R + h * R), R), :]).then_inc(r["load"], 16)
                        sp.dma_start(vx[:, :, 0:DH], xv_sc[ds(slot * H * P + (b * NG * H * P + h * P), P), :]
                                     .rearrange("p (c d) -> p c d", d=DH)).then_inc(r["load"], 16)
                        sp.dma_start(mx[:, :, :], mask_sc[b * S:(b + 1) * S, ds(slot * GK, GK)]
                                     .rearrange("(i p) k -> p i k", p=P)).then_inc(r["load"], 16)

            def load_expert(e):
                sp.dma_start(xw[:, e * KC * D:(e + 1) * KC * D].rearrange("p (k n) -> p k n", k=KC),
                             ew[e * D:(e + 1) * D, :].rearrange("(k p) n -> p k n", p=P)).then_inc(s["f_w"], 16)

            for b in range(B):
                if b > 0:
                    sp.wait_ge(s["c_pv"], 32 * b + 2)
                    mask_slot(b)
                rest_loads(b, 0, 0)
                rest_loads(b, 7, 1)
                for n in range(2):
                    row_of_maxima("c", n, 16 * b + n)
                if b == 0:
                    load_expert(3)
                else:
                    sp.wait_ge(s["f_ebs"], 2)
                    for part, src in enumerate((hi, lo)):
                        sp.dma_start(eb_sc[part * E:(part + 1) * E, :], src[0:E, 0, :].bitcast(F32)).then_inc(s["f_ebd"], 16)
                    sp.wait_ge(s["f_ebd"], 32)
                    sums_load(1, 0)

                def cross_units(j, last=False):
                    for g in range(4):
                        n = 14 + 14 * (4 * j + g)
                        if last and g == 3:
                            n = n - 7
                        if not (last and g > 0 and b == B - 1):
                            sp.wait_ge(s["c_pv"], 2 * (16 * b + 4 * j + g) + 2)
                            sp.sem_inc(s["passed"], 1)
                            if last and g > 0:
                                cross_load(b + 1, 0, g - 1)
                            else:
                                cross_load(b, j + (g + 3) // 4, (g + 3) % 4)
                        if not (last and g >= 2):
                            rest_loads(b, n, 4 * j + g + 2)
                        rest_loads(b, n if last and g >= 2 else n + 7, 4 * j + g)
                        if not (last and g >= 2):
                            row_of_maxima("c", (g + 2) % 4, 16 * b + 4 * j + g + 2)

                with sp.Fori(0, 3) as j:
                    cross_units(j)
                if b == 1:
                    sums_store(1, 0)
                cross_units(3, last=True)

            out_stage(1)
            sp.wait_ge(s["o_mm"], 2 * NT)
            for e in (0, 1, 4):
                load_expert(e)
            sp.wait_ge(s["o_add"], 2 * NT)
            load_expert(2)
            sp.wait_ge(s["f_ebz"], 4)
            for part in range(2):
                sp.dma_start(eb_s[part * DH:part * DH + 1, :].bitcast(F32),
                             eb_sc[part * E:(part + 1) * E, :].rearrange("(o e) n -> o (e n)", o=1)).then_inc(s["f_ebi"], 16)
            sp.wait_ge(s["f_lm"], 4)
            for e in range(5, E):
                load_expert(e)
            used = used_tiles(sp)
            sp.wait_ge(s["f_sc"], 16 * NT)
            for n in range(XT):
                with where_used(sp, used, n):
                    if n >= XB:
                        sp.wait_ge(s[f"f_os{(n - XB) % YB}"], 16 * ((n - XB) // YB + 1))
                    sp.dma_start(xs[n % XB], xs_sc[n * P:(n + 1) * P, :]).then_inc(s[f"f_xs{n % XB}"], 16)
            for n in range(NT - YB, XT):
                with where_used(sp, used, n):
                    sp.wait_ge(s[f"f_os{n % YB}"], 16 * (n // YB + 1))
                    sp.sem_inc(s["passed"], 1)

        @block.gpsimd
        def _(pool):
            nc.gpsimd.memset(ident[:, :], 0.0).then_inc(s["consts"], 1)
            nc.gpsimd.memset(neg_ident[:, :], 0.0).then_inc(s["consts"], 1)
            nc.gpsimd.memset(vst[:, :, :, :], 1.0).then_inc(s["consts"], 1)
            nc.gpsimd.memset(vx[:, :, :], 1.0).then_inc(s["consts"], 1)
            pool.wait_ge(s["consts"], 4)
            nc.gpsimd.memset(kst[96:97, :, :].bitcast(F32), -1.0).then_inc(s["consts"], 1)
            pool.wait_ge(s["consts"], 5)
            nc.gpsimd.memset(kx[96:97, :].bitcast(F32), -1.0).then_inc(s["consts"], 1)
            pool.wait_ge(s["consts"], 6)
            nc.gpsimd.memset(eps_s[:, :], EPS).then_inc(s["consts"], 1)
            pool.wait_ge(s["consts"], 7)
            nc.gpsimd.affine_select(out=ident[:, :], in_=ident[:, :], compare_op=ALU.not_equal, fill=1.0, base=0,
                                    pattern=[[-1, P]], channel_multiplier=1).then_inc(s["consts"], 1)
            nc.gpsimd.affine_select(out=neg_ident[:, :], in_=neg_ident[:, :], compare_op=ALU.not_equal, fill=MASKED, base=0,
                                    pattern=[[-1, P]], channel_multiplier=1).then_inc(s["consts"], 1)
            nc.gpsimd.iota(iota8[:, :], pattern=[[1, E]], base=0, channel_multiplier=0,
                           allow_small_or_imprecise_dtypes=True).then_inc(s["consts"], 1)
            nc.gpsimd.iota(iota8_m[:, :], pattern=[[1, E]], base=-E, channel_multiplier=0,
                           allow_small_or_imprecise_dtypes=True).then_inc(s["consts"], 1)
            nc.gpsimd.iota(steps[:, :], pattern=[[P, NT]], base=0, channel_multiplier=0,
                           allow_small_or_imprecise_dtypes=True).then_inc(s["consts"], 1)
            nc.gpsimd.iota(iotaT[:, :], pattern=[[1, XT]], base=0, channel_multiplier=0,
                           allow_small_or_imprecise_dtypes=True).then_inc(s["consts"], 1)
            nc.gpsimd.memset(ones[:, :], 1.0).then_inc(s["consts"], 1)
            nc.gpsimd.memset(zeros[:, :], 0.0).then_inc(s["consts"], 1)
            nc.gpsimd.iota(number[:, :], pattern=[[P, NT]], base=0, channel_multiplier=1).then_inc(s["consts"], 1)
            pool.wait_ge(s["consts"], 16)
            nc.gpsimd.iota(zeros[:, D + 1:D + 2].bitcast(I32), pattern=[[0, 1]], base=T, channel_multiplier=0).then_inc(s["consts"], 1)
            nc.gpsimd.affine_select(out=earlier[:, :], in_=ones[:, :], compare_op=ALU.is_gt, fill=0.0, base=0,
                                    pattern=[[1, P]], channel_multiplier=-1).then_inc(s["consts"], 1)
            for pre in "sc":
                pool.sem_inc(s[f"{pre}_free"], 2)

            def store_unit(pre, a, u, par):
                pool.wait_ge(s[f"{pre}_acc"], u + 2)
                pool.sem_inc(s["passed"], 1)
                pool.dma_start(att_sc[a][ds(u * P, P), :], o_stage[:, par, :]).then_inc(s[f"{pre}_out"], 16)
                pool.wait_ge(s[f"{pre}_out"], u * 16 + 16)
                pool.sem_inc(s[f"{pre}_free"], 1)

            def mask_load(i, par):
                pool.dma_start(mask_i[:, par, :], mask[ds(i * P, P), :]).then_inc(s[f"mask_in{par}"], 16)

            def mask_pair(j, last=False):
                for par in range(2):
                    i = 2 * j + par
                    if not (last and par == 1):
                        mask_load(i + 1, 1 - par)
                    pool.wait_ge(s[f"mask_in{par}"], 16 * j + 16)
                    pool.wait_ge(s["mask_red"], 4 * i + 4)
                    pool.sem_inc(s["passed"], 1)
                    nc.gpsimd.tensor_scalar(mask_b[:, par, :], mask_i[:, par, :], 1.0, None, ALU.is_equal).then_inc(s["mask_eq"], 1)
                    pool.wait_ge(s["mask_eq"], i + 1)
                    pool.sem_inc(s["passed"], 1)
                    pool.dma_start(mask_sc[ds(i * P, P), :], mask_b[:, par, :]).then_inc(s["mask_st"], 16)
                    pool.wait_ge(s["mask_st"], i * 16 + 16)
                    pool.sem_inc(s["passed"], 1)
                    store_unit("s", 0, i, par)

            pool.wait_ge(s["xt3"], 16)
            mask_load(0, 0)
            with pool.Fori(0, 7) as j:
                mask_pair(j)
            mask_pair(7, last=True)
            pool.wait_ge(s["grp_ok"], 1)
            nc.gpsimd.partition_all_reduce(grp_r[:, :, :].rearrange("p b g -> p (b g)"),
                                           grp_m[:, :, :].rearrange("p b g -> p (b g)"), P, RMAX).then_inc(s["grp_all"], 1)
            with pool.Fori(8, 16) as j:
                pool.dma_start(xs_sc[ds(j * (ZT * P) - 8 * ZT * P, ZT * P), :].rearrange("(n p) d -> p n d", p=P),
                               zeros[:, :].rearrange("p (o d) -> p o d", o=1).broadcast_to([P, ZT, ROW])).then_inc(s["f_zero"], 16)
                for par in range(2):
                    store_unit("s", 0, 2 * j + par, par)

            def residuals(a):
                for t in range(8):
                    pool.wait_ge(s[f"o_x{t % 2}"], 64 * a + 16 * (t // 2) + 16)
                    for i in range(2):
                        nc.gpsimd.tensor_tensor(xres[a][t % 2][:, i, :], xres[a][t % 2][:, i, :], bo_s[a][:, :], ALU.add).then_inc(s["o_xb"], 1)

            pool.wait_ge(s["bias"], 16 * 11)
            residuals(0)
            with pool.Fori(0, 16) as j:
                for par in range(2):
                    store_unit("c", 1, 2 * j + par, par)
            residuals(1)

            pool.wait_ge(s["c_pv"], 2 * B * H + 2)
            pool.sem_inc(s["passed"], 1)
            nc.gpsimd.memset(eb_s.bitcast(F32), 0.0).then_inc(s["f_ebz"], 1)
            nc.gpsimd.memset(two_ones[:, :].bitcast(F32), 0.0).then_inc(s["f_ebz"], 1)
            pool.wait_ge(s["f_ebz"], 2)
            nc.gpsimd.memset(two_ones[0:1, :].bitcast(F32), 1.0).then_inc(s["f_ebz"], 1)
            pool.wait_ge(s["f_ebz"], 3)
            nc.gpsimd.memset(two_ones[DH:DH + 1, :].bitcast(F32), 1.0).then_inc(s["f_ebz"], 1)
            pool.wait_ge(s["f_zero"], 16 * 8)
            pool.wait_ge(s["f_slot"], 1)
            for i in range(NT):
                nc.gpsimd.indirect_dma_start(xs_sc, bass.IndirectOffsetOnAxis(ap=slot_u[:, i:i + 1], axis=0), y[:, i, :], None)\
                  .then_inc(s["f_sc"], 16)
            used = used_tiles(pool)
            for n in range(XT):
                with where_used(pool, used, n):
                    pool.wait_ge(s["f_n"], n + 1)
                    nc.gpsimd.indirect_dma_start(out, bass.IndirectOffsetOnAxis(ap=xs[n % XB][:, D + 1:D + 2].bitcast(U32), axis=0),
                                                 ys[n % YB], None, bounds_check=T - 1, oob_is_err=False)\
                      .then_inc(s[f"f_os{n % YB}"], 16)

        @block.scalar
        def _(act):
            for pre in "sc":
                act.sem_inc(s[f"{pre}_exp"], 2)
                act.sem_inc(s[f"{pre}_acc"], 1)
                act.sem_inc(s[f"{pre}_arow"], 1)
                act.sem_inc(s[f"{pre}_mrow"], 16)
            def copy_maxima(pre, n):
                act.wait_ge(s[f"{pre}_at"], n + 3)
                act.wait_ge(s[f"{pre}_mrow"], 16 * n + 16)
                nc.scalar.activation(m_row[:, :], ps[0:QT, BANK_T, 0:P], ACT.Copy).then_inc(s[f"{pre}_arow"], 1)

            act.wait_ge(s["bias"], 16 * 3)
            for n, j in enumerate(HEADJOBS):
                t, kind = JOBS[j]
                act.wait_ge(s["pj_mm"], j + 1)
                if n >= 2:
                    act.wait_ge(s[f"pj_st{n % 2}"], 48 * (n // 2))
                bias = bk_s[:, 0:1] if kind == "k" else bq_s[:, kind:kind + 1]
                nc.scalar.activation(hi[:, n % 2, :], ps[:, j % PJ_BANKS, :], ACT.Identity, bias=bias).then_inc(s["pj_hi"], 1)
                if j == FIRST_ROW:
                    copy_maxima("s", 0)

            def exps(pre, n, c):
                act.wait_ge(s[f"{pre}_score"], n + 1)
                act.wait_ge(s[f"{pre}_pv"], n + 1)
                nc.scalar.activation(probs[:, c % 2, :].rearrange("p (a b) -> p a b", a=2),
                                     ps[:, BANK_S + 2 * (c % 2):BANK_S + 2 * (c % 2) + 2, :],
                                     ACT.Exp, scale=SCALE).then_inc(s[f"{pre}_exp"], 1)

            def unit_result(pre, u, chunks, par):
                act.wait_ge(s[f"{pre}_pv"], chunks * u + chunks + 2)
                act.wait_ge(s[f"{pre}_free"], u + 1)
                nc.scalar.activation(o_stage[:, par, :], ps[:, BANK_O, :], ACT.Copy).then_inc(s[f"{pre}_acc"], 1)

            def self_units(j, last=False):
                for g in range(4):
                    u = 4 * j + g
                    for c in range(QT):
                        if c == 2 and not (last and g == 3):
                            copy_maxima("s", u + 1)
                        exps("s", 8 * u + c, c)
                    unit_result("s", u, QT, g % 2)

            def context_slot(k, n):
                for m in range(4):
                    act.wait_ge(k["mm"], 6 * n + m + 1)
                    act.wait_ge(k["st"], KV_ST * n + KV_ST)
                    nc.scalar.activation(hi4[:, m, :], ps[:, m, 0:GK], ACT.Identity, bias=xbk_s[:, m:m + 1]).then_inc(k["hi"], 1)

            with act.Fori(0, 6) as j:
                self_units(j)
            act.wait_ge(s["tbl_ok"], 1)
            dense = [act.value_load(tbl[0:1, b:b + 1], min_val=0, max_val=1) for b in range(B)]
            act.wait_ge(s["bias"], 16 * 11)
            for n in range(2):
                act.wait_ge(s[f"pj_st{n}"], 48 * 10)
            context_slot(kv[2], 0)
            act.wait_ge(kv[2]["st"], 2 * KV_ST)
            context_slot(kv[3], 0)
            self_units(6)
            self_units(7, last=True)

            def norm_stage(a):
                products, turned_ones = OUT_BANKS[a]

                def turned(t):
                    for i in range(2 * t, 2 * t + 2):
                        act.wait_ge(s["o_tr"], NT * a + i + 1)
                        nc.scalar.activation(xt[:, :, i * P:(i + 1) * P],
                                             ps[:, products + i % turned_ones, :].rearrange("p (k t) -> p k t", k=KC), ACT.Copy)\
                          .then_inc(s["o_xt"], 1)

                def query_parts(t):
                    for j in query_jobs(t) if a == 0 else ():
                        act.wait_ge(s["pj_mm"], len(JOBS) + j + 1)
                        if j == 0:
                            act.wait_ge(kv[3]["st"], 2 * KV_ST)
                        if j >= 2:
                            act.wait_ge(s[f"pj_st{j % 2}"], 48 * (10 + j // 2))
                        nc.scalar.activation(hi[:, j % 2, :], ps[:, BANK_Q + j % 4, :], ACT.Identity, bias=xbq_s[:, j % 4:j % 4 + 1])\
                          .then_inc(s["pj_hi"], 1)

                def logits(q):
                    act.wait_ge(s["f_lm"], q + 1)
                    nc.scalar.activation(lgT[:, q * 512:(q + 1) * 512], ps[0:E, BANK_L, :], ACT.Copy).then_inc(s["f_lc"], 1)

                for t in range(8):
                    act.wait_ge(s["o_var"], 16 * a + 2 * t + 2)
                    nc.scalar.activation(sd[:, t % 2 * 2:t % 2 * 2 + 2, 0], mv[:, t % 2 * 2:t % 2 * 2 + 2, 1], ACT.Sqrt,
                                         bias=eps_s[:, 0:1]).then_inc(s["o_sd"], 1)
                    if t:
                        turned(t - 1)
                    if a == 1 and t in (3, 5, 7):
                        logits((t - 3) // 2)
                    query_parts(t + 1)
                turned(7)
                if a == 1:
                    logits(3)
                query_parts(9)

            norm_stage(0)


            for b in range(B):
                with act.If(dense[b]):
                    for n in range(2):
                        act.wait_ge(s[f"pj_st{n}"], 48 * 18)
                    act.sem_inc(s["passed"], 1)
                    with act.Fori(0, NG - 1) as n:
                        context_slot(kv[b], n)
                    act.wait_ge(kv[b]["st"], NG * KV_ST)
                    act.sem_inc(s["passed"], 1)

            for b in range(B):
                if b == 1:
                    for n in range(2):
                        act.wait_ge(s[f"pj_st{n}"], 48 * 18)
                    nc.scalar.activation(hi[0:E, 0, :], eb_in[:, :], ACT.Copy).then_inc(s["f_ebs"], 1)
                for n in range(2):
                    copy_maxima("c", 16 * b + n)

                def cross_units(j, last=False):
                    for g in range(4):
                        u = 4 * j + g
                        n = 16 * b + u
                        exps("c", 2 * n, 0)
                        exps("c", 2 * n + 1, 1)
                        r = rest[b]
                        with act.If(dense[b]):
                            act.wait_ge(s["c_pv"], 2 * n + 3)
                            with act.Fori(0, NG - 1) as sl:
                                for c in range(2):
                                    act.wait_ge(r["score"], 14 * u + sl * 2 + c + 1)
                                    act.wait_ge(r["pv"], 14 * u + sl * 2 + c + 1)
                                    nc.scalar.activation(probs[:, 0, :].rearrange("p (a b) -> p a b", a=2),
                                                         ps[:, BANK_S:BANK_S + 2, :], ACT.Exp, scale=SCALE).then_inc(r["exp"], 1)
                            act.wait_ge(r["pv"], 14 * u + 15)
                            act.sem_inc(s["passed"], 1)
                        if not (last and g >= 2):
                            copy_maxima("c", n + 2)
                        unit_result("c", n, 2, g % 2)

                with act.Fori(0, 3) as j:
                    cross_units(j)
                cross_units(3, last=True)
            norm_stage(1)

            act.wait_ge(s["f_l"], 3)
            nc.scalar.activation(ex[:, :, :], lg[:, :, :], ACT.Exp).then_inc(s["f_ex"], 1)

            used = used_tiles(act)
            for n in range(XT + 3):
                if n < XT:
                    with where_used(act, used, n):
                        act.wait_ge(s["f_tr"], n + 1)
                        if n >= 2:
                            act.wait_ge(s["f_mm"], n - 1)
                        nc.scalar.activation(xsT[:, n % 2, :, :], ps[:, 4 + n % 2, :].rearrange("p (k t) -> p k t", k=KC), ACT.Copy)\
                          .then_inc(s["f_xc"], 1)
                if n >= 3:
                    m = n - 3
                    with where_used(act, used, m):
                        act.wait_ge(s["f_var"], m + 1)
                        nc.scalar.activation(sd[:, m % 4, 0:1], mv[:, m % 4, 1:2], ACT.Sqrt, bias=eps_s[:, 0:1]).then_inc(s["f_sd"], 1)

        @block.tensor
        def _(pe):
            for pre in "sc":
                pe.sem_inc(s[f"{pre}_pv"], 2)
                pe.sem_inc(s[f"{pre}_at"], 2)
            for r in rest:
                pe.sem_inc(r["free"], 1)
                pe.sem_inc(r["pv"], 1)
            mm = nc.tensor.matmul
            def scores(bank, st_buf, q_buf, c, masked=None):
                for half in range(2):
                    cols = slice(half * 512, half * 512 + 512)
                    last = mm(ps[:, bank + half, :], st_buf[:, c * P:(c + 1) * P], qst[:, q_buf, cols],
                              start=True, stop=True)
                    if masked is not None:
                        for i in range(4):
                            last = mm(ps[:, bank + half, i * P:(i + 1) * P], masked[:, 4 * half + i, c * P:(c + 1) * P],
                                      neg_ident[:, :], start=False, stop=True, skip_group_check=True)
                return last

            def weighted(v_buf, par, first, stop):
                for half in range(2):
                    last = mm(ps[64 * half:64 * half + 64, BANK_O, :], v_buf, probs[:, par, half * 512:half * 512 + 512],
                              start=first, stop=stop, skip_group_check=True)
                return last

            def transpose_maxima(pre, n, par):
                pe.wait_ge(s[f"{pre}_afin"], n + 2)
                pe.wait_ge(s[f"{pre}_arow"], n + 1)
                nc.tensor.transpose(ps[0:QT, BANK_T, 0:P], m_fin[:, par, :], ident[:, :]).then_inc(s[f"{pre}_at"], 1)

            def self_max(n, buf, i):
                for half in range(2):
                    pe.wait_ge(s["s_amax"], 16 * n + 2 * i + half + 1)
                    mm(ps[:, BANK_A + half, :], qst[0:96, buf, i * P:(i + 1) * P],
                       kst[0:96, buf, half * 512:half * 512 + 512], start=True, stop=True).then_inc(s["s_amm"], 1)

            for j, (t, kind) in enumerate(JOBS):
                if j >= PJ_BANKS:
                    pe.wait_ge(s["pj_done"], j - PJ_BANKS + 1)
                if j == 0:
                    pe.wait_ge(s["w_k"], 16)
                if j == 1:
                    pe.wait_ge(s["w_self"], 32)
                if kind == "k":
                    pe.wait_ge(s[f"xt{t}"], 16)
                if j == FIRST_MAX:
                    pe.wait_ge(s["consts"], 18)
                    for n in range(2):
                        pe.wait_ge(s[f"s_stk{n}"], STK)
                if j == FIRST_ROW:
                    transpose_maxima("s", 0, 0)
                bank = j % PJ_BANKS
                for half in range(2):
                    if kind == "v":
                        for i in range(2 * half, 2 * half + 2):
                            for k in range(KC):
                                last = mm(ps[:, bank, i * P:(i + 1) * P], xt[:, k, t * 512 + i * P:t * 512 + (i + 1) * P],
                                          W[1][:, k, P:2 * P], start=(k == 0), stop=(k == KC - 1))
                    else:
                        for k in range(KC // 2 * half, KC // 2 * (half + 1)):
                            w = W[1][:, k, 0:P] if kind == "k" else W[0][:, k, kind * P:(kind + 1) * P]
                            last = mm(ps[:, bank, :], w, xt[:, k, t * 512:(t + 1) * 512], start=(k == 0), stop=(k == KC - 1))
                    if half == 1:
                        last.then_inc(s["pj_mm"], 1)
                    if j >= FIRST_MAX:
                        i = 2 * (j - FIRST_MAX) + half
                        self_max(i // QT, i // QT, i % QT)
            pe.wait_ge(s["pj_done"], len(JOBS))

            def self_units(j, last=False):
                for g in range(4):
                    u = 4 * j + g
                    ahead = not (last and g >= 2)
                    buf2 = (g + 2) % 4
                    pe.wait_ge(s["s_mrow"], 16 * u + 32)
                    for c in range(QT + 1):
                        if c < QT:
                            pe.wait_ge(s["s_exp"], 8 * u + c + 1)
                            scores(BANK_S + 2 * (c % 2), kst[:, g, :], g, c).then_inc(s["s_score"], 1)
                        if c == 2 and not (last and g == 3):
                            transpose_maxima("s", u + 1, (g + 1) % 2)
                        if c >= 1:
                            if c == 1:
                                pe.wait_ge(s["s_acc"], u + 1)
                            pe.wait_ge(s["s_exp"], 8 * u + c + 2)
                            weighted(vst[:, g, c - 1, :], (c - 1) % 2, c == 1, c == QT).then_inc(s["s_pv"], 1)
                        if ahead and c < QT:
                            if c == 0:
                                pe.wait_ge(s[f"s_stk{buf2}"], STK * (j + (g + 2) // 4) + STK)
                            self_max(u + 2, buf2, c)

            def context_slot(k_, n, buf, bank_free=None):
                pe.wait_ge(k_["ctx"], 16 * n + 16)
                for m in range(4):
                    if bank_free is not None:
                        pe.wait_ge(bank_free, m + 2)
                    for k in range(KC):
                        last = mm(ps[:, m, 0:GK], W[0][:, k, m * P:(m + 1) * P], cx[buf][:, k, :], start=(k == 0), stop=(k == KC - 1))
                    last.then_inc(k_["mm"], 1)
                for c in range(2):
                    if bank_free is not None:
                        pe.wait_ge(bank_free, c + 6)
                    for k in range(KC):
                        last = mm(ps[:, BANK_A + c, :], cx[buf][:, k, c * P:(c + 1) * P], W[1][:, k, :], start=(k == 0), stop=(k == KC - 1))
                    last.then_inc(k_["mm"], 1)

            with pe.Fori(0, 6) as j:
                self_units(j)
            pe.wait_ge(s["w_kv"], 32)
            pe.wait_ge(s["s_amax"], 16 * 26 + 2)
            context_slot(kv[2], 0, 0)
            context_slot(kv[3], 0, 1, kv[2]["done"])
            pe.wait_ge(s["tbl_ok"], 1)
            dense = [pe.value_load(tbl[0:1, b:b + 1], min_val=0, max_val=1) for b in range(B)]
            pe.wait_ge(kv[3]["done"], 7)
            self_units(6)
            self_units(7, last=True)

            def out_stage(a, w):
                products, turned_ones = OUT_BANKS[a]
                pe.wait_ge(s["w_out" if a == 0 else "w_xo"], 16)

                def turn(t):
                    for i in range(2):
                        n = NT * a + 2 * t + i
                        pe.wait_ge(s["o_y"], n + 1)
                        if 2 * t + i >= turned_ones:
                            pe.wait_ge(s["o_xt"], n - turned_ones + 1)
                        for k in range(KC):
                            last = nc.tensor.transpose(ps[:, products + (2 * t + i) % turned_ones, k * P:(k + 1) * P], xnew[a][t][:, i, k * P:(k + 1) * P], ident[:, :])
                        last.then_inc(s["o_tr"], 1)

                def queries(t):
                    for j in query_jobs(t) if a == 0 else ():
                        if j == 0:
                            pe.wait_ge(s["w_xq"], 16)
                            pe.wait_ge(s["s_acc"], 33)
                        if j % 4 == 0:
                            pe.wait_ge(s["o_xt"], j + 4)
                        if j >= 4:
                            pe.wait_ge(s["pj_done"], len(JOBS) + j - 3)
                        for k in range(KC):
                            last = mm(ps[:, BANK_Q + j % 4, :], W[3][:, k, (j % 4) * P:(j % 4 + 1) * P],
                                      xt[:, k, (j // 4) * 512:(j // 4 + 1) * 512], start=(k == 0), stop=(k == KC - 1))
                        last.then_inc(s["pj_mm"], 1)

                def router(q):
                    pe.wait_ge(s["o_xt"], NT + 4 * q + 4)
                    if q:
                        pe.wait_ge(s["f_lc"], q)
                    for k in range(KC):
                        last = mm(ps[0:E, BANK_L, :], rw_s[:, k, :], xt[:, k, q * 512:(q + 1) * 512], start=(k == 0), stop=(k == KC - 1))
                    last.then_inc(s["f_lm"], 1)

                for t in range(8):
                    pe.wait_ge(s["o_ready"], 8 * a + t + 1)
                    for i in range(2):
                        n = NT * a + 2 * t + i
                        if 2 * t + i >= products:
                            pe.wait_ge(s["o_add"], n - products + 1)
                        for k in range(KC):
                            last = mm(ps[:, n % products, :], onum[a][t % 2][:, k, i * P:(i + 1) * P], w[:, k, :], start=(k == 0), stop=(k == KC - 1))
                        last.then_inc(s["o_mm"], 1)
                    if t >= 2:
                        turn(t - 2)
                        queries(t)
                    if a == 1 and t in (4, 6):
                        router(t // 2 - 2)
                for t in (6, 7):
                    turn(t)
                    queries(t + 2)
                    if a == 1:
                        router(t - 4)

            out_stage(0, W[2])
            pe.wait_ge(s["pj_done"], len(JOBS) + QJOBS - 1)
            for b in range(B):
                with pe.If(dense[b]):
                    with pe.Fori(0, NG - 1) as n:
                        context_slot(kv[b], n, 0)
                        pe.wait_ge(kv[b]["done"], n * 6 + 7)
                        pe.sem_inc(s["passed"], 1)

            def max_pair(bank, q_buf, keys, masked, f):
                for i in range(2):
                    mm(ps[:, bank, i * GK:(i + 1) * GK], qst[0:96, q_buf, (2 * f + i) * P:(2 * f + i + 1) * P], keys,
                       start=(i == 0), stop=True, skip_group_check=True)
                for i in range(2):
                    last = mm(ps[:, bank, i * GK:(i + 1) * GK], neg_ident[:, :], masked[:, 2 * f + i, :],
                              start=False, stop=True, skip_group_check=True)
                return last

            def cross_max(b, a, buf, n):
                r = rest[b]
                with pe.If(dense[b]):
                    pe.wait_ge(s["c_amax"], 64 * b + a * 4 + 2)
                    pe.sem_inc(s["passed"], 1)
                    with pe.Fori(0, NG - 1) as sl:
                        pe.wait_ge(r["load"], sl * 48 + n * 48 + 48)
                        for f in range(4):
                            pe.wait_ge(r["amax"], a * 28 + sl * 4 + f + 1)
                            last = max_pair(BANK_A, buf, kx[0:96, :], mx, f)
                            last.then_inc(r["amm"], 1)
                        pe.wait_ge(r["amm"], a * 28 + sl * 4 + 4)
                        pe.sem_inc(r["free"], 1)
                    pe.wait_ge(r["amax"], a * 28 + 29)
                    pe.sem_inc(s["passed"], 1)

            def cross_max_slot(b, a, buf, pairs):
                for f in pairs:
                    pe.wait_ge(s["c_amax"], 64 * b + a * 4 + f + 1)
                    max_pair(BANK_A + f % 2, buf, kst[0:96, buf, 0:GK], mask0, f).then_inc(s["c_amm"], 1)

            for b in range(B):
                pe.wait_ge(s["c_mask"], 16 * b + 16)
                for n in range(2):
                    pe.wait_ge(s[f"c_stk{n}"], STK * (4 * b + 1))
                    cross_max(b, n, n, 7 * n)
                    cross_max_slot(b, n, n, range(4))
                pe.wait_ge(s["pj_done"], len(JOBS) + QJOBS)
                for n in range(2):
                    transpose_maxima("c", 16 * b + n, n)

                def cross_units(j, last=False):
                    for g in range(4):
                        u = 4 * j + g
                        n = 16 * b + u
                        before = 14 + 14 * u
                        if last and g == 3:
                            before = before - 7
                        ahead = not (last and g >= 2)
                        buf2 = (g + 2) % 4
                        pe.wait_ge(s["c_mrow"], 16 * n + 32)
                        for c in range(2):
                            pe.wait_ge(s["c_exp"], 2 * n + c + 1)
                            scores(BANK_S + 2 * c, kst[:, g, :], g, c, masked=mask0).then_inc(s["c_score"], 1)
                            if ahead:
                                if c == 0:
                                    pe.wait_ge(s[f"c_stk{buf2}"], STK * (4 * b + j + (g + 2) // 4) + STK)
                                    cross_max(b, u + 2, buf2, before)
                                cross_max_slot(b, u + 2, buf2, range(2 * c, 2 * c + 2))
                        pe.wait_ge(s["c_acc"], n + 1)
                        pe.wait_ge(s["c_exp"], 2 * n + 3)
                        weighted(vst[:, g, 0, :], 0, True, True).then_inc(s["c_pv"], 1)
                        r = rest[b]
                        taken = before + 7 if ahead else before
                        with pe.If(dense[b]):
                            with pe.Fori(0, NG - 1) as sl:
                                pe.wait_ge(r["load"], sl * 48 + taken * 48 + 48)
                                for c in range(2):
                                    scores(BANK_S, kx, g, c, masked=mx).then_inc(r["score"], 1)
                                    pe.wait_ge(r["exp"], 14 * u + sl * 2 + c + 1)
                                    weighted(vx[:, c, :], 0, False, True).then_inc(r["pv"], 1)
                                pe.wait_ge(r["pv"], 14 * u + sl * 2 + 3)
                                pe.sem_inc(r["free"], 1)
                        pe.wait_ge(s["c_exp"], 2 * n + 4)
                        weighted(vst[:, g, 1, :], 1, False, True).then_inc(s["c_pv"], 1)
                        if ahead:
                            transpose_maxima("c", n + 2, g % 2)

                with pe.Fori(0, 3) as j:
                    cross_units(j)
                cross_units(3, last=True)
            out_stage(1, W[4])

            pe.wait_ge(s["f_lc"], 4)
            for i in range(NT):
                last = nc.tensor.transpose(ps[:, BANK_L, i * E:(i + 1) * E], lgT[:, i * P:(i + 1) * P], ident[0:E, 0:E])
            last.then_inc(s["f_lg"], 1)
            pe.wait_ge(s["f_sel"], 1)
            mm(ps[:, 2, 0:NT * E], earlier[:, :], chosen[:, :, :].rearrange("p i e -> p (i e)"), start=True, stop=True).then_inc(s["f_cum"], 1)
            mm(ps[:, 3, 0:NT * E], ones[:, :], chosen[:, :, :].rearrange("p i e -> p (i e)"), start=True, stop=True).then_inc(s["f_cum"], 1)
            def turn(n):
                pe.wait_ge(s[f"f_xs{n % XB}"], 16 * (n // XB) + 16)
                if n >= 2:
                    pe.wait_ge(s["f_xc"], n - 1)
                for k in range(KC):
                    last = nc.tensor.transpose(ps[:, 4 + n % 2, k * P:(k + 1) * P], xs[n % XB][:, k * P:(k + 1) * P], ident[:, :])
                last.then_inc(s["f_tr"], 1)

            used = used_tiles(pe)
            turn(0)
            turn(1)
            pe.wait_ge(s["f_ebi"], 32)
            pe.wait_ge(s["f_w"], 16 * E)
            for n in range(XT):
                with where_used(pe, used, n):
                    expert = pe.value_load(tile_i[0:1, n:n + 1], min_val=0, max_val=E - 1)
                    pe.wait_ge(s["f_xc"], n + 1)
                    if n >= 4:
                        pe.wait_ge(s["f_acc"], n - 3)
                    for k in range(KC):
                        mm(ps[:, n % 4, :], xsT[:, n % 2, k, :], xw[:, ds(expert * (KC * D) + k * D, D)], start=(k == 0), stop=True,
                           skip_group_check=True)
                    last = mm(ps[:, n % 4, :], two_ones[:, :], eb_s[:, ds(expert * D, D)], start=False, stop=True, skip_group_check=True)
                    last.then_inc(s["f_mm"], 1)
                if n + 2 < XT:
                    with where_used(pe, used, n + 2):
                        turn(n + 2)

        @block.vector
        def _(dve):
            for pre in "sc":
                dve.sem_inc(s[f"{pre}_amax"], 2)
                dve.sem_inc(s[f"{pre}_afin"], 1)
            for k in kv:
                dve.sem_inc(k["done"], 1)
                dve.sem_inc(k["st"], KV_ST)
            for r in rest:
                dve.sem_inc(r["amax"], 1)
            dve.sem_inc(s["mask_red"], 8)
            dve.wait_ge(s["bias"], 16 * 3)
            def invert_sums(a, b):
                dve.wait_ge(s[f"r_den{b}"], 16 * a + 16)
                nc.vector.reciprocal(den_s[:, b, :], den_s[:, b, :]).then_inc(s["r_rec"], 1)

            def final_max(pre, n, par, src):
                dve.wait_ge(s[f"{pre}_at"], n + 1)
                if pre == "s":
                    nc.vector.tensor_reduce(m_fin[:, par, :], m_part[:, :, :], AX.X, ALU.max).then_inc(s["s_afin"], 1)
                else:
                    nc.vector.tensor_tensor(m_fin[:, par, :], m_slot[:, :], m_rest[:, :], ALU.max).then_inc(s["c_afin"], 1)

            def self_max(n, par, parts=range(2 * QT), tile=None):
                for k in parts:
                    if k == 0:
                        dve.wait_ge(s["s_afin"], n + 1)
                    dve.wait_ge(s["s_amm"], 16 * n + k + 1)
                    nc.vector.reduce_max(m_part[:, k // 2, k % 2:k % 2 + 1], ps[:, BANK_A + k % 2, :], AX.X).then_inc(s["s_amax"], 1)
                    if tile is not None and k % 4 == 3:
                        mask_groups(tile, k // 4)
                    if k == 2 * QT - 1:
                        dve.wait_ge(s["s_amax"], 16 * n + 18)
                        final_max("s", n, par, None)

            def first_max(j, half):
                if j >= FIRST_MAX:
                    i = 2 * (j - FIRST_MAX) + half
                    self_max(i // QT, i // QT, range(2 * (i % QT), 2 * (i % QT) + 2))

            n = v = 0
            for j, (t, kind) in enumerate(JOBS):
                first_max(j, 0)
                if kind == "v":
                    dve.wait_ge(s["pj_mm"], j + 1)
                    if v >= 2:
                        dve.wait_ge(s[f"pv_st{v % 2}"], 64 * (v // 2))
                    nc.vector.tensor_tensor(v_stage[:, v % 2, :].rearrange("p (i n) -> p i n", i=4),
                                            ps[:, j % PJ_BANKS, :].rearrange("p (i n) -> p i n", i=4),
                                            bv_s[:, :].rearrange("p (o n) -> p o n", o=1).broadcast_to([P, 4, P]),
                                            ALU.add).then_inc(s["pj_done"], 1)
                    v += 1
                else:
                    dve.wait_ge(s["pj_hi"], n + 1)
                    if n >= 2:
                        dve.wait_ge(s[f"pj_st{n % 2}"], 48 * (n // 2))
                    bias = bk_s[:, 0:1] if kind == "k" else bq_s[:, kind:kind + 1]
                    nc.vector.scalar_tensor_tensor(out=lo[:, n % 2, :], in0=ps[:, j % PJ_BANKS, :], scalar=bias,
                                                   in1=hi[:, n % 2, :].bitcast(F32), op0=ALU.add, op1=ALU.subtract)\
                      .then_inc(s["pj_done"], 1)
                    n += 1
                first_max(j, 1)

            def mask_groups(tile, quarter):
                i, par = tile
                if quarter == 0:
                    dve.wait_ge(s["mask_eq"], i + 1)
                nc.vector.tensor_reduce(grp[:, :, :].rearrange("p i g -> p (i g)")[:, ds(i * (NG + 1) + quarter * (NG // 4), NG // 4)],
                                        mask_b[:, par, quarter * (SK // 4):(quarter + 1) * (SK // 4)].rearrange("p (g k) -> p g k", k=GK),
                                        AX.X, ALU.min).then_inc(s["mask_red"], 1)

            self_max(2, 0)
            with dve.Fori(0, 8) as j:
                for par in range(2):
                    self_max(2 * j + 3 + par, 1 - par, tile=(2 * j + par, par))
            nc.vector.memset(scan[:, :, :, :], 0.0).then_inc(s["f_cum"], 1)
            nc.vector.memset(scan_e[:, :, :], 0.0).then_inc(s["f_cum"], 1)
            dve.wait_ge(s["mask_red"], 4 * (NT + 2))
            step = [0]

            def flag(ins):
                step[0] += 1
                ins.then_inc(s["flag"], 1)
                dve.wait_ge(s["flag"], step[0])

            flag(nc.vector.tensor_reduce(grp[:, :, NG], grp[:, :, 0:NG], AX.X, ALU.min))
            flag(nc.vector.tensor_scalar(grp[:, :, 0:NG], grp[:, :, 0:NG], -1.0, 1.0, ALU.mult, ALU.add))
            nc.vector.tensor_reduce(grp_m[:, :, :], grp[:, :, :].rearrange("p (b i) g -> p b g i", b=B), AX.X, ALU.max)\
              .then_inc(s["grp_ok"], 1)

            self_max(19, 1)
            def group_table(b):
                g = grp_r[0:1, b, :]
                flag(nc.vector.reduce_sum(fl[:, b, 0:1], g[:, 0:NG], AX.X))
                flag(nc.vector.tensor_scalar(fl[:, b, 1:2], g[:, NG:NG + 1], 2.0, fl[:, b, 0:1], ALU.mult, ALU.add))
                flag(nc.vector.tensor_scalar(fl[:, b, 2:3], fl[:, b, 1:2], 1.5, None, ALU.is_gt))
                flag(nc.vector.tensor_tensor(fl[:, 2 + b, :], g[:, 0:NG], iota8[0:1, :], ALU.mult))
                flag(nc.vector.reduce_max(fl[:, b, 3:4], fl[:, 2 + b, :], AX.X))
                flag(nc.vector.tensor_scalar(fl[:, b, 4:5], fl[:, b, 2:3], -1.0, 1.0, ALU.mult, ALU.add))
                flag(nc.vector.tensor_tensor(fl[:, b, 5:6], fl[:, b, 4:5], fl[:, b, 3:4], ALU.mult))
                flag(nc.vector.tensor_copy(tbl[:, b:b + 1], fl[:, b, 2:3]))
                flag(nc.vector.tensor_copy(tbl[:, 2 + b:3 + b], fl[:, b, 5:6]))

            self_max(20, 0)
            dve.wait_ge(s["grp_all"], 1)
            group_table(0)
            self_max(21, 1)
            group_table(1)
            dve.sem_inc(s["tbl_ok"], 1)
            with dve.Fori(11, 13) as j:
                self_max(2 * j, 0)
                self_max(2 * j + 1, 1)

            def context_slot(k, n):
                for m in range(4):
                    dve.wait_ge(k["hi"], 4 * n + m + 1)
                    nc.vector.scalar_tensor_tensor(out=lo4[:, m, :], in0=ps[:, m, 0:GK], scalar=xbk_s[:, m:m + 1],
                                                   in1=hi4[:, m, :].bitcast(F32), op0=ALU.add, op1=ALU.subtract)\
                      .then_inc(k["done"], 1)
                for c in range(2):
                    dve.wait_ge(k["mm"], 6 * n + 5 + c)
                    nc.vector.tensor_tensor(cv_stage[:, c, :], ps[:, BANK_A + c, :], xbv_s[:, :], ALU.add).then_inc(k["done"], 1)

            dense = [dve.value_load(tbl[0:1, b:b + 1], min_val=0, max_val=1) for b in range(B)]
            dve.wait_ge(s["bias"], 16 * 11)
            for n in range(2):
                dve.wait_ge(s[f"pj_st{n}"], 48 * 10)
            context_slot(kv[2], 0)
            dve.wait_ge(kv[2]["st"], 2 * KV_ST)
            context_slot(kv[3], 0)
            self_max(26, 0)
            self_max(27, 1)
            invert_sums(0, 0)
            with dve.Fori(14, 16) as j:
                self_max(2 * j, 0)
                self_max(2 * j + 1, 1)

            def out_stage(a):
                products, _ = OUT_BANKS[a]
                def sums(t):
                    if a == 0 and t >= 2:
                        dve.wait_ge(s[f"o_yst{t % 2}"], 16 * (t // 2))
                        dve.wait_ge(s["o_tr"], 2 * t - 2)
                    for i in range(2):
                        n = NT * a + 2 * t + i
                        dve.wait_ge(s["o_mm"], n + 1)
                        dve.wait_ge(s["o_xb"], n + 1)
                        nc.vector.tensor_tensor(xnew[a][t][:, i, :], ps[:, n % products, :], xres[a][t % 2][:, i, :], ALU.add).then_inc(s["o_add"], 1)
                    for i in range(2):
                        n = NT * a + 2 * t + i
                        dve.wait_ge(s["o_add"], n + 1)
                        dve.wait_ge(s["o_y"], NT * a + 2 * t - 2) if t >= 2 else None
                        nc.vector.bn_stats(st[:, n % 4, :], xnew[a][t][:, i, :]).then_inc(s["o_st"], 1)
                    for i in range(2):
                        n = NT * a + 2 * t + i
                        dve.wait_ge(s["o_st"], n + 1)
                        nc.vector.bn_aggr(mv[:, n % 4, :], st[:, n % 4, :]).then_inc(s["o_var"], 1)

                def norm(t):
                    lanes = slice(t % 2 * 2, t % 2 * 2 + 2)
                    dve.wait_ge(s["o_sd"], 8 * a + t + 1)
                    nc.vector.reciprocal(sd[:, lanes, 1], sd[:, lanes, 0]).then_inc(s["o_rs"], 1)
                    dve.wait_ge(s["o_rs"], 8 * a + t + 1)
                    for i in range(2):
                        n = NT * a + 2 * t + i
                        nc.vector.tensor_scalar(xnew[a][t][:, i, :], xnew[a][t][:, i, :], mv[:, n % 4, 0:1], sd[:, n % 4, 1:2],
                                                ALU.subtract, ALU.mult).then_inc(s["o_y"], 1)

                def scaled(t):
                    dve.wait_ge(s[f"o_num{t % 2}"], 512 * a + 128 * (t // 2) + 128)
                    nc.vector.tensor_tensor(onum[a][t % 2], onum[a][t % 2], orec[a][t % 2], ALU.mult).then_inc(s["o_ready"], 1)

                def query_parts(t):
                    for j in query_jobs(t) if a == 0 else ():
                        dve.wait_ge(s["pj_hi"], len(HEADJOBS) + j + 1)
                        if j == 0:
                            dve.wait_ge(kv[3]["st"], 2 * KV_ST)
                        if j >= 2:
                            dve.wait_ge(s[f"pj_st{j % 2}"], 48 * (10 + j // 2))
                        nc.vector.scalar_tensor_tensor(out=lo[:, j % 2, :], in0=ps[:, BANK_Q + j % 4, :], scalar=xbq_s[:, j % 4:j % 4 + 1],
                                                       in1=hi[:, j % 2, :].bitcast(F32), op0=ALU.add, op1=ALU.subtract)\
                          .then_inc(s["pj_done"], 1)

                scaled(0)
                scaled(1)
                for t in range(1, 10):
                    if t == 2:
                        invert_sums(a, 1)
                    if t < 9:
                        sums(t - 1)
                        norm(t - 1)
                    if t < 7:
                        scaled(t + 1)
                    query_parts(t)

            out_stage(0)
            for b in range(B):
                with dve.If(dense[b]):
                    for n in range(2):
                        dve.wait_ge(s[f"pj_st{n}"], 48 * 18)
                    dve.sem_inc(s["passed"], 1)
                    with dve.Fori(0, NG - 1) as n:
                        dve.wait_ge(kv[b]["st"], n * KV_ST + KV_ST)
                        context_slot(kv[b], n)
                    dve.wait_ge(kv[b]["st"], NG * KV_ST)
                    dve.sem_inc(s["passed"], 1)

            def cross_max(b, a, par):
                r = rest[b]
                n = 16 * b + a
                with dve.If(dense[b]):
                    dve.wait_ge(s["c_afin"], n + 1)
                    dve.wait_ge(r["top"], 8 * a + 1)
                    nc.vector.memset(m_rest[:, :], MASKED).then_inc(r["top"], 1)
                    with dve.Fori(0, NG - 1) as sl:
                        dve.wait_ge(r["top"], a * 8 + sl + 2)
                        for f in range(4):
                            dve.wait_ge(r["amm"], a * 28 + sl * 4 + f + 1)
                            nc.vector.reduce_max(m_slot[:, 2 * f:2 * f + 2], ps[:, BANK_A, :].rearrange("p (i k) -> p i k", i=2), AX.X)\
                              .then_inc(r["amax"], 1)
                        dve.wait_ge(r["amax"], a * 28 + sl * 4 + 5)
                        nc.vector.tensor_tensor(m_rest[:, :], m_rest[:, :], m_slot[:, :], ALU.max).then_inc(r["top"], 1)
                    dve.wait_ge(r["top"], a * 8 + 9)
                    dve.sem_inc(s["passed"], 1)
                dve.wait_ge(s["c_afin"], n + 1)
                for f in range(4):
                    dve.wait_ge(s["c_amm"], 4 * n + f + 1)
                    nc.vector.reduce_max(m_slot[:, 2 * f:2 * f + 2], ps[:, BANK_A + f % 2, :].rearrange("p (i k) -> p i k", i=2), AX.X)\
                      .then_inc(s["c_amax"], 1)
                dve.wait_ge(s["c_amax"], 4 * n + 6)
                final_max("c", n, par, None)

            for b in range(B):
                if b == 1:
                    for n in range(2):
                        dve.wait_ge(s[f"pj_st{n}"], 48 * 18)
                    dve.wait_ge(s["f_ebs"], 1)
                    nc.vector.tensor_tensor(lo[0:E, 0, :], eb_in[:, :], hi[0:E, 0, :].bitcast(F32), ALU.subtract).then_inc(s["f_ebs"], 1)
                dve.wait_ge(s["c_afin"], 16 * b + 1)
                nc.vector.memset(m_rest[:, :], MASKED).then_inc(rest[b]["top"], 1)
                dve.wait_ge(rest[b]["top"], 1)
                for half in range(2):
                    if b == 1 and half == 1:
                        invert_sums(1, 0)
                    with dve.Fori(4 * half, 4 * half + 4) as j:
                        cross_max(b, 2 * j, 0)
                        cross_max(b, 2 * j + 1, 1)
            out_stage(1)

            def per_expert(v):
                return v.rearrange("p (o e) -> p o e", o=1).broadcast_to([P, NT, E])

            def per_token(v):
                return v.rearrange("p (i o) -> p i o", o=1).broadcast_to([P, NT, E])

            dve.wait_ge(s["f_lg"], 1)
            nc.vector.tensor_tensor(lg[:, :, :], ps[:, BANK_L, 0:NT * E].rearrange("p (i e) -> p i e", i=NT), per_expert(rb_s[:, :]), ALU.add)\
              .then_inc(s["f_l"], 1)
            dve.wait_ge(s["f_l"], 1)
            nc.vector.reduce_max(top[:, :], lg[:, :, :], AX.X).then_inc(s["f_l"], 1)
            dve.wait_ge(s["f_l"], 2)
            nc.vector.tensor_tensor(lg[:, :, :], lg[:, :, :], per_token(top[:, :]), ALU.subtract).then_inc(s["f_l"], 1)
            dve.wait_ge(s["f_ex"], 1)
            flag(nc.vector.reduce_max(top[:, :], ex[:, :, :], AX.X))
            flag(nc.vector.tensor_tensor(chosen[:, :, :], ex[:, :, :], per_token(top[:, :]), ALU.is_equal))
            flag(nc.vector.tensor_tensor(chosen[:, :, :], chosen[:, :, :], per_expert(iota8_m[:, :]), ALU.mult))
            flag(nc.vector.tensor_reduce(ixf[:, :], chosen[:, :, :], AX.X, ALU.min))
            nc.vector.tensor_tensor(chosen[:, :, :], per_expert(iota8_m[:, :]), per_token(ixf[:, :]), ALU.is_equal).then_inc(s["f_sel"], 1)
            flag(nc.vector.reduce_sum(gate[:, :], ex[:, :, :], AX.X))
            flag(nc.vector.reciprocal(gate[:, :], gate[:, :]))
            flag(nc.vector.tensor_tensor(y[:, :, D:ROW], gate[:, :].rearrange("p (i o) -> p i o", o=1).broadcast_to([P, NT, ROW - D]),
                                         top[:, :].rearrange("p (i o) -> p i o", o=1).broadcast_to([P, NT, ROW - D]), ALU.mult))
            flag(nc.vector.tensor_copy(y.bitcast(I32)[:, :, D + 1:D + 2], number[:, :].rearrange("p (i o) -> p i o", o=1)))
            dve.wait_ge(s["f_cum"], 4)
            totals = ps[:, 3, 0:NT * E].rearrange("p (i e) -> p i e", i=NT)
            flag(nc.vector.tensor_copy(scan[:, 0, NT + 1:, :], totals))
            for n, d in enumerate((1, 2, 4, 8)):
                flag(nc.vector.tensor_tensor(scan[:, (n + 1) % 2, NT:, :], scan[:, n % 2, NT:, :],
                                             scan[:, n % 2, NT - d:2 * NT + 1 - d, :], ALU.add))
            flag(nc.vector.tensor_tensor(many[:, :, :], before[:, NT, :].rearrange("p (e o) -> p e o", o=1).broadcast_to([P, E, NT]),
                                         steps[:, :].rearrange("p (o k) -> p o k", o=1).broadcast_to([P, E, NT]), ALU.is_gt))
            flag(nc.vector.reduce_sum(scan_e[:, 0, E + 1:], many[:, :, :], AX.X))
            for n, d in enumerate((1, 2, 4)):
                flag(nc.vector.tensor_tensor(scan_e[:, (n + 1) % 2, E:], scan_e[:, n % 2, E:], scan_e[:, n % 2, E - d:2 * E + 1 - d], ALU.add))
            flag(nc.vector.tensor_tensor(lg[:, :, :], ps[:, 2, 0:NT * E].rearrange("p (i e) -> p i e", i=NT), before[:, 0:NT, :], ALU.add))
            flag(nc.vector.scalar_tensor_tensor(out=lg[:, :, :], in0=per_expert(first[:, 0:E]), scalar=float(P), in1=lg[:, :, :],
                                                op0=ALU.mult, op1=ALU.add))
            flag(nc.vector.tensor_tensor(lg[:, :, :], lg[:, :, :], chosen[:, :, :], ALU.mult))
            flag(nc.vector.reduce_sum(slotf[:, :], lg[:, :, :], AX.X))
            nc.vector.tensor_copy(slot_u[:, :], slotf[:, :]).then_inc(s["f_slot"], 1)
            flag(nc.vector.tensor_tensor(tile_e[:, :, :], iotaT[:, :].rearrange("p (n o) -> p n o", o=1).broadcast_to([1, XT, E]),
                                         first[0:1, 0:E].rearrange("p (o e) -> p o e", o=1).broadcast_to([1, XT, E]), ALU.is_ge))
            flag(nc.vector.reduce_sum(tile_f[:, :], tile_e[:, :, :], AX.X))
            flag(nc.vector.tensor_scalar(tile_i[:, :], tile_f[:, :], -1.0, None, ALU.add))
            nc.vector.tensor_scalar(tile_u[:, :], iotaT[:, :], first[0:1, E:E + 1], None, ALU.is_lt).then_inc(s["f_te"], 1)

            used = used_tiles(dve)
            for n in range(XT + 1):
                if n < XT:
                    with where_used(dve, used, n):
                        dve.wait_ge(s["f_mm"], n + 1)
                        if n >= YB:
                            dve.wait_ge(s[f"f_os{n % YB}"], 16 * (n // YB))
                        nc.vector.scalar_tensor_tensor(out=ys[n % YB], in0=ps[:, n % 4, :], scalar=xs[n % XB][:, D:D + 1],
                                                       in1=xs[n % XB][:, 0:D], op0=ALU.mult, op1=ALU.add).then_inc(s["f_acc"], 1)
                if n >= 1:
                    m = n - 1
                    with where_used(dve, used, m):
                        dve.wait_ge(s["f_sd"], m + 1)
                        nc.vector.reciprocal(sd[:, m % 4, 1:2], sd[:, m % 4, 0:1]).then_inc(s["f_rs"], 1)
                        dve.wait_ge(s["f_rs"], m + 1)
                        nc.vector.tensor_scalar(ys[m % YB], ys[m % YB], mv[:, m % 4, 0:1], sd[:, m % 4, 1:2],
                                                ALU.subtract, ALU.mult).then_inc(s["f_n"], 1)
                if n < XT:
                    with where_used(dve, used, n):
                        dve.wait_ge(s["f_acc"], n + 1)
                        nc.vector.bn_stats(st[:, n % 4, :], ys[n % YB]).then_inc(s["f_st"], 1)
                        dve.wait_ge(s["f_st"], n + 1)
                        if n >= 4:
                            dve.wait_ge(s["f_n"], n - 3)
                        nc.vector.bn_aggr(mv[:, n % 4, :], st[:, n % 4, :]).then_inc(s["f_var"], 1)


def kernel(**inputs):
    import numpy as _np
    import concourse.bacc as _bacc
    from concourse import mybir as _mybir
    from concourse.bass_utils import run_bass_kernel_spmd as _run

    a = {k: _np.asarray(v) for k, v in inputs.items()}

    def column(v, n):
        return v.reshape(n, -1).T

    def turned(m):
        return m.reshape(-1, m.shape[-1]).T

    laid = {
        "x": a["x"].reshape(T, D), "xT": turned(a["x"]), "ctxT": turned(a["ctx_1024"]),
        "mask": a["mask_Bx1xSxS2_ik1"].reshape(T, SK),
        "wqT": a["L0_attn_wq"].T, "bq": column(a["L0_attn_bq"], KC), "wkT": a["L0_attn_wk"].T, "bk": column(a["L0_attn_bk"], 1),
        "wvT": a["L0_attn_wv"].T, "bv": a["L0_attn_bv"].reshape(1, -1), "woT": a["L0_attn_wo"].T, "bo": a["L0_attn_bo"].reshape(1, -1),
        "xwqT": a["L0_xattn_Wq"].T, "xbq": column(a["L0_xattn_bq"], KC), "xwkT": a["L0_xattn_Wk"].T, "xbk": column(a["L0_xattn_bk"], KC),
        "xwvT": a["L0_xattn_Wv"].T, "xbv": a["L0_xattn_bv"].reshape(1, -1), "xwoT": a["L0_xattn_Wo"].T, "xbo": a["L0_xattn_bo"].reshape(1, -1),
        "rw": a["L0_ffn_router_w"], "rb": a["L0_ffn_router_b"].reshape(1, -1),
        "ew": a["L0_ffn_expert_w"].reshape(E * D, D), "eb": a["L0_ffn_expert_b"],
    }
    nc = _bacc.Bacc("TRN2", target_bir_lowering=False, num_devices=1)
    arrays, args = {}, []
    for name, v in laid.items():
        v = _np.ascontiguousarray(v)
        arrays[f"{name}_dram"] = v
        args.append(nc.dram_tensor(f"{name}_dram", v.shape, _mybir.dt.from_np(v.dtype), kind="ExternalInput").ap())
    args.append(nc.dram_tensor("out_dram", (T, D), F32, kind="ExternalOutput").ap())
    decoder_layer(nc, *args)
    r = _run(nc, [arrays], core_ids=[0])
    return r.results[0]["out_dram"].reshape(B, S, D)
```
